# Optimizing a Trainium2 kernel written in Bass

```python
import numpy as np
import jax
import jax.numpy as jnp

def _softmax(x, axis=-1):
    return jax.nn.softmax(x, axis=axis)

def _gelu(x):
    return jax.nn.gelu(x, approximate=True)

def _silu(x):
    return jax.nn.silu(x)

def _sigmoid(x):
    return jax.nn.sigmoid(x)

def _layernorm(x, axis=-1, eps=1e-05):
    m = jnp.mean(x, axis=axis, keepdims=True)
    v = jnp.var(x, axis=axis, keepdims=True)
    return (x - m) / jnp.sqrt(v + eps)

def _scatter_add(tgt, idx, src, axis=0):
    return tgt.at[idx].add(src)

def _segment_sum(src, seg, n):
    return jax.ops.segment_sum(src, seg, n)
kernel_name = 'mk_macaron_d1_jaxref_r4_6d1dfb'

def setup_inputs(seed: int=0):
    np.random.seed(seed)
    _w = jnp.asarray

    def _L0_attn_setup():
        import jax, jax.numpy as jnp
        import numpy as np
        D_MODEL = 256
        N_LAYERS = 2
        N_HEADS = 16
        HEAD_DIM = D_MODEL // N_HEADS
        D_FFN = 4 * D_MODEL
        B, L = (4, 256)

        def layer_norm(x, g, b, eps=1e-05):
            mu = jnp.mean(x, axis=-1, keepdims=True)
            var = jnp.var(x, axis=-1, keepdims=True)
            return (x - mu) * jax.lax.rsqrt(var + eps) * g + b

        def make_decay(length):
            gamma = 1.0 - 2.0 ** (-5.0 - jnp.arange(N_HEADS, dtype=jnp.float32))
            n = jnp.arange(length, dtype=jnp.float32)[:, None]
            m = jnp.arange(length, dtype=jnp.float32)[None, :]
            diff = n - m
            pow_ = gamma[:, None, None] ** diff[None]
            return jnp.where(diff[None] >= 0, pow_, 0.0)

        def _forward(x, proj_w, proj_b, reto_w, reto_b, ln1_g, ln1_b, ln2_g, ln2_b, ffn1_w, ffn1_b, ffn2_w, ffn2_b, lnf_g, lnf_b):
            Bx, Lx, _ = x.shape
            D = make_decay(Lx)
            for i in range(N_LAYERS):
                ln_x = layer_norm(x, ln1_g[i], ln1_b[i])
                p = ln_x @ proj_w[i] + proj_b[i]
                q, k, v, xo = jnp.split(p, 4, axis=-1)
                q = q.reshape(Bx, Lx, N_HEADS, HEAD_DIM).transpose(0, 2, 1, 3)
                k = k.reshape(Bx, Lx, N_HEADS, HEAD_DIM).transpose(0, 2, 1, 3)
                v = v.reshape(Bx, Lx, N_HEADS, HEAD_DIM).transpose(0, 2, 1, 3)
                scores = jnp.einsum('bhld,bhmd->bhlm', q, k) * D[None]
                ret = jnp.einsum('bhlm,bhmd->bhld', scores, v)
                ret = ret.transpose(0, 2, 1, 3).reshape(Bx, Lx, D_MODEL)
                ret = ret * jax.nn.silu(xo)
                ret = ret @ reto_w[i] + reto_b[i]
                x = x + ret
                h = layer_norm(x, ln2_g[i], ln2_b[i])
                h = jax.nn.gelu(h @ ffn1_w[i] + ffn1_b[i], approximate=False) @ ffn2_w[i] + ffn2_b[i]
                x = x + h
            return layer_norm(x, lnf_g, lnf_b)
        key = jax.random.key(seed)
        ks = jax.random.split(key, 16)
        s = 0.02
        inp = {'x': jax.random.normal(ks[0], (B, L, D_MODEL), jnp.float32), 'proj_w': jax.random.normal(ks[1], (N_LAYERS, D_MODEL, 4 * D_MODEL), jnp.float32) * s, 'proj_b': jnp.zeros((N_LAYERS, 4 * D_MODEL), jnp.float32), 'reto_w': jax.random.normal(ks[2], (N_LAYERS, D_MODEL, D_MODEL), jnp.float32) * s, 'reto_b': jnp.zeros((N_LAYERS, D_MODEL), jnp.float32), 'ln1_g': jnp.ones((N_LAYERS, D_MODEL), jnp.float32), 'ln1_b': jnp.zeros((N_LAYERS, D_MODEL), jnp.float32), 'ln2_g': jnp.ones((N_LAYERS, D_MODEL), jnp.float32), 'ln2_b': jnp.zeros((N_LAYERS, D_MODEL), jnp.float32), 'ffn1_w': jax.random.normal(ks[3], (N_LAYERS, D_MODEL, D_FFN), jnp.float32) * s, 'ffn1_b': jnp.zeros((N_LAYERS, D_FFN), jnp.float32), 'ffn2_w': jax.random.normal(ks[4], (N_LAYERS, D_FFN, D_MODEL), jnp.float32) * s, 'ffn2_b': jnp.zeros((N_LAYERS, D_MODEL), jnp.float32), 'lnf_g': jnp.ones((D_MODEL,), jnp.float32), 'lnf_b': jnp.zeros((D_MODEL,), jnp.float32)}
        return inp
    _L0_attn_in = _L0_attn_setup()

    def _L0_ffn_setup():
        import jax, jax.numpy as jnp
        import numpy as np
        B, S, H, I, E, TOPK, KS = (4, 1024, 256, 128, 16, 2, 3)
        key = jax.random.key(seed)
        ks = jax.random.split(key, 9)
        sc = 0.02
        return {'hidden_states': jax.random.normal(ks[0], (B, S, H), dtype=jnp.float32), 'router_w': jax.random.normal(ks[1], (H, E), dtype=jnp.float32) * sc, 'router_bias': jnp.zeros((E,), dtype=jnp.float32), 'expert_gate_w': jax.random.normal(ks[2], (E - 1, H, I), dtype=jnp.float32) * sc, 'expert_up_w': jax.random.normal(ks[3], (E - 1, H, I), dtype=jnp.float32) * sc, 'expert_down_w': jax.random.normal(ks[4], (E - 1, I, H), dtype=jnp.float32) * sc, 'conv_w': jax.random.normal(ks[5], (I, H, KS), dtype=jnp.float32) * sc, 'shared_up_w': jax.random.normal(ks[6], (H, I), dtype=jnp.float32) * sc, 'shared_down_w': jax.random.normal(ks[7], (I, H), dtype=jnp.float32) * sc}
    _L0_ffn_in = _L0_ffn_setup()
    _d = {'L0_attn_x': _L0_attn_in['x'], 'L0_attn_proj_w': _L0_attn_in['proj_w'], 'L0_attn_proj_b': _L0_attn_in['proj_b'], 'L0_attn_reto_w': _L0_attn_in['reto_w'], 'L0_attn_reto_b': _L0_attn_in['reto_b'], 'L0_attn_ln1_g': _L0_attn_in['ln1_g'], 'L0_attn_ln1_b': _L0_attn_in['ln1_b'], 'L0_attn_ln2_g': _L0_attn_in['ln2_g'], 'L0_attn_ln2_b': _L0_attn_in['ln2_b'], 'L0_attn_ffn1_w': _L0_attn_in['ffn1_w'], 'L0_attn_ffn1_b': _L0_attn_in['ffn1_b'], 'L0_attn_ffn2_w': _L0_attn_in['ffn2_w'], 'L0_attn_ffn2_b': _L0_attn_in['ffn2_b'], 'L0_attn_lnf_g': _L0_attn_in['lnf_g'], 'L0_attn_lnf_b': _L0_attn_in['lnf_b'], 'L0_ffn_router_w': _L0_ffn_in['router_w'], 'L0_ffn_router_bias': _L0_ffn_in['router_bias'], 'L0_ffn_expert_gate_w': _L0_ffn_in['expert_gate_w'], 'L0_ffn_expert_up_w': _L0_ffn_in['expert_up_w'], 'L0_ffn_expert_down_w': _L0_ffn_in['expert_down_w'], 'L0_ffn_conv_w': _L0_ffn_in['conv_w'], 'L0_ffn_shared_up_w': _L0_ffn_in['shared_up_w'], 'L0_ffn_shared_down_w': _L0_ffn_in['shared_down_w']}
    _x0 = _d['L0_attn_x']
    _d['L0_attn_x'] = jax.random.normal(jax.random.fold_in(jax.random.key(seed), 1), (4, 1024, 256), dtype=_x0.dtype)
    del _x0
    return _d

def reference(L0_attn_x, L0_attn_proj_w, L0_attn_proj_b, L0_attn_reto_w, L0_attn_reto_b, L0_attn_ln1_g, L0_attn_ln1_b, L0_attn_ln2_g, L0_attn_ln2_b, L0_attn_ffn1_w, L0_attn_ffn1_b, L0_attn_ffn2_w, L0_attn_ffn2_b, L0_attn_lnf_g, L0_attn_lnf_b, L0_ffn_router_w, L0_ffn_router_bias, L0_ffn_expert_gate_w, L0_ffn_expert_up_w, L0_ffn_expert_down_w, L0_ffn_conv_w, L0_ffn_shared_up_w, L0_ffn_shared_down_w):

    def _L0_attn_ref(x, proj_w, proj_b, reto_w, reto_b, ln1_g, ln1_b, ln2_g, ln2_b, ffn1_w, ffn1_b, ffn2_w, ffn2_b, lnf_g, lnf_b):
        import jax, jax.numpy as jnp
        import numpy as np
        D_MODEL = 256
        N_LAYERS = 2
        N_HEADS = 16
        HEAD_DIM = D_MODEL // N_HEADS
        D_FFN = 4 * D_MODEL
        B, L = (4, 256)

        def layer_norm(x, g, b, eps=1e-05):
            mu = jnp.mean(x, axis=-1, keepdims=True)
            var = jnp.var(x, axis=-1, keepdims=True)
            return (x - mu) * jax.lax.rsqrt(var + eps) * g + b

        def make_decay(length):
            gamma = 1.0 - 2.0 ** (-5.0 - jnp.arange(N_HEADS, dtype=jnp.float32))
            n = jnp.arange(length, dtype=jnp.float32)[:, None]
            m = jnp.arange(length, dtype=jnp.float32)[None, :]
            diff = n - m
            pow_ = gamma[:, None, None] ** diff[None]
            return jnp.where(diff[None] >= 0, pow_, 0.0)

        def _forward(x, proj_w, proj_b, reto_w, reto_b, ln1_g, ln1_b, ln2_g, ln2_b, ffn1_w, ffn1_b, ffn2_w, ffn2_b, lnf_g, lnf_b):
            Bx, Lx, _ = x.shape
            D = make_decay(Lx)
            for i in range(N_LAYERS):
                ln_x = layer_norm(x, ln1_g[i], ln1_b[i])
                p = ln_x @ proj_w[i] + proj_b[i]
                q, k, v, xo = jnp.split(p, 4, axis=-1)
                q = q.reshape(Bx, Lx, N_HEADS, HEAD_DIM).transpose(0, 2, 1, 3)
                k = k.reshape(Bx, Lx, N_HEADS, HEAD_DIM).transpose(0, 2, 1, 3)
                v = v.reshape(Bx, Lx, N_HEADS, HEAD_DIM).transpose(0, 2, 1, 3)
                scores = jnp.einsum('bhld,bhmd->bhlm', q, k) * D[None]
                ret = jnp.einsum('bhlm,bhmd->bhld', scores, v)
                ret = ret.transpose(0, 2, 1, 3).reshape(Bx, Lx, D_MODEL)
                ret = ret * jax.nn.silu(xo)
                ret = ret @ reto_w[i] + reto_b[i]
                x = x + ret
                h = layer_norm(x, ln2_g[i], ln2_b[i])
                h = jax.nn.gelu(h @ ffn1_w[i] + ffn1_b[i], approximate=False) @ ffn2_w[i] + ffn2_b[i]
                x = x + h
            return layer_norm(x, lnf_g, lnf_b)
        return _forward(x, proj_w, proj_b, reto_w, reto_b, ln1_g, ln1_b, ln2_g, ln2_b, ffn1_w, ffn1_b, ffn2_w, ffn2_b, lnf_g, lnf_b)

    def _L0_ffn_ref(hidden_states, router_w, router_bias, expert_gate_w, expert_up_w, expert_down_w, conv_w, shared_up_w, shared_down_w):
        import jax, jax.numpy as jnp
        import numpy as np
        B, S, H, I, E, TOPK, KS = (4, 1024, 256, 128, 16, 2, 3)
        b, s, h = hidden_states.shape
        flat = hidden_states.reshape(b * s, h)
        logits = (flat @ router_w).astype(jnp.float32) + router_bias
        probs = jax.nn.softmax(logits, axis=-1)
        top_w, top_i = jax.lax.top_k(probs, TOPK)
        norm_w = top_w / (jnp.sum(top_w, axis=-1, keepdims=True) + 1e-06)
        norm_w = norm_w.astype(hidden_states.dtype)
        combine = jnp.sum(jax.nn.one_hot(top_i, E, dtype=norm_w.dtype) * norm_w[..., None], axis=1)
        routed = combine[:, E - 1:E] * flat
        for e in range(E - 1):
            y = jax.nn.silu(flat @ expert_gate_w[e]) * (flat @ expert_up_w[e]) @ expert_down_w[e]
            routed = routed + combine[:, e:e + 1] * y
        routed = routed.reshape(b, s, h)
        x_ncw = jnp.transpose(hidden_states, (0, 2, 1))
        gate = jax.lax.conv_general_dilated(x_ncw, conv_w, window_strides=(1,), padding=[(KS - 1, 0)], dimension_numbers=('NCW', 'OIW', 'NCW'))
        gate = jnp.transpose(gate, (0, 2, 1))
        shared = jax.nn.silu(gate) * (hidden_states @ shared_up_w) @ shared_down_w
        return shared + routed
    x = L0_attn_x
    x = x + 0.5 * _L0_ffn_ref(_layernorm(x, axis=-1), L0_ffn_router_w, L0_ffn_router_bias, L0_ffn_expert_gate_w, L0_ffn_expert_up_w, L0_ffn_expert_down_w, L0_ffn_conv_w, L0_ffn_shared_up_w, L0_ffn_shared_down_w)
    x = x + _L0_attn_ref(_layernorm(x, axis=-1), L0_attn_proj_w, L0_attn_proj_b, L0_attn_reto_w, L0_attn_reto_b, L0_attn_ln1_g, L0_attn_ln1_b, L0_attn_ln2_g, L0_attn_ln2_b, L0_attn_ffn1_w, L0_attn_ffn1_b, L0_attn_ffn2_w, L0_attn_ffn2_b, L0_attn_lnf_g, L0_attn_lnf_b)
    x = x + 0.5 * _L0_ffn_ref(_layernorm(x, axis=-1), L0_ffn_router_w, L0_ffn_router_bias, L0_ffn_expert_gate_w, L0_ffn_expert_up_w, L0_ffn_expert_down_w, L0_ffn_conv_w, L0_ffn_shared_up_w, L0_ffn_shared_down_w)
    return x

_drawn_inputs = setup_inputs


def setup_inputs(seed=0):
    import zlib

    import numpy as np

    out = dict(_drawn_inputs(seed))
    spreads = {'L0_attn_proj_b': (0.0, 0.1),
     'L0_attn_reto_b': (0.0, 0.1),
     'L0_attn_ln1_g': (1.0, 0.2),
     'L0_attn_ln1_b': (0.0, 0.1),
     'L0_attn_ln2_g': (1.0, 0.6),
     'L0_attn_ln2_b': (0.0, 0.613),
     'L0_attn_ffn1_b': (0.0, 0.1),
     'L0_attn_ffn2_b': (0.0, 0.1),
     'L0_attn_lnf_g': (1.0, 0.2),
     'L0_attn_lnf_b': (0.0, 0.1),
     'L0_ffn_router_bias': (0.0, 0.1)}
    factors = {'L0_ffn_expert_gate_w': 8.0,
     'L0_ffn_expert_up_w': 8.0,
     'L0_ffn_expert_down_w': 8.0,
     'L0_ffn_conv_w': 3.511,
     'L0_ffn_shared_up_w': 3.363,
     'L0_ffn_shared_down_w': 3.477}
    for name, (base, spread) in spreads.items():
        noise = np.random.default_rng([zlib.crc32(name.encode()), seed]).standard_normal(out[name].shape)
        drawn = base * np.exp(spread * noise) if base else spread * noise
        out[name] = jnp.asarray(drawn.astype(out[name].dtype))
    for name, factor in factors.items():
        out[name] = (out[name] * factor).astype(out[name].dtype)
    return out
```

```python
from contextlib import ExitStack

import numpy as np

import concourse.bass as bass
from concourse import mybir

F32 = mybir.dt.float32
F32R = mybir.dt.float32r
U32 = mybir.dt.uint32
ALU = mybir.AluOpType
ACT = mybir.ActivationFunctionType
AX_X = mybir.AxisListType.X

P = 128
B, S, D = 4, 1024, 256
TOK = B * S
TILE = 512
SUB = TILE // P
NT = TOK // TILE
PAIRS = NT // 2
KD = D // P
E = 16
NE = E - 1
TAPS = 3
HALO = TAPS - 1
SHARED_COLS = (TAPS * KD + KD) * P + D
EXPERT_COLS = 2 * KD * P + D
CB_GROUP = 3
GROUPS = NE // CB_GROUP
EPS = 1e-5
CREDIT = 2
CB_CREDIT = 2 * CB_GROUP

NL = 2
H = 16
HD = D // H
F = 4 * D
KF = F // P
HG = P // HD


def split3(tensor, out, w_hi, w_lo, x_hi, x_lo, start, stop):
    tensor.matmul(out, w_hi, x_hi, start=start, stop=False)
    tensor.matmul(out, w_hi, x_lo, start=False, stop=False)
    return tensor.matmul(out, w_lo, x_hi, start=False, stop=stop)


def moe(nc, tag, x_sb, ident, iota16, eps, x_in, out, router_w, router_b, gate_w, up_w, down_w, conv_w,
        shared_up, shared_down, comb_dram):
    with ExitStack() as ctx:
        def sb(name, shape, dt=F32):
            return ctx.enter_context(nc.sbuf_tensor(f"{tag}_{name}", shape, dt))

        sems = []

        def sem(name):
            sems.append(nc.alloc_semaphore(f"{tag}_{name}"))
            return sems[-1]

        w_hi = sb("w_hi", [P, SHARED_COLS + NE * EXPERT_COLS], F32R)
        w_lo = sb("w_lo", [P, SHARED_COLS + NE * EXPERT_COLS], F32R)
        stage = sb("stage", [P, 2, EXPERT_COLS])
        rw_f = sb("rw_f", [P, KD, P])
        rw_hi = sb("rw_hi", [P, KD, P], F32R)
        rw_lo = sb("rw_lo", [P, KD, P], F32R)
        rb = sb("rb", [P, 1])
        xn = sb("xn", [P, 2, SUB, D])
        x_hi = sb("x_hi", [P, 2, KD, HALO + TILE], F32R)
        x_lo = sb("x_lo", [P, 2, KD, HALO + TILE], F32R)
        silu_g = sb("silu_g", [P, 2, TILE])
        weighted = sb("weighted", [P, 2, TILE])
        h = sb("h", [P, 2, TILE])
        h_hi = sb("h_hi", [P, 2, TILE], F32R)
        h_lo = sb("h_lo", [P, 2, TILE], F32R)
        cb = sb("cb", [P, 2, CB_GROUP * TILE])
        oT = sb("oT", [P, KD, TILE])
        stats = sb("stats", [P, SUB, 6])
        mv = sb("mv", [P, SUB, 2])
        std = sb("std", [P, SUB])
        rstd = sb("rstd", [P, SUB])
        lgT = sb("lgT", [P, TILE])
        carrier = sb("carrier", [P, 1])
        lmax = sb("lmax", [P, SUB])
        shifted = sb("shifted", [P, SUB, E])
        ex = sb("ex", [P, SUB, E])
        probs = sb("probs", [P, SUB, E])
        top = sb("top", [P, SUB, 8])
        top_i = sb("top_i", [P, SUB, 8], U32)
        top_f = sb("top_f", [P, SUB, 2])
        sums = sb("sums", [P, SUB])
        norm_w = sb("norm_w", [P, SUB, 2])
        pick = sb("pick", [P, 2, SUB, E])
        comb = sb("comb", [P, 2, SUB, E])
        combT = lgT

        gate_ps = ctx.enter_context(nc.psum_tensor(f"{tag}_gate_ps", [P, 2, TILE], F32))
        up_ps = ctx.enter_context(nc.psum_tensor(f"{tag}_up_ps", [P, 2, TILE], F32))
        acc_ps = ctx.enter_context(nc.psum_tensor(f"{tag}_acc_ps", [P, KD, TILE], F32))
        t_ps = ctx.enter_context(nc.psum_tensor(f"{tag}_t_ps", [P, 2, TILE], F32))

        x0_in, x_rest_in = sem("x0_in"), sem("x_rest_in")
        stage_in = [sem(f"stage_in{i}") for i in range(2)]
        rw_in, rw_zero, rw_hi_done = sem("rw_in"), sem("rw_zero"), sem("rw_hi_done")
        w_hi_done, w_lo_done = sem("w_hi_done"), sem("w_lo_done")
        halo_zero = sem("halo_zero")
        stats_done, var_done, std_done, rstd_done = (
            sem("stats_done"), sem("var_done"), sem("std_done"), sem("rstd_done"))
        xn_done, xT_done, x_hi_done, x_lo_done, halo_done = (
            sem("xn_done"), sem("xT_done"), sem("x_hi_done"), sem("x_lo_done"), sem("halo_done"))
        logits_done, lgT_done, lg_done = sem("logits_done"), sem("lgT_done"), sem("lg_done")
        lmax_done, shifted_done, ex_done = sem("lmax_done"), sem("shifted_done"), sem("ex_done")
        soft_step = sem("soft_step")
        comb_done, combT_ps_done, combT_done = sem("comb_done"), sem("combT_ps_done"), sem("combT_done")
        comb_stored = sem("comb_stored")
        cb_in = [sem(f"cb_in{i}") for i in range(2)]
        gateup_done, silu_done, weighted_done, h_done, h_hi_done, h_lo_done, down_done = (
            sem("gateup_done"), sem("silu_done"), sem("weighted_done"), sem("h_done"),
            sem("h_hi_done"), sem("h_lo_done"), sem("down_done"))
        oT_done, back_done, mixed_done, x_done = (
            sem("oT_done"), sem("back_done"), sem("mixed_done"), sem("x_done"))
        stored = sem("stored")

        def wcol(u):
            return 0 if u == 0 else SHARED_COLS + (u - 1) * EXPERT_COLS

        def cols(u):
            return SHARED_COLS if u == 0 else EXPERT_COLS

        taps, pair = TAPS * KD * P, KD * P
        pieces = [(0, [(0, taps, conv_w)]), (taps, [(0, pair, shared_up), (pair, D, shared_down)])]
        pieces += [(wcol(e + 1), [(0, pair, gate_w[e]), (pair, pair, up_w[e]), (2 * pair, D, down_w[e])])
                   for e in range(NE)]

        def piece_cols(n):
            return sum(width for _, width, _ in pieces[n][1])

        def stage_count(n):
            return 16 * sum(len(pieces[m][1]) for m in range(n % 2, n + 1, 2))

        def tile_view(dram, t):
            return dram.rearrange("(t s p) d -> t p s d", s=SUB, p=P)[t]

        with nc.Block() as block:

            @block.sync
            def _(sp):
                if x_in is not None:
                    sp.dma_start(x_sb[:, 0:SUB, :], tile_view(x_in, 0)).then_inc(x0_in, 16)
                sp.wait_ge(rw_zero, 2)
                sp.dma_start(rw_f[:, :, 0:E], router_w.rearrange("(k p) e -> p k e", p=P)).then_inc(rw_in, 16)
                sp.dma_start(rb[0:E, :], router_b).then_inc(rw_in, 16)
                for n, (_, parts) in enumerate(pieces):
                    if n >= 2:
                        sp.wait_ge(w_lo_done, n)
                    for at, width, src in parts:
                        dst = stage[:, n % 2, at:at + width]
                        if width > D or src.shape[0] > P:
                            dst = dst.rearrange("p (k i) -> p k i", i=P)
                            src = src.rearrange("(k p) i -> p k i", p=P)
                        sp.dma_start(dst, src).then_inc(stage_in[n % 2], 16)

                def store_comb(t, j):
                    sp.wait_ge(combT_done, t + 1)
                    sp.dma_start(comb_dram[j], combT[0:E, :]).then_inc(comb_stored, 16)
                    sp.wait_ge(comb_stored, 16 * (t + 1))

                def load_cb(t, i, j, g):
                    q = 10 * i + 5 * j + g
                    sp.wait_ge(weighted_done, CB_GROUP * (q - 1) + CB_CREDIT)
                    src = comb_dram[j][g * CB_GROUP:(g + 1) * CB_GROUP, :].rearrange("e n -> (e n)")
                    sp.dma_start(cb[:, (5 * j + g) % 2, :], src.partition_broadcast(P)).then_inc(cb_in[(5 * j + g) % 2], 16)

                def tile(i, j, last):
                    t = 2 * i + j
                    for g in range(2, GROUPS):
                        load_cb(t, i, j, g)
                    if not last:
                        ni, nj = (i, 1) if j == 0 else (i + 1, 0)
                        store_comb(t + 1, nj)
                        for g in range(2):
                            load_cb(t + 1, ni, nj, g)
                    if out is not None:
                        sp.wait_ge(x_done, t + 1 + CREDIT)
                        sp.dma_start(tile_view(out, t), x_sb[:, bass.ds(t * SUB, SUB), :]).then_inc(stored, 16)

                store_comb(0, 0)
                for g in range(2):
                    load_cb(0, 0, 0, g)
                with sp.Fori(0, PAIRS - 1) as i:
                    tile(i, 0, False)
                    tile(i, 1, False)
                tile(PAIRS - 1, 0, False)
                tile(PAIRS - 1, 1, True)
                if out is not None:
                    sp.wait_ge(stored, 16 * NT)

            @block.scalar
            def _(act):
                if x_in is not None:
                    for t in range(1, NT):
                        act.dma_start(x_sb[:, t * SUB:(t + 1) * SUB, :], tile_view(x_in, t)).then_inc(x_rest_in, 16)
                act.sem_inc(h_hi_done, CREDIT)
                act.sem_inc(oT_done, CREDIT)

                def root(t):
                    act.wait_ge(var_done, t + 1)
                    nc.scalar.activation(std[:, :], mv[:, :, 1], ACT.Sqrt, bias=eps[:, :]).then_inc(std_done, 1)

                def evacuate_xT(t, j):
                    act.wait_ge(xT_done, t + 1)
                    nc.scalar.activation(x_hi[:, j, :, HALO:], t_ps[:, :, :], ACT.Copy).then_inc(x_hi_done, 1)

                def evacuate_logits(t):
                    act.wait_ge(logits_done, t + 1)
                    nc.scalar.activation(lgT[:, :], t_ps[:, 0, :], ACT.Identity, bias=rb[:, :]).then_inc(lgT_done, 1)

                def exponent(t):
                    act.wait_ge(shifted_done, t + 1)
                    nc.scalar.activation(ex[:, :, :], shifted[:, :, :], ACT.Exp).then_inc(ex_done, 1)

                def evacuate_comb(t):
                    act.wait_ge(combT_ps_done, t + 1)
                    if not isinstance(t, int) or t > 0:
                        act.wait_ge(comb_stored, 16 * t)
                    nc.scalar.activation(combT[0:E, :], t_ps[0:E, 0, :], ACT.Copy).then_inc(combT_done, 1)

                def unit(t, u):
                    n, b = E * t + u, u % 2
                    act.wait_ge(gateup_done, n + 1)
                    nc.scalar.activation(silu_g[:, b, :], gate_ps[:, b, :], ACT.Silu).then_inc(silu_done, 1)
                    act.wait_ge(h_done, n + 1 + CREDIT)
                    act.wait_ge(down_done, n - 1 + CREDIT)
                    nc.scalar.activation(h_hi[:, b, :], h[:, b, :], ACT.Copy).then_inc(h_hi_done, 1)

                def finish(t):
                    act.wait_ge(down_done, E * (t + 1) + CREDIT)
                    nc.scalar.activation(oT[:, :, :], acc_ps[:, :, :], ACT.Copy).then_inc(oT_done, 1)

                def tile(i, j, last):
                    t = 2 * i + j
                    for u in range(1, E):
                        unit(t, u)
                        if not last:
                            if u == 1:
                                root(t + 1)
                            if u == 4:
                                evacuate_xT(t + 1, 1 - j)
                            if u == 6:
                                evacuate_logits(t + 1)
                            if u == 8:
                                exponent(t + 1)
                            if u == 12:
                                evacuate_comb(t + 1)
                    if not last:
                        unit(t + 1, 0)
                    finish(t)

                root(0)
                evacuate_xT(0, 0)
                evacuate_logits(0)
                exponent(0)
                evacuate_comb(0)
                unit(0, 0)
                with act.Fori(0, PAIRS - 1) as i:
                    tile(i, 0, False)
                    tile(i, 1, False)
                tile(PAIRS - 1, 0, False)
                tile(PAIRS - 1, 1, True)

            @block.gpsimd
            def _(pool):
                pool.memset(rw_f[:, :, :], 0.0).then_inc(rw_zero, 1)
                pool.memset(rb[:, :], 0.0).then_inc(rw_zero, 1)
                pool.memset(x_hi[:, 0, :, 0:HALO].bitcast(F32), 0.0).then_inc(halo_zero, 1)
                pool.memset(x_lo[:, 0, :, 0:HALO].bitcast(F32), 0.0).then_inc(halo_zero, 1)
                pool.sem_inc(weighted_done, CB_CREDIT)
                pool.wait_ge(rw_hi_done, 1)
                pool.tensor_tensor(rw_lo[:, :, :], rw_f[:, :, :], rw_hi[:, :, :].bitcast(F32), ALU.subtract).then_inc(w_lo_done, 1)
                for n, (a, _) in enumerate(pieces):
                    width = piece_cols(n)
                    pool.wait_ge(w_hi_done, n + 1)
                    pool.tensor_tensor(w_lo[:, a:a + width], stage[:, n % 2, 0:width],
                                       w_hi[:, a:a + width].bitcast(F32), ALU.subtract).then_inc(w_lo_done, 1)

                def unit(t, i, j, u):
                    n, e = E * t + u, u - 1
                    g = e // CB_GROUP
                    slot, loads = (5 * j + g) % 2, 5 * i + (5 * j + g) // 2
                    if e % CB_GROUP == 0:
                        pool.wait_ge(cb_in[slot], 16 * (loads + 1))
                    pool.wait_ge(silu_done, n + 1)
                    pool.wait_ge(h_done, n - 1 + CREDIT)
                    pool.tensor_tensor(weighted[:, u % 2, :], silu_g[:, u % 2, :],
                                       cb[:, slot, (e % CB_GROUP) * TILE:(e % CB_GROUP + 1) * TILE],
                                       ALU.mult).then_inc(weighted_done, 1)

                def tile(i, j):
                    t = 2 * i + j
                    for u in range(1, E):
                        unit(t, i, j, u)

                with pool.Fori(0, PAIRS) as i:
                    tile(i, 0)
                    tile(i, 1)

            @block.vector
            def _(dve):
                dve.sem_inc(h_done, CREDIT)
                dve.sem_inc(x_done, CREDIT)
                dve.wait_ge(rw_in, 32)
                dve.tensor_copy(rw_hi[:, :, :], rw_f[:, :, :]).then_inc(rw_hi_done, 1)

                def split_weights(n):
                    a, width = pieces[n][0], piece_cols(n)
                    dve.wait_ge(stage_in[n % 2], stage_count(n))
                    dve.tensor_copy(w_hi[:, a:a + width], stage[:, n % 2, 0:width]).then_inc(w_hi_done, 1)

                def statistics(t):
                    if x_in is not None:
                        if isinstance(t, int) and t == 0:
                            dve.wait_ge(x0_in, 16)
                        else:
                            dve.wait_ge(x_rest_in, 16 * (NT - 1))
                    for s in range(SUB):
                        last = dve.bn_stats(stats[:, s, :], x_sb[:, t * SUB + s, :])
                    last.then_inc(stats_done, 1)
                    dve.wait_ge(stats_done, t + 1)
                    dve.memset(carrier[:, :], 0.0)
                    for s in range(SUB):
                        last = dve.bn_aggr(mv[:, s, :], stats[:, s, :])
                    last.then_inc(var_done, 1)

                def normalise(t, j):
                    dve.wait_ge(std_done, t + 1)
                    dve.reciprocal(rstd[:, :], std[:, :]).then_inc(rstd_done, 1)
                    dve.wait_ge(rstd_done, t + 1)
                    for s in range(SUB):
                        last = dve.tensor_scalar(xn[:, j, s, :], x_sb[:, t * SUB + s, :], mv[:, s, 0:1],
                                                 rstd[:, s:s + 1], ALU.subtract, ALU.mult)
                    last.then_inc(xn_done, 1)

                def low_parts(t, j):
                    if j == 1:
                        dve.wait_ge(x_lo_done, t)
                        dve.tensor_copy(x_lo[:, 1, :, 0:HALO], x_lo[:, 0, :, TILE:]).then_inc(halo_done, 1)
                        dve.tensor_copy(x_hi[:, 1, :, 0:HALO], x_hi[:, 0, :, TILE:]).then_inc(halo_done, 1)
                    dve.wait_ge(x_hi_done, t + 1)
                    dve.tensor_tensor(x_lo[:, j, :, HALO:], t_ps[:, :, :], x_hi[:, j, :, HALO:].bitcast(F32),
                                      ALU.subtract).then_inc(x_lo_done, 1)

                def take_maximum(t):
                    dve.wait_ge(lg_done, t + 1)
                    lg = t_ps[:, 1, :].rearrange("p (s e) -> p s e", e=P)[:, :, 0:E]
                    dve.reduce_max(lmax[:, :], lg, AX_X).then_inc(lmax_done, 1)
                    dve.wait_ge(lmax_done, t + 1)
                    dve.tensor_tensor(shifted[:, :, :], lg, lmax[:, :].unsqueeze(2).broadcast_to([P, SUB, E]),
                                      ALU.subtract).then_inc(shifted_done, 1)

                SOFT_STEPS = 10

                def choose(t, j):
                    step = [0]

                    def link(ins):
                        step[0] += 1
                        ins.then_inc(soft_step, 1)
                        dve.wait_ge(soft_step, t * SOFT_STEPS + step[0])

                    dve.wait_ge(ex_done, t + 1)
                    link(dve.reduce_sum(sums[:, :], ex[:, :, :], AX_X))
                    link(dve.reciprocal(sums[:, :], sums[:, :]))
                    link(dve.tensor_tensor(probs[:, :, :], ex[:, :, :], sums[:, :].unsqueeze(2).broadcast_to([P, SUB, E]), ALU.mult))
                    dve.memset(carrier[:, :], 0.0)
                    for s in range(SUB):
                        last = dve.max(top[:, s, :], probs[:, s, :])
                    link(last)
                    dve.memset(carrier[:, :], 0.0)
                    for s in range(SUB):
                        dve.max_index(top_i[:, s, :], top[:, s, :], probs[:, s, :])
                    link(dve.tensor_tensor(sums[:, :], top[:, :, 0], top[:, :, 1], ALU.add))
                    dve.tensor_copy(top_f[:, :, :], top_i[:, :, 0:2])
                    link(dve.tensor_scalar_add(sums[:, :], sums[:, :], 1e-6))
                    link(dve.reciprocal(sums[:, :], sums[:, :]))
                    link(dve.tensor_tensor(norm_w[:, :, :], top[:, :, 0:2], sums[:, :].unsqueeze(2).broadcast_to([P, SUB, 2]), ALU.mult))
                    for k in range(2):
                        last = dve.tensor_tensor(pick[:, k, :, :], iota16[:, :].unsqueeze(1).broadcast_to([P, SUB, E]),
                                                 top_f[:, :, k:k + 1].broadcast_to([P, SUB, E]), ALU.is_equal)
                    link(last)
                    for k in range(2):
                        last = dve.tensor_tensor(pick[:, k, :, :], pick[:, k, :, :],
                                                 norm_w[:, :, k:k + 1].broadcast_to([P, SUB, E]), ALU.mult)
                    link(last)
                    assert step[0] == SOFT_STEPS
                    dve.tensor_tensor(comb[:, j, :, :], pick[:, 0, :, :], pick[:, 1, :, :], ALU.add).then_inc(comb_done, 1)

                def unit(t, u):
                    n, b = E * t + u, u % 2
                    if u == 0:
                        dve.wait_ge(silu_done, n + 1)
                        gate = silu_g[:, b, :]
                    else:
                        dve.wait_ge(weighted_done, NE * t + u + CB_CREDIT)
                        gate = weighted[:, b, :]
                    dve.tensor_tensor(h[:, b, :], gate, up_ps[:, b, :], ALU.mult).then_inc(h_done, 1)
                    dve.wait_ge(h_hi_done, n + 1 + CREDIT)
                    dve.tensor_tensor(h_lo[:, b, :], h[:, b, :], h_hi[:, b, :].bitcast(F32), ALU.subtract).then_inc(h_lo_done, 1)

                def finish(t, j):
                    dve.wait_ge(back_done, t + 1)
                    back = t_ps[:, :, :].rearrange("p a n -> p (a n)").rearrange("p (s d) -> p s d", d=D)
                    for s in range(SUB):
                        last = dve.scalar_tensor_tensor(xn[:, j, s, :], xn[:, j, s, :], comb[:, j, s, E - 1:E],
                                                        back[:, s, :], ALU.mult, ALU.add)
                    last.then_inc(mixed_done, 1)
                    dve.wait_ge(mixed_done, t + 1)
                    for s in range(SUB):
                        last = dve.scalar_tensor_tensor(x_sb[:, t * SUB + s, :], xn[:, j, s, :], 0.5,
                                                        x_sb[:, t * SUB + s, :], ALU.mult, ALU.add)
                    last.then_inc(x_done, 1)

                def tile(i, j, last):
                    t = 2 * i + j
                    for u in range(1, E):
                        unit(t, u)
                        if not last:
                            if u == 1:
                                statistics(t + 1)
                            if u == 2:
                                normalise(t + 1, 1 - j)
                            if u == 4:
                                low_parts(t + 1, 1 - j)
                            if u == 8:
                                take_maximum(t + 1)
                            if u == 9:
                                choose(t + 1, 1 - j)
                    if not last:
                        unit(t + 1, 0)
                    finish(t, j)

                statistics(0)
                normalise(0, 0)
                split_weights(0)
                low_parts(0, 0)
                split_weights(1)
                take_maximum(0)
                choose(0, 0)
                for n in range(2, len(pieces)):
                    split_weights(n)
                unit(0, 0)
                with dve.Fori(0, PAIRS - 1) as i:
                    tile(i, 0, False)
                    tile(i, 1, False)
                tile(PAIRS - 1, 0, False)
                tile(PAIRS - 1, 1, True)

            @block.tensor
            def _(pe):
                pe.sem_inc(down_done, CREDIT)

                def turn_x(t, j):
                    pe.wait_ge(xn_done, t + 1)
                    pe.wait_ge(x_done, t - 1 + CREDIT)
                    for k in range(KD):
                        for s in range(SUB):
                            last = pe.transpose(t_ps[:, k, s * P:(s + 1) * P], xn[:, j, s, k * P:(k + 1) * P], ident[:, :])
                    last.then_inc(xT_done, 1)

                def route(t, j):
                    pe.wait_ge(x_lo_done, t + 1)
                    pe.wait_ge(w_lo_done, 1)
                    for k in range(KD):
                        last = split3(pe, t_ps[:, 0, :], rw_hi[:, k, :], rw_lo[:, k, :], x_hi[:, j, k, HALO:],
                                      x_lo[:, j, k, HALO:], k == 0, k == KD - 1)
                    last.then_inc(logits_done, 1)

                def turn_logits(t):
                    pe.wait_ge(lgT_done, t + 1)
                    for s in range(SUB):
                        last = pe.transpose(t_ps[:, 1, s * P:(s + 1) * P], lgT[:, s * P:(s + 1) * P], ident[:, :])
                    last.then_inc(lg_done, 1)

                def turn_comb(t, j):
                    pe.wait_ge(comb_done, t + 1)
                    for s in range(SUB):
                        last = pe.transpose(t_ps[0:E, 0, s * P:(s + 1) * P], comb[:, j, s, :], ident[:, :])
                    last.then_inc(combT_ps_done, 1)

                def gateup(t, j, u):
                    n, b = E * t + u, u % 2
                    pe.wait_ge(w_lo_done, u + 3)
                    pe.wait_ge(h_done, n - 1 + CREDIT)
                    a = wcol(u)
                    if u == 0:
                        if j == 1:
                            pe.wait_ge(halo_done, t + 1)
                        if j == 0:
                            pe.wait_ge(halo_zero, 2)
                        taps = TAPS
                    else:
                        taps = 1
                    for c in range(taps):
                        lead = c if u == 0 else HALO
                        for k in range(KD):
                            w = slice(a + (c * KD + k) * P, a + (c * KD + k + 1) * P)
                            split3(pe, gate_ps[:, b, :], w_hi[:, w], w_lo[:, w], x_hi[:, j, k, lead:lead + TILE],
                                   x_lo[:, j, k, lead:lead + TILE], c == 0 and k == 0, c == taps - 1 and k == KD - 1)
                    a += taps * KD * P
                    for k in range(KD):
                        w = slice(a + k * P, a + (k + 1) * P)
                        last = split3(pe, up_ps[:, b, :], w_hi[:, w], w_lo[:, w], x_hi[:, j, k, HALO:],
                                      x_lo[:, j, k, HALO:], k == 0, k == KD - 1)
                    last.then_inc(gateup_done, 1)

                def down(t, u):
                    n, b = E * t + u, u % 2
                    pe.wait_ge(h_lo_done, n + 1)
                    if u == 0:
                        pe.wait_ge(oT_done, t + CREDIT)
                    a = wcol(u) + cols(u) - D
                    for k in range(KD):
                        w = slice(a + k * P, a + (k + 1) * P)
                        last = split3(pe, acc_ps[:, k, :], w_hi[:, w], w_lo[:, w], h_hi[:, b, :], h_lo[:, b, :],
                                      u == 0, u == E - 1)
                    last.then_inc(down_done, 1)

                def turn_back(t, last):
                    pe.wait_ge(oT_done, t + 1 + CREDIT)
                    if not last:
                        pe.wait_ge(combT_done, t + 2)
                    back = t_ps[:, :, :].rearrange("p a n -> p (a n)")
                    for s in range(SUB):
                        for k in range(KD):
                            done = pe.transpose(back[:, s * D + k * P:s * D + (k + 1) * P], oT[:, k, s * P:(s + 1) * P], ident[:, :])
                    done.then_inc(back_done, 1)

                def tile(i, j, last):
                    t = 2 * i + j
                    for u in range(E):
                        if u + 2 < E:
                            gateup(t, j, u + 2)
                        elif not last:
                            gateup(t + 1, 1 - j, u + 2 - E)
                        down(t, u)
                        if not last:
                            if u == 2:
                                turn_x(t + 1, 1 - j)
                            if u == 5:
                                route(t + 1, 1 - j)
                            if u == 7:
                                turn_logits(t + 1)
                            if u == 11:
                                turn_comb(t + 1, 1 - j)
                    turn_back(t, last)

                turn_x(0, 0)
                route(0, 0)
                turn_logits(0)
                turn_comb(0, 0)
                gateup(0, 0, 0)
                gateup(0, 0, 1)
                with pe.Fori(0, PAIRS - 1) as i:
                    tile(i, 0, False)
                    tile(i, 1, False)
                tile(PAIRS - 1, 0, False)
                tile(PAIRS - 1, 1, True)

        hand_back(nc, sems)


def hand_back(nc, sems):
    nc.clear_and_free_semaphores(sems)
    nc.all_engine_barrier()


def retention_layer(nc, layer, h_sb, ident, eps, ins, x_dram):
    first, final = layer == 0, layer == NL - 1
    tag = f"l{layer}"
    with ExitStack() as ctx:
        def sb(name, shape, dt=F32):
            return ctx.enter_context(nc.sbuf_tensor(f"{tag}_{name}", shape, dt))

        sems = []

        def sem(name):
            sems.append(nc.alloc_semaphore(f"{tag}_{name}"))
            return sems[-1]

        def halves(name, shape):
            return sb(name + "_hi", shape, F32R), sb(name + "_lo", shape, F32R)

        wp_hi, wp_lo = halves("wp", [P, KD, 4 * D])
        wr_hi, wr_lo = halves("wr", [P, KD, D])
        w1_hi, w1_lo = halves("w1", [P, KD, F])
        w2_hi, w2_lo = halves("w2", [P, KF, D])
        decay = sb("decay", [P, H * P])
        key_decay = sb("key_decay", [P, D])
        query_decay = sb("query_decay", [P, KD, P])
        state_decay = sb("state_decay", [P, KD])
        own_head = sb("own_head", [P, P])
        head_mask = sb("head_mask", [P, HG])
        norm1 = sb("norm1", [P, 2, KD])
        norm2 = sb("norm2", [P, 2, KD])
        proj_b = sb("proj_b", [P, 8])
        ffn1_b = sb("ffn1_b", [P, KF])
        ffn2_b = sb("ffn2_b", [P, KD])
        v_b = sb("v_b", [P, D])
        reto_b = sb("reto_b", [P, D])
        if final:
            normf = sb("normf", [P, 2, D])
            x_old = sb("x_old", [P, SUB, D])
        carrier = sb("carrier", [P, 1])

        xn = sb("xn", [P, SUB, D])
        full = sb("full", [P, KD, TILE])
        a_hi, a_lo = halves("a", [P, KD, TILE])
        b_hi, b_lo = halves("b", [P, KD, TILE])
        q = sb("q", [P, KD, TILE])
        gated = q
        qs = sb("qs", [P, KD, TILE])
        kT = sb("kT", [P, KD, TILE])
        gate = sb("gate", [P, KD, TILE])
        v = sb("v", [P, SUB, D])
        q_wide = sb("q_wide", [P, KD, HG, P])
        v_wide = sb("v_wide", [P, KD, HG * (P + HD)])
        probs = sb("probs", [P, H * P])
        stage = probs[:, :].rearrange("p (b n) -> p b n", b=2)
        ks = sb("ks", [P, D])
        state = sb("state", [P, KD, P])
        fresh = sb("fresh", [P, KD, P])
        g_hi, g_lo = halves("g", [P, KD, TILE])
        act_f = sb("act_f", [P, 2, TILE])
        f_hi, f_lo = halves("f", [P, 2, TILE])
        oT = sb("oT", [P, KD, TILE])

        banks = ctx.enter_context(nc.psum_tensor(f"{tag}_banks", [P, 4, TILE], F32))
        t_ps = ctx.enter_context(nc.psum_tensor(f"{tag}_t_ps", [P, 2, TILE], F32))
        ret_ps = ctx.enter_context(nc.psum_tensor(f"{tag}_ret_ps", [P, TILE], F32))
        m_ps = ctx.enter_context(nc.psum_tensor(f"{tag}_m_ps", [P, TILE], F32))
        token_ps = banks[:, 0:2, :].rearrange("p a n -> p (a n)").rearrange("p (s d) -> p s d", d=D)
        back_ps = t_ps[:, :, :].rearrange("p a n -> p (a n)").rearrange("p (s d) -> p s d", d=D)

        const_in = sem("const_in")
        stage_in = [sem(f"stage_in{i}") for i in range(2)]
        w_hi_done, w_lo_done, wide_zero = sem("w_hi_done"), sem("w_lo_done"), sem("wide_zero")
        xn0_done, xn_done, xn2_done = sem("xn0_done"), sem("xn_done"), sem("xn2_done")
        aT_done, a_full, a_hi_done, a_lo_done = sem("aT_done"), sem("a_full"), sem("a_hi_done"), sem("a_lo_done")
        bT_done, b_full, b_hi_done, b_lo_done = sem("bT_done"), sem("b_full"), sem("b_hi_done"), sem("b_lo_done")
        proj_done, q_done, k_done, gate_done, v_done, qs_done = (
            sem("proj_done"), sem("q_done"), sem("k_done"), sem("gate_done"), sem("v_done"), sem("qs_done"))
        wide_q_done, wide_v_done = sem("wide_q_done"), sem("wide_v_done")
        scores_done, probs_done, kturn_done, ks_done = (
            sem("scores_done"), sem("probs_done"), sem("kturn_done"), sem("ks_done"))
        ret_done, gated_done, st_done, fresh_done, state_done = (
            sem("ret_done"), sem("gated_done"), sem("st_done"), sem("fresh_done"), sem("state_done"))
        g_hi_done, g_lo_done, reto_done, reto_read, reto_added = (
            sem("g_hi_done"), sem("g_lo_done"), sem("reto_done"), sem("reto_read"), sem("reto_added"))
        ffn1_done, act_done, f_hi_done, f_lo_done, ffn2_done = (
            sem("ffn1_done"), sem("act_done"), sem("f_hi_done"), sem("f_lo_done"), sem("ffn2_done"))
        oT_done, back_done, added = sem("oT_done"), sem("back_done"), sem("added")
        x_old_in, final_step, final_done = sem("x_old_in"), sem("final_step"), sem("final_done")
        norms = {}
        for kind in ("0", "1", "2", "f"):
            norms[kind] = (sb(f"stats{kind}", [P, SUB, 6]), sb(f"mv{kind}", [P, SUB, 2]), sb(f"std{kind}", [P, SUB]),
                           sb(f"rstd{kind}", [P, SUB]), sem(f"stats{kind}_done"), sem(f"var{kind}_done"),
                           sem(f"std{kind}_done"), sem(f"rstd{kind}_done"))

        def rows(w, k, n=1):
            return w[k * P:(k + n) * P, :].rearrange("(k p) i -> p k i", p=P)

        proj_w, reto_w, ffn1_w, ffn2_w = (ins[n][layer] for n in ("proj_w", "reto_w", "ffn1_w", "ffn2_w"))
        half = KF // 2
        pieces = [(wp_hi[:, k:k + 1, :], wp_lo[:, k:k + 1, :], rows(proj_w, k)) for k in range(KD)]
        pieces += [(wr_hi[:, :, :], wr_lo[:, :, :], rows(reto_w, 0, KD))]
        pieces += [(w1_hi[:, k:k + 1, :], w1_lo[:, k:k + 1, :], rows(ffn1_w, k)) for k in range(KD)]
        pieces += [(w2_hi[:, k:k + half, :], w2_lo[:, k:k + half, :], rows(ffn2_w, k, half)) for k in (0, half)]
        PROJ_READY, RETO_READY, FFN_READY = KD, KD + 1, len(pieces)

        def staged(n):
            blocks, width = pieces[n][2].shape[1:]
            return stage[:, n % 2, 0:blocks * width].rearrange("p (k i) -> p k i", k=blocks)

        consts = [(decay[:, :], ins["decay"]), (key_decay[:, :], ins["key_decay"]),
                  (query_decay[:, :, :], ins["query_decay"]), (state_decay[:, :], ins["state_decay"]),
                  (own_head[:, :], ins["own_head"]), (head_mask[:, :], ins["head_mask"]),
                  (norm1[:, 0, :], ins["ln1_g"][layer]), (norm1[:, 1, :], ins["ln1_b"][layer]),
                  (norm2[:, 0, :], ins["ln2_g"][layer]), (norm2[:, 1, :], ins["ln2_b"][layer]),
                  (proj_b[:, :], ins["proj_b_cols"][layer]), (ffn1_b[:, :], ins["ffn1_b"][layer]),
                  (ffn2_b[:, :], ins["ffn2_b"][layer]),
                  (v_b[:, :], ins["proj_b"][layer, 2 * D:3 * D].partition_broadcast(P)),
                  (reto_b[:, :], ins["reto_b"][layer].partition_broadcast(P))]
        if final:
            consts += [(normf[:, 0, :], ins["lnf_g"].partition_broadcast(P)),
                       (normf[:, 1, :], ins["lnf_b"].partition_broadcast(P))]
        consts_ready = 16 * len(consts)
        UPDATES = 2 * SUB - 1

        def steps(engine, step):
            step(0, 0, 0, None, True)
            with engine.Fori(0, PAIRS - 1) as i:
                step(2 * i + 1, 1, i, 2 * i, True)
                step(2 * i + 2, 0, i + 1, 2 * i + 1, True)
            step(NT - 1, 1, PAIRS - 1, NT - 2, False)
            step(None, None, None, NT - 1, False)

        with nc.Block() as block:

            @block.sync
            def _(sp):
                for n, (_, _, src) in enumerate(pieces):
                    if n >= 2:
                        sp.wait_ge(w_lo_done, n - 1)
                    sp.dma_start(staged(n), src).then_inc(stage_in[n % 2], 16)
                if final:
                    view = x_dram.rearrange("(t s p) d -> t p s d", s=SUB, p=P)
                    sp.dma_start(x_old[:, :, :], view[0]).then_inc(x_old_in, 16)
                    with sp.Fori(1, NT) as t:
                        sp.wait_ge(final_done, t)
                        sp.dma_start(x_old[:, :, :], view[t]).then_inc(x_old_in, 16)

            @block.scalar
            def _(act):
                for dst, src in consts:
                    act.dma_start(dst, src).then_inc(const_in, 16)

                def root(kind, t):
                    _, mv, std, _, _, var_done, std_done, _ = norms[kind]
                    act.wait_ge(var_done, t + 1)
                    nc.scalar.activation(std[:, :], mv[:, :, 1], ACT.Sqrt, bias=eps[:, :]).then_inc(std_done, 1)

                def high(full_sem, hi, done, t):
                    act.wait_ge(full_sem, t + 1)
                    nc.scalar.activation(hi[:, :, :], full[:, :, :], ACT.Copy).then_inc(done, 1)

                def first_norms(t):
                    if first:
                        root("0", t)
                    root("1", t)

                def project(a):
                    for g in range(KD):
                        act.wait_ge(proj_done, 10 * a + g + 1)
                        nc.scalar.activation(q[:, g, :], banks[:, g, :], ACT.Identity, bias=proj_b[:, g:g + 1]).then_inc(q_done, 1)
                    for g in range(KD):
                        act.wait_ge(proj_done, 10 * a + g + 3)
                        nc.scalar.activation(kT[:, g, :], banks[:, 2 + g, :], ACT.Identity, bias=proj_b[:, 2 + g:3 + g]).then_inc(k_done, 1)
                    for g in range(KD):
                        act.wait_ge(proj_done, 10 * a + g + 5)
                        nc.scalar.activation(gate[:, g, :], banks[:, g, :], ACT.Silu, bias=proj_b[:, 6 + g:7 + g]).then_inc(gate_done, 1)

                def widen_values(a, c):
                    cc = SUB * a + c
                    act.wait_ge(v_done, cc + 1)
                    act.wait_ge(ret_done, 2 * cc + CREDIT)
                    blocks = v_wide[:, :, :].rearrange("p g (h x) -> p g h x", h=HG)
                    for g in range(KD):
                        last = nc.scalar.activation(blocks[:, g, :, 0:HD], v[:, c, g * P:(g + 1) * P].rearrange("p (h x) -> p h x", h=HG), ACT.Copy)
                    last.then_inc(wide_v_done, 1)

                def feed(b, f):
                    n, slot = KF * b + f, f % 2
                    act.wait_ge(ffn1_done, n + 1)
                    act.wait_ge(f_lo_done, n - 1 + CREDIT)
                    nc.scalar.activation(act_f[:, slot, :], banks[:, slot, :], ACT.Gelu, bias=ffn1_b[:, f:f + 1]).then_inc(act_done, 1)
                    act.wait_ge(ffn2_done, n - 1 + CREDIT)
                    nc.scalar.activation(f_hi[:, slot, :], banks[:, slot, :], ACT.Gelu, bias=ffn1_b[:, f:f + 1]).then_inc(f_hi_done, 1)

                def step(a, j, batch, b, more):
                    if a is not None:
                        project(a)
                        widen_values(a, 0)
                        widen_values(a, 1)
                        widen_values(a, 2)
                    if b is not None:
                        high(b_full, b_hi, b_hi_done, b)
                    if a is not None:
                        widen_values(a, 3)
                        if more:
                            first_norms(a + 1)
                        act.wait_ge(gated_done, SUB * (a + 1))
                        nc.scalar.activation(g_hi[:, :, :], gated[:, :, :], ACT.Copy).then_inc(g_hi_done, 1)
                    if b is not None:
                        for f in range(KF):
                            feed(b, f)
                            if f == 5 and more:
                                high(a_full, a_hi, a_hi_done, a + 1)
                        act.wait_ge(ffn2_done, KF * (b + 1) + CREDIT)
                        for k in range(KD):
                            last = nc.scalar.activation(oT[:, k, :], banks[:, 2 + k, :], ACT.Identity, bias=ffn2_b[:, k:k + 1])
                        last.then_inc(oT_done, 1)
                    elif more:
                        high(a_full, a_hi, a_hi_done, a + 1)
                    if a is not None:
                        root("2", a)
                    if b is not None and final:
                        root("f", b)

                act.wait_ge(const_in, consts_ready)
                act.wait_ge(wide_zero, 1)
                first_norms(0)
                high(a_full, a_hi, a_hi_done, 0)
                steps(act, step)

            @block.gpsimd
            def _(pool):
                pool.memset(v_wide[:, :, :], 0.0).then_inc(wide_zero, 1)

                def widen_queries(a, c):
                    cc = SUB * a + c
                    for g in range(KD):
                        if g == 0:
                            pool.wait_ge(q_done, KD * (a + 1))
                        pool.wait_ge(scores_done, 2 * cc - 1 + g + CREDIT)
                        pool.tensor_tensor(q_wide[:, g, :, :],
                                           q[:, g, c * P:(c + 1) * P].unsqueeze(1).broadcast_to([P, HG, P]),
                                           head_mask[:, :].unsqueeze(2).broadcast_to([P, HG, P]), ALU.mult).then_inc(wide_q_done, 1)

                def low(hi_sem, source, hi, lo, done, t):
                    pool.wait_ge(hi_sem, t + 1)
                    pool.tensor_tensor(lo[:, :, :], source[:, :, :], hi[:, :, :].bitcast(F32), ALU.subtract).then_inc(done, 1)

                def step(a, j, batch, b, more):
                    if a is not None:
                        for c in range(SUB):
                            widen_queries(a, c)
                    if b is not None:
                        low(b_hi_done, full, b_hi, b_lo, b_lo_done, b)
                    if a is not None:
                        low(g_hi_done, gated, g_hi, g_lo, g_lo_done, a)
                        if more:
                            low(a_hi_done, full, a_hi, a_lo, a_lo_done, a + 1)

                for n, (hi, lo, _) in enumerate(pieces):
                    pool.wait_ge(w_hi_done, n + 1)
                    pool.tensor_tensor(lo, staged(n), hi.bitcast(F32), ALU.subtract).then_inc(w_lo_done, 1)
                    if n == KD - 1:
                        low(a_hi_done, full, a_hi, a_lo, a_lo_done, 0)
                pool.wait_ge(const_in, consts_ready)
                pool.wait_ge(wide_zero, 1)
                steps(pool, step)

            @block.vector
            def _(dve):
                dve.sem_inc(f_lo_done, CREDIT)
                dve.sem_inc(added, CREDIT)

                def tile_of(t, s=None):
                    if s is None:
                        return h_sb[:, bass.ds(t * SUB, SUB), :]
                    return h_sb[:, t * SUB + s, :]

                def normalise(kind, t, dst):
                    stats, mv, std, rstd, stats_done, var_done, std_done, rstd_done = norms[kind]
                    dve.memset(carrier[:, :], 0.0)
                    for s in range(SUB):
                        last = dve.bn_stats(stats[:, s, :], tile_of(t, s))
                    last.then_inc(stats_done, 1)
                    dve.wait_ge(stats_done, t + 1)
                    dve.memset(carrier[:, :], 0.0)
                    for s in range(SUB):
                        last = dve.bn_aggr(mv[:, s, :], stats[:, s, :])
                    last.then_inc(var_done, 1)
                    dve.wait_ge(std_done, t + 1)
                    dve.reciprocal(rstd[:, :], std[:, :]).then_inc(rstd_done, 1)
                    dve.wait_ge(rstd_done, t + 1)
                    for s in range(SUB):
                        last = dve.tensor_scalar(dst(s), tile_of(t, s), mv[:, s, 0:1], rstd[:, s:s + 1],
                                                 ALU.subtract, ALU.mult)
                    return last

                def first_norms(t):
                    if first:
                        normalise("0", t, lambda s: tile_of(t, s)).then_inc(xn0_done, 1)
                        dve.wait_ge(xn0_done, t + 1)
                    normalise("1", t, lambda s: xn[:, s, :]).then_inc(xn_done, 1)

                def scale(turned, norm, done, t):
                    dve.wait_ge(turned, t + 1)
                    for k in range(KD):
                        last = dve.tensor_scalar(full[:, k, :], t_ps[:, k, :], norm[:, 0, k:k + 1], norm[:, 1, k:k + 1],
                                                 ALU.mult, ALU.add)
                    last.then_inc(done, 1)

                def project(a):
                    dve.wait_ge(q_done, KD * (a + 1))
                    for g in range(KD):
                        last = dve.tensor_tensor(qs[:, g, :].rearrange("p (c n) -> p c n", n=P),
                                                 q[:, g, :].rearrange("p (c n) -> p c n", n=P),
                                                 query_decay[:, g:g + 1, :].broadcast_to([P, SUB, P]), ALU.mult)
                    last.then_inc(qs_done, 1)
                    for s in range(SUB):
                        dve.wait_ge(proj_done, 10 * a + 7 + s)
                        dve.tensor_tensor(v[:, s, :], banks[:, 2 + s % 2, 0:D], v_b[:, :], ALU.add).then_inc(v_done, 1)

                def decayed(a, c, j):
                    cc, w = SUB * a + c, 4 * P
                    dve.wait_ge(scores_done, 2 * cc + j // 2 + 1 + CREDIT)
                    dve.wait_ge(ret_done, 2 * cc - 1 + j // 2 + CREDIT)
                    dve.tensor_tensor(probs[:, j * w:(j + 1) * w], banks[:, j, :], decay[:, j * w:(j + 1) * w],
                                      ALU.mult).then_inc(probs_done, 1)

                def decay_keys(a, c, n):
                    dve.wait_ge(kturn_done, n + 1)
                    dve.tensor_tensor(ks[:, :], m_ps[:, 0:D], key_decay[:, :], ALU.mult).then_inc(ks_done, 1)

                def gate_result(a, c):
                    cc = SUB * a + c
                    dve.wait_ge(ret_done, 2 * (cc + 1) + CREDIT)
                    part = slice(c * P, (c + 1) * P)
                    dve.tensor_tensor(gated[:, :, part], ret_ps[:, 0:KD * P].rearrange("p (g n) -> p g n", g=KD),
                                      gate[:, :, part], ALU.mult).then_inc(gated_done, 1)

                def update_state(batch, k):
                    dve.wait_ge(st_done, UPDATES * batch + k + 1)
                    part = m_ps[:, D:2 * D].rearrange("p (g n) -> p g n", g=KD)
                    mask = own_head[:, :].unsqueeze(1).broadcast_to([P, KD, P])
                    if k == 0:
                        dve.tensor_tensor(state[:, :, :], part, mask, ALU.mult).then_inc(state_done, 1)
                        return
                    dve.tensor_tensor(fresh[:, :, :], part, mask, ALU.mult).then_inc(fresh_done, 1)
                    dve.wait_ge(fresh_done, (UPDATES - 1) * batch + k)
                    for g in range(KD):
                        last = dve.scalar_tensor_tensor(state[:, g, :], state[:, g, :], state_decay[:, g:g + 1],
                                                        fresh[:, g, :], ALU.mult, ALU.add)
                    last.then_inc(state_done, 1)

                def feed(b, f):
                    dve.wait_ge(f_hi_done, KF * b + f + 1)
                    dve.tensor_tensor(f_lo[:, f % 2, :], act_f[:, f % 2, :], f_hi[:, f % 2, :].bitcast(F32),
                                      ALU.subtract).then_inc(f_lo_done, 1)

                def add_retention(a):
                    dve.wait_ge(reto_done, a + 1)
                    dve.tensor_tensor(tile_of(a), tile_of(a), token_ps, ALU.add).then_inc(reto_read, 1)
                    dve.wait_ge(reto_read, a + 1)
                    dve.tensor_tensor(tile_of(a), tile_of(a), reto_b[:, :].unsqueeze(1).broadcast_to([P, SUB, D]),
                                      ALU.add).then_inc(reto_added, 1)
                    dve.wait_ge(reto_added, a + 1)
                    normalise("2", a, lambda s: xn[:, s, :]).then_inc(xn2_done, 1)

                def add_feed(b):
                    dve.wait_ge(back_done, b + 1)
                    dve.tensor_tensor(tile_of(b), tile_of(b), back_ps, ALU.add).then_inc(added, 1)
                    if not final:
                        return
                    dve.wait_ge(added, b + 1 + CREDIT)
                    normalise("f", b, lambda s: tile_of(b, s)).then_inc(final_step, 1)
                    for r, op in ((0, ALU.mult), (1, ALU.add)):
                        dve.wait_ge(final_step, 3 * b + r + 1)
                        dve.tensor_tensor(tile_of(b), tile_of(b), normf[:, r:r + 1, :].broadcast_to([P, SUB, D]),
                                          op).then_inc(final_step, 1)
                    dve.wait_ge(final_step, 3 * b + 3)
                    dve.wait_ge(x_old_in, 16 * (b + 1))
                    dve.tensor_tensor(tile_of(b), tile_of(b), x_old[:, :, :], ALU.add).then_inc(final_done, 1)

                def step(a, j, batch, b, more):
                    if a is not None:
                        project(a)
                        if isinstance(a, int) and a == 0:
                            dve.wait_ge(w_lo_done, FFN_READY)
                        for bank in range(4):
                            decayed(a, 0, bank)
                        for c in range(SUB):
                            k = SUB * j + c
                            if k < UPDATES:
                                decay_keys(a, c, UPDATES * batch + k)
                            if c == 2 and b is not None:
                                scale(bT_done, norm2, b_full, b)
                            if c + 1 < SUB:
                                decayed(a, c + 1, 0)
                                decayed(a, c + 1, 1)
                            gate_result(a, c)
                            if c + 1 < SUB:
                                decayed(a, c + 1, 2)
                                decayed(a, c + 1, 3)
                            if k < UPDATES:
                                update_state(batch, k)
                            if c == 2 and more:
                                first_norms(a + 1)
                    elif b is not None:
                        scale(bT_done, norm2, b_full, b)
                    if b is not None:
                        for f in range(KF):
                            feed(b, f)
                            if f == 5 and more:
                                scale(aT_done, norm1, a_full, a + 1)
                    elif more:
                        scale(aT_done, norm1, a_full, a + 1)
                    if a is not None:
                        add_retention(a)
                    if b is not None:
                        add_feed(b)

                dve.wait_ge(const_in, consts_ready)
                first_norms(0)
                scale(aT_done, norm1, a_full, 0)
                for n, (hi, _, _) in enumerate(pieces):
                    dve.wait_ge(stage_in[n % 2], 16 * (n // 2 + 1))
                    dve.tensor_copy(hi, staged(n)).then_inc(w_hi_done, 1)
                steps(dve, step)

            @block.tensor
            def _(pe):
                pe.sem_inc(scores_done, CREDIT)
                pe.sem_inc(ret_done, CREDIT)
                pe.sem_inc(ffn2_done, CREDIT)

                def turn(ready, done, t):
                    pe.wait_ge(ready, t + 1)
                    for k in range(KD):
                        for s in range(SUB):
                            last = pe.transpose(t_ps[:, k, s * P:(s + 1) * P], xn[:, s, k * P:(k + 1) * P], ident[:, :])
                    last.then_inc(done, 1)

                def project(a):
                    pe.wait_ge(a_lo_done, a + 1)
                    pe.wait_ge(w_lo_done, PROJ_READY)
                    if not isinstance(a, int) or a > 0:
                        pe.wait_ge(reto_read, a)
                    for n, m in enumerate((0, 1, 2, 3, 6, 7)):
                        if n >= 4:
                            pe.wait_ge(q_done, KD * a + n - 3)
                        for k in range(KD):
                            w = slice(m * P, (m + 1) * P)
                            last = split3(pe, banks[:, n % 4, :], wp_hi[:, k, w], wp_lo[:, k, w], a_hi[:, k, :],
                                          a_lo[:, k, :], k == 0, k == KD - 1)
                        last.then_inc(proj_done, 1)
                    for s in range(SUB):
                        if s < 2:
                            pe.wait_ge(k_done, KD * a + s + 1)
                        else:
                            pe.wait_ge(v_done, SUB * a + s - 1)
                        for k in range(KD):
                            t, w = slice(s * P, (s + 1) * P), slice(2 * D, 3 * D)
                            last = split3(pe, banks[:, 2 + s % 2, 0:D], a_hi[:, k, t], a_lo[:, k, t], wp_hi[:, k, w],
                                          wp_lo[:, k, w], k == 0, k == KD - 1)
                        last.then_inc(proj_done, 1)

                def scores(a, c):
                    cc = SUB * a + c
                    for bank in range(4):
                        g = bank // 2
                        if bank % 2 == 0:
                            pe.wait_ge(wide_q_done, 2 * cc + g + 1)
                        if c == 0 and bank == 0:
                            pe.wait_ge(k_done, KD * (a + 1))
                        if c > 0:
                            pe.wait_ge(probs_done, 4 * (cc - 1) + bank + 1)
                        elif bank < 2:
                            pe.wait_ge(gate_done, KD * a + bank + 1)
                        else:
                            pe.wait_ge(v_done, SUB * a + bank + 1)
                        wide = q_wide[:, g, 4 * (bank % 2):4 * (bank % 2) + 4, :].rearrange("p h n -> p (h n)")
                        last = pe.matmul(banks[:, bank, :], kT[:, g, c * P:(c + 1) * P], wide, start=True, stop=True)
                        if bank % 2 == 1:
                            last.then_inc(scores_done, 1)

                def turn_keys(c, n):
                    if not isinstance(n, int) or n > 0:
                        pe.wait_ge(state_done, n)
                    for g in range(KD):
                        last = pe.transpose(m_ps[:, g * P:(g + 1) * P], kT[:, g, c * P:(c + 1) * P], ident[:, :])
                    last.then_inc(kturn_done, 1)

                def retain(a, c, k, n):
                    cc = SUB * a + c
                    if not isinstance(a, int) or cc > 0:
                        pe.wait_ge(gated_done, cc)
                    pe.wait_ge(wide_v_done, cc + 1)
                    if k > 0:
                        pe.wait_ge(qs_done, a + 1)
                        pe.wait_ge(state_done, n)
                    for g in range(KD):
                        out = ret_ps[:, g * P:(g + 1) * P]
                        if k > 0:
                            pe.matmul(out, state[:, g, :], qs[:, g, c * P:(c + 1) * P], start=True, stop=False)
                        for hh in range(HG):
                            if hh % 4 == 0:
                                pe.wait_ge(probs_done, 4 * cc + 2 * g + hh // 4 + 1)
                            head = g * HG + hh
                            last = pe.matmul(out, v_wide[:, g, hh * P:(hh + 1) * P], probs[:, head * P:(head + 1) * P],
                                             start=(k == 0 and hh == 0), stop=(hh == HG - 1))
                        last.then_inc(ret_done, 1)

                def outer(c, n):
                    pe.wait_ge(ks_done, n + 1)
                    for g in range(KD):
                        w = slice(g * P, (g + 1) * P)
                        last = pe.matmul(m_ps[:, D + g * P:D + (g + 1) * P], ks[:, w], v[:, c, w], start=True, stop=True)
                    last.then_inc(st_done, 1)

                def feed_in(b, f):
                    if f >= 2:
                        pe.wait_ge(f_hi_done, KF * b + f - 1)
                    for k in range(KD):
                        w = slice(f * P, (f + 1) * P)
                        last = split3(pe, banks[:, f % 2, :], w1_hi[:, k, w], w1_lo[:, k, w], b_hi[:, k, :], b_lo[:, k, :],
                                      k == 0, k == KD - 1)
                    last.then_inc(ffn1_done, 1)

                def feed_out(b, f):
                    pe.wait_ge(f_lo_done, KF * b + f + 1 + CREDIT)
                    for k in range(KD):
                        w = slice(k * P, (k + 1) * P)
                        last = split3(pe, banks[:, 2 + k, :], w2_hi[:, f, w], w2_lo[:, f, w], f_hi[:, f % 2, :],
                                      f_lo[:, f % 2, :], f == 0, f == KF - 1)
                    last.then_inc(ffn2_done, 1)

                def project_out(a):
                    pe.wait_ge(g_lo_done, a + 1)
                    pe.wait_ge(w_lo_done, RETO_READY)
                    for s in range(SUB):
                        t = slice(s * P, (s + 1) * P)
                        for k in range(KD):
                            last = split3(pe, token_ps[:, s, :], g_hi[:, k, t], g_lo[:, k, t], wr_hi[:, k, :],
                                          wr_lo[:, k, :], k == 0, k == KD - 1)
                    last.then_inc(reto_done, 1)

                def turn_back(a, b, more):
                    pe.wait_ge(oT_done, b + 1)
                    if more:
                        pe.wait_ge(a_lo_done, a + 2)
                    for s in range(SUB):
                        for k in range(KD):
                            last = pe.transpose(back_ps[:, s, k * P:(k + 1) * P], oT[:, k, s * P:(s + 1) * P], ident[:, :])
                    last.then_inc(back_done, 1)

                def turn_b(b):
                    pe.wait_ge(added, b + CREDIT)
                    turn(xn2_done, bT_done, b)

                def step(a, j, batch, b, more):
                    if a is not None:
                        project(a)
                        scores(a, 0)
                        for c in range(SUB):
                            k = SUB * j + c
                            n = UPDATES * batch + k
                            if c + 1 < SUB:
                                scores(a, c + 1)
                            if k < UPDATES:
                                turn_keys(c, n)
                            retain(a, c, k, n)
                            if k < UPDATES:
                                outer(c, n)
                            if c == 1 and b is not None:
                                turn_b(b)
                        pe.wait_ge(probs_done, 4 * SUB * (a + 1))
                    else:
                        turn_b(b)
                    if b is not None:
                        pe.wait_ge(b_lo_done, b + 1)
                        pe.wait_ge(w_lo_done, FFN_READY)
                        feed_in(b, 0)
                        feed_in(b, 1)
                        for f in range(KF):
                            feed_out(b, f)
                            if f + 2 < KF:
                                feed_in(b, f + 2)
                            if f == 4 and more:
                                turn(xn_done, aT_done, a + 1)
                    elif more:
                        turn(xn_done, aT_done, a + 1)
                    if a is not None:
                        project_out(a)
                    if b is not None:
                        turn_back(a, b, more)

                turn(xn_done, aT_done, 0)
                steps(pe, step)

        hand_back(nc, sems)


def macaron(nc, ins, out):
    with ExitStack() as ctx:
        x_sb = ctx.enter_context(nc.sbuf_tensor("x_sb", [P, TOK // P, D], F32))
        ident = ctx.enter_context(nc.sbuf_tensor("ident", [P, P], F32))
        iota16 = ctx.enter_context(nc.sbuf_tensor("iota16", [P, E], F32))
        eps = ctx.enter_context(nc.sbuf_tensor("eps", [P, 1], F32))
        const_in = ctx.enter_context(nc.semaphore("const_in"))
        eps_set = ctx.enter_context(nc.semaphore("eps_set"))
        x_dram = nc.dram_tensor("x_dram", (TOK, D), F32).ap()
        comb_dram = nc.dram_tensor("comb_dram", (2, E, TILE), F32).ap()

        with nc.Block() as block:
            @block.sync
            def _(sp):
                sp.dma_start(ident[:, :], ins["ident"]).then_inc(const_in, 16)
                sp.dma_start(iota16[:, :], ins["iota16"]).then_inc(const_in, 16)
                sp.wait_ge(const_in, 32)
                sp.wait_ge(eps_set, 1)

            @block.vector
            def _(dve):
                dve.memset(eps[:, :], EPS).then_inc(eps_set, 1)

        def ffn(tag, x_in, x_out):
            moe(nc, tag, x_sb, ident, iota16, eps, x_in, x_out, ins["router_w"], ins["router_b"], ins["gate_w"],
                ins["up_w"], ins["down_w"], ins["conv_w"], ins["shared_up"], ins["shared_down"], comb_dram)

        ffn("a", ins["x"], x_dram)
        for layer in range(NL):
            retention_layer(nc, layer, x_sb, ident, eps, ins, x_dram)
        ffn("b", None, out)


def kernel(**inputs):
    import concourse.bacc as bacc
    from concourse.bass_utils import run_bass_kernel_spmd

    a = {k: np.ascontiguousarray(v) for k, v in inputs.items()}
    arrays = {
        "x": a["L0_attn_x"].reshape(TOK, D),
        "router_w": a["L0_ffn_router_w"],
        "router_b": a["L0_ffn_router_bias"].reshape(E, 1),
        "gate_w": a["L0_ffn_expert_gate_w"],
        "up_w": a["L0_ffn_expert_up_w"],
        "down_w": a["L0_ffn_expert_down_w"],
        "conv_w": np.ascontiguousarray(a["L0_ffn_conv_w"].transpose(2, 1, 0)).reshape(TAPS * D, P),
        "shared_up": a["L0_ffn_shared_up_w"],
        "shared_down": a["L0_ffn_shared_down_w"],
    }
    for name in ("proj_w", "proj_b", "reto_w", "reto_b", "ffn1_w", "ffn2_w", "lnf_g", "lnf_b"):
        arrays[name] = a[f"L0_attn_{name}"]

    def by_partition(name):
        return np.ascontiguousarray(a[f"L0_attn_{name}"].reshape(NL, -1, P).transpose(0, 2, 1))

    for name in ("ln1_g", "ln1_b", "ln2_g", "ln2_b", "ffn1_b", "ffn2_b"):
        arrays[name] = by_partition(name)
    arrays["proj_b_cols"] = by_partition("proj_b")
    arrays.update(shape_constants())
    nc = bacc.Bacc("TRN2", target_bir_lowering=False, num_devices=1)
    ins = {k: nc.dram_tensor(f"in_{k}", v.shape, F32, kind="ExternalInput").ap() for k, v in arrays.items()}
    out = nc.dram_tensor("out_x", (TOK, D), F32, kind="ExternalOutput").ap()
    macaron(nc, ins, out)
    result = run_bass_kernel_spmd(nc, [{f"in_{k}": v for k, v in arrays.items()}], core_ids=[0])
    return result.results[0]["out_x"].reshape(B, S, D)


def shape_constants():
    gamma = 1.0 - 2.0 ** (-5.0 - np.arange(H, dtype=np.float64))
    n = np.arange(P)
    ahead = n[None, :] - n[:, None]
    decay = np.where(ahead[:, None, :] >= 0, gamma[None, :, None] ** np.maximum(ahead, 0)[:, None, :], 0.0)
    head = (np.arange(D) // HD).reshape(KD, P).T
    own = n // HD
    f32 = np.float32
    return {
        "decay": decay.reshape(P, H * P).astype(f32),
        "key_decay": (gamma[np.arange(D) // HD][None, :] ** (P - n)[:, None]).astype(f32),
        "query_decay": (gamma[head][:, :, None] ** n[None, None, :]).astype(f32),
        "state_decay": (gamma[head] ** P).astype(f32),
        "own_head": (own[:, None] == own[None, :]).astype(f32),
        "head_mask": (own[:, None] == np.arange(HG)[None, :]).astype(f32),
        "ident": np.eye(P, dtype=np.float32),
        "iota16": np.tile(np.arange(E, dtype=np.float32), (P, 1)),
    }
```

```python
from contextlib import ExitStack

import numpy as np

import concourse.bass as bass
from concourse import mybir

F32 = mybir.dt.float32
F32R = mybir.dt.float32r
U32 = mybir.dt.uint32
ALU = mybir.AluOpType
ACT = mybir.ActivationFunctionType
AX_X = mybir.AxisListType.X

P = 128
B, S, D = 4, 1024, 256
TOK = B * S
TILE = 512
SUB = TILE // P
NT = TOK // TILE
PAIRS = NT // 2
KD = D // P
E = 16
NE = E - 1
TAPS = 3
HALO = TAPS - 1
SHARED_COLS = (TAPS * KD + KD) * P + D
EXPERT_COLS = 2 * KD * P + D
CB_GROUP = 3
GROUPS = NE // CB_GROUP
EPS = 1e-5
CREDIT = 2
PREPARED = 4

NL = 2
H = 16
HD = D // H
F = 4 * D
KF = F // P
HG = P // HD


def split3(tensor, out, w_hi, w_lo, x_hi, x_lo, start, stop):
    tensor.matmul(out, w_hi, x_hi, start=start, stop=False)
    tensor.matmul(out, w_hi, x_lo, start=False, stop=False)
    return tensor.matmul(out, w_lo, x_hi, start=False, stop=stop)


def moe(nc, tag, x_sb, ident, iota16, eps, x_in, out, router_w, router_b, gate_w, up_w, down_w, conv_w,
        shared_up, shared_down, comb_dram):
    with ExitStack() as ctx:
        def sb(name, shape, dt=F32):
            return ctx.enter_context(nc.sbuf_tensor(f"{tag}_{name}", shape, dt))

        sems = []

        def sem(name):
            sems.append(nc.alloc_semaphore(f"{tag}_{name}"))
            return sems[-1]

        w_hi = sb("w_hi", [P, SHARED_COLS + NE * EXPERT_COLS], F32R)
        w_lo = sb("w_lo", [P, SHARED_COLS + NE * EXPERT_COLS], F32R)
        stage = sb("stage", [P, 2, EXPERT_COLS])
        rw_f = sb("rw_f", [P, KD, P])
        rw_hi = sb("rw_hi", [P, KD, P], F32R)
        rw_lo = sb("rw_lo", [P, KD, P], F32R)
        rb = sb("rb", [P, 1])
        xn = sb("xn", [P, 2, SUB, D])
        x_hi = sb("x_hi", [P, 2, KD, HALO + TILE], F32R)
        x_lo = sb("x_lo", [P, 2, KD, HALO + TILE], F32R)
        silu_g = sb("silu_g", [P, 2, TILE])
        weighted = sb("weighted", [P, 2, TILE])
        h = sb("h", [P, 2, TILE])
        h_hi = sb("h_hi", [P, 2, TILE], F32R)
        h_lo = sb("h_lo", [P, 2, TILE], F32R)
        cb = sb("cb", [P, 2, CB_GROUP * TILE])
        oT = sb("oT", [P, KD, TILE])
        stats = sb("stats", [P, SUB, 6])
        mv = sb("mv", [P, SUB, 2])
        std = sb("std", [P, SUB])
        rstd = sb("rstd", [P, SUB])
        lgT = sb("lgT", [P, TILE])
        carrier = sb("carrier", [P, 1])
        warm_out = sb("warm_out", [P, 1])
        lmax = sb("lmax", [P, SUB])
        shifted = sb("shifted", [P, SUB, E])
        ex = sb("ex", [P, SUB, E])
        probs = sb("probs", [P, SUB, E])
        top = sb("top", [P, SUB, 8])
        top_i = sb("top_i", [P, SUB, 8], U32)
        top_f = sb("top_f", [P, SUB, 2])
        sums = sb("sums", [P, SUB])
        norm_w = sb("norm_w", [P, SUB, 2])
        pick = sb("pick", [P, 2, SUB, E])
        comb = sb("comb", [P, 2, SUB, E])
        combT = lgT

        gate_ps = ctx.enter_context(nc.psum_tensor(f"{tag}_gate_ps", [P, 2, TILE], F32))
        up_ps = ctx.enter_context(nc.psum_tensor(f"{tag}_up_ps", [P, 2, TILE], F32))
        acc_ps = ctx.enter_context(nc.psum_tensor(f"{tag}_acc_ps", [P, KD, TILE], F32))
        t_ps = ctx.enter_context(nc.psum_tensor(f"{tag}_t_ps", [P, 2, TILE], F32))

        x0_in, x1_in, x_rest_in, group_used = sem("x0_in"), sem("x1_in"), sem("x_rest_in"), sem("group_used")
        stage_in = [sem(f"stage_in{i}") for i in range(2)]
        rw_in, rw_zero, rw_hi_done = sem("rw_in"), sem("rw_zero"), sem("rw_hi_done")
        w_hi_done, w_lo_done = sem("w_hi_done"), sem("w_lo_done")
        halo_zero = sem("halo_zero")
        stats_done, var_done, std_done, rstd_done = (
            sem("stats_done"), sem("var_done"), sem("std_done"), sem("rstd_done"))
        xn_done, xT_done, x_hi_done, x_lo_done, halo_done = (
            sem("xn_done"), sem("xT_done"), sem("x_hi_done"), sem("x_lo_done"), sem("halo_done"))
        logits_done, lgT_done, lg_done = sem("logits_done"), sem("lgT_done"), sem("lg_done")
        lmax_done, shifted_done, ex_done = sem("lmax_done"), sem("shifted_done"), sem("ex_done")
        soft_step = sem("soft_step")
        comb_done, combT_ps_done, combT_done = sem("comb_done"), sem("combT_ps_done"), sem("combT_done")
        comb_stored = sem("comb_stored")
        cb_in = [sem(f"cb_in{i}") for i in range(2)]
        gateup_done, silu_done, weighted_done, h_done, h_hi_done, h_lo_done, down_done = (
            sem("gateup_done"), sem("silu_done"), sem("weighted_done"), sem("h_done"),
            sem("h_hi_done"), sem("h_lo_done"), sem("down_done"))
        oT_done, back_done, mixed_done, x_done = (
            sem("oT_done"), sem("back_done"), sem("mixed_done"), sem("x_done"))
        stored = sem("stored")

        def wcol(u):
            return 0 if u == 0 else SHARED_COLS + (u - 1) * EXPERT_COLS

        def cols(u):
            return SHARED_COLS if u == 0 else EXPERT_COLS

        taps, pair = TAPS * KD * P, KD * P
        pieces = [(0, [(0, taps, conv_w)]), (taps, [(0, pair, shared_up), (pair, D, shared_down)])]
        pieces += [(wcol(e + 1), [(0, pair, gate_w[e]), (pair, pair, up_w[e]), (2 * pair, D, down_w[e])])
                   for e in range(NE)]

        def piece_cols(n):
            return sum(width for _, width, _ in pieces[n][1])

        def stage_count(n):
            return 16 * sum(len(pieces[m][1]) for m in range(n % 2, n + 1, 2))

        def tile_view(dram, t):
            return dram.rearrange("(t s p) d -> t p s d", s=SUB, p=P)[t]

        def steps(engine, tile):
            tile(0, 0, False)
            with engine.Fori(0, PAIRS - 1) as i:
                tile(i, 1, False)
                tile(i, 2, False)
            tile(0, NT - 1, True)

        with nc.Block() as block:

            @block.sync
            def _(sp):
                if x_in is not None:
                    sp.dma_start(x_sb[:, 0:SUB, :], tile_view(x_in, 0)).then_inc(x0_in, 16)
                sp.wait_ge(rw_zero, 2)
                sp.dma_start(rw_f[:, :, 0:E], router_w.rearrange("(k p) e -> p k e", p=P)).then_inc(rw_in, 16)
                sp.dma_start(rb[0:E, :], router_b).then_inc(rw_in, 16)

                def load_pieces(first, end):
                    for n in range(first, end):
                        if n >= 2:
                            sp.wait_ge(w_lo_done, n)
                        for at, width, src in pieces[n][1]:
                            dst = stage[:, n % 2, at:at + width]
                            if width > D or src.shape[0] > P:
                                dst = dst.rearrange("p (k i) -> p k i", i=P)
                                src = src.rearrange("(k p) i -> p k i", p=P)
                            sp.dma_start(dst, src).then_inc(stage_in[n % 2], 16)

                def store_comb(i, off):
                    t = 2 * i + off
                    sp.wait_ge(combT_done, t + 1)
                    sp.dma_start(comb_dram[off % 2], combT[0:E, :]).then_inc(comb_stored, 16)

                def load_cb(i, off, g):
                    s = GROUPS * off + g
                    if g == 0:
                        sp.wait_ge(comb_stored, 16 * (2 * i + off + 1))
                    else:
                        sp.wait_ge(group_used, 2 * GROUPS * i + s - 1 + CREDIT)
                    src = comb_dram[off % 2][g * CB_GROUP:(g + 1) * CB_GROUP, :].rearrange("e n -> (e n)")
                    sp.dma_start(cb[:, s % 2, :], src.partition_broadcast(P)).then_inc(cb_in[s % 2], 16)

                def tile(i, off, last):
                    t = 2 * i + off
                    begin = isinstance(i, int) and off == 0
                    for g, upto in ((2, 10), (3, 13), (4, 16)):
                        if begin:
                            load_pieces(upto - (4 if g == 2 else 3), upto)
                        load_cb(i, off, g)
                    if begin:
                        load_pieces(16, len(pieces))
                    if out is not None and not begin:
                        sp.wait_ge(x_done, t + CREDIT)
                        sp.dma_start(tile_view(out, t - 1), x_sb[:, bass.ds((t - 1) * SUB, SUB), :]).then_inc(stored, 16)
                    if not last:
                        store_comb(i, off + 1)
                        for g in range(2):
                            load_cb(i, off + 1, g)

                load_pieces(0, 6)
                store_comb(0, 0)
                for g in range(2):
                    load_cb(0, 0, g)
                steps(sp, tile)
                if out is not None:
                    sp.wait_ge(x_done, NT + CREDIT)
                    sp.dma_start(tile_view(out, NT - 1), x_sb[:, (NT - 1) * SUB:, :]).then_inc(stored, 16)
                    sp.wait_ge(stored, 16 * NT)

            @block.scalar
            def _(act):
                def load_x(t, done):
                    act.dma_start(x_sb[:, t * SUB:(t + 1) * SUB, :], tile_view(x_in, t)).then_inc(done, 16)

                if x_in is not None:
                    load_x(1, x1_in)
                act.sem_inc(h_hi_done, CREDIT)
                act.sem_inc(oT_done, CREDIT)
                act.sem_inc(silu_done, CREDIT)

                def warm(func):
                    nc.scalar.activation(warm_out[:, :], eps[:, :], func)

                def root(t):
                    act.wait_ge(var_done, t + 1)
                    nc.scalar.activation(std[:, :], mv[:, :, 1], ACT.Sqrt, bias=eps[:, :]).then_inc(std_done, 1)
                    warm(ACT.Silu)

                def evacuate_xT(t, j):
                    act.wait_ge(xT_done, t + 1)
                    nc.scalar.activation(x_hi[:, j, :, HALO:], t_ps[:, :, :], ACT.Copy).then_inc(x_hi_done, 1)

                def evacuate_logits(t):
                    act.wait_ge(logits_done, t + 1)
                    nc.scalar.activation(lgT[:, :], t_ps[:, 0, :], ACT.Identity, bias=rb[:, :]).then_inc(lgT_done, 1)

                def exponent(t):
                    act.wait_ge(shifted_done, t + 1)
                    nc.scalar.activation(ex[:, :, :], shifted[:, :, :], ACT.Exp).then_inc(ex_done, 1)
                    warm(ACT.Silu)

                def evacuate_comb(t):
                    act.wait_ge(combT_ps_done, t + 1)
                    if not isinstance(t, int) or t > 0:
                        act.wait_ge(comb_stored, 16 * t)
                        act.wait_ge(group_used, GROUPS * t - 1 + CREDIT)
                    nc.scalar.activation(combT[0:E, :], t_ps[0:E, 0, :], ACT.Copy).then_inc(combT_done, 1)

                def unit(t, u):
                    n, b = E * t + u, u % 2
                    act.wait_ge(gateup_done, n + 1)
                    act.wait_ge(h_done, n - 1 + CREDIT)
                    nc.scalar.activation(silu_g[:, b, :], gate_ps[:, b, :], ACT.Silu).then_inc(silu_done, 1)
                    act.wait_ge(h_done, n + 1 + CREDIT)
                    act.wait_ge(down_done, n - 1 + CREDIT)
                    nc.scalar.activation(h_hi[:, b, :], h[:, b, :], ACT.Copy).then_inc(h_hi_done, 1)

                def copy_sum(t):
                    act.wait_ge(down_done, E * t + CREDIT)
                    nc.scalar.activation(oT[:, :, :], acc_ps[:, :, :], ACT.Copy).then_inc(oT_done, 1)

                def tile(i, off, last):
                    t, j = 2 * i + off, off % 2
                    begin = isinstance(i, int) and off == 0
                    for u in range(E):
                        unit(t, u)
                        if u == 0 and not begin:
                            copy_sum(t)
                        if begin and u == 4 and x_in is not None:
                            for later in range(2, NT):
                                load_x(later, x_rest_in)
                        if not last:
                            if u == 2:
                                root(t + 1)
                            if u == 5:
                                evacuate_xT(t + 1, 1 - j)
                            if u == 7:
                                evacuate_logits(t + 1)
                            if u == 9:
                                exponent(t + 1)
                            if u == 13:
                                evacuate_comb(t + 1)

                root(0)
                evacuate_xT(0, 0)
                evacuate_logits(0)
                exponent(0)
                evacuate_comb(0)
                steps(act, tile)
                copy_sum(NT)

            @block.gpsimd
            def _(pool):
                pool.memset(rw_f[:, :, :], 0.0).then_inc(rw_zero, 1)
                pool.memset(rb[:, :], 0.0).then_inc(rw_zero, 1)
                pool.memset(x_hi[:, 0, :, 0:HALO].bitcast(F32), 0.0).then_inc(halo_zero, 1)
                pool.memset(x_lo[:, 0, :, 0:HALO].bitcast(F32), 0.0).then_inc(halo_zero, 1)
                pool.sem_inc(h_done, CREDIT)
                pool.wait_ge(rw_hi_done, 1)
                pool.tensor_tensor(rw_lo[:, :, :], rw_f[:, :, :], rw_hi[:, :, :].bitcast(F32), ALU.subtract).then_inc(w_lo_done, 1)

                def low_weights(n):
                    a, width = pieces[n][0], piece_cols(n)
                    pool.wait_ge(w_hi_done, n + 1)
                    pool.tensor_tensor(w_lo[:, a:a + width], stage[:, n % 2, 0:width],
                                       w_hi[:, a:a + width].bitcast(F32), ALU.subtract).then_inc(w_lo_done, 1)

                def unit(t, u):
                    n, b = E * t + u, u % 2
                    pool.wait_ge(silu_done, n + 1 + CREDIT)
                    pool.wait_ge(weighted_done, n + 1 + CREDIT)
                    pool.wait_ge(h_lo_done, n - 1 + CREDIT)
                    pool.tensor_tensor(h[:, b, :], silu_g[:, b, :], weighted[:, b, :], ALU.mult).then_inc(h_done, 1)

                def tile(i, off, last):
                    for u in range(E):
                        unit(2 * i + off, u)
                        if isinstance(i, int) and off == 0 and u + PREPARED < len(pieces):
                            low_weights(u + PREPARED)

                for n in range(PREPARED):
                    low_weights(n)
                steps(pool, tile)

            @block.vector
            def _(dve):
                dve.sem_inc(weighted_done, CREDIT)
                dve.sem_inc(h_lo_done, CREDIT)
                dve.sem_inc(group_used, CREDIT)
                dve.sem_inc(x_done, CREDIT)
                dve.wait_ge(rw_in, 32)
                dve.tensor_copy(rw_hi[:, :, :], rw_f[:, :, :]).then_inc(rw_hi_done, 1)

                def split_weights(n):
                    a, width = pieces[n][0], piece_cols(n)
                    dve.wait_ge(stage_in[n % 2], stage_count(n))
                    dve.tensor_copy(w_hi[:, a:a + width], stage[:, n % 2, 0:width]).then_inc(w_hi_done, 1)

                def statistics(t):
                    if x_in is not None:
                        if not isinstance(t, int) or t > 1:
                            dve.wait_ge(x_rest_in, 16 * (NT - 2))
                        else:
                            dve.wait_ge((x0_in, x1_in)[t], 16)
                    for s in range(SUB):
                        last = dve.bn_stats(stats[:, s, :], x_sb[:, t * SUB + s, :])
                    last.then_inc(stats_done, 1)
                    dve.wait_ge(stats_done, t + 1)
                    dve.memset(carrier[:, :], 0.0)
                    for s in range(SUB):
                        last = dve.bn_aggr(mv[:, s, :], stats[:, s, :])
                    last.then_inc(var_done, 1)

                def normalise(t, j):
                    dve.wait_ge(std_done, t + 1)
                    dve.reciprocal(rstd[:, :], std[:, :]).then_inc(rstd_done, 1)
                    dve.wait_ge(rstd_done, t + 1)
                    for s in range(SUB):
                        last = dve.tensor_scalar(xn[:, j, s, :], x_sb[:, t * SUB + s, :], mv[:, s, 0:1],
                                                 rstd[:, s:s + 1], ALU.subtract, ALU.mult)
                    last.then_inc(xn_done, 1)

                def low_parts(t, j):
                    if j == 1:
                        dve.wait_ge(x_lo_done, t)
                        dve.tensor_copy(x_lo[:, 1, :, 0:HALO], x_lo[:, 0, :, TILE:]).then_inc(halo_done, 1)
                        dve.tensor_copy(x_hi[:, 1, :, 0:HALO], x_hi[:, 0, :, TILE:]).then_inc(halo_done, 1)
                    dve.wait_ge(x_hi_done, t + 1)
                    dve.tensor_tensor(x_lo[:, j, :, HALO:], t_ps[:, :, :], x_hi[:, j, :, HALO:].bitcast(F32),
                                      ALU.subtract).then_inc(x_lo_done, 1)

                def take_maximum(t):
                    dve.wait_ge(lg_done, t + 1)
                    lg = t_ps[:, 1, :].rearrange("p (s e) -> p s e", e=P)[:, :, 0:E]
                    dve.reduce_max(lmax[:, :], lg, AX_X).then_inc(lmax_done, 1)
                    dve.wait_ge(lmax_done, t + 1)
                    dve.tensor_tensor(shifted[:, :, :], lg, lmax[:, :].unsqueeze(2).broadcast_to([P, SUB, E]),
                                      ALU.subtract).then_inc(shifted_done, 1)

                SOFT_STEPS = 10

                def choose(t, j):
                    step = [0]

                    def link(ins):
                        step[0] += 1
                        ins.then_inc(soft_step, 1)
                        dve.wait_ge(soft_step, t * SOFT_STEPS + step[0])

                    dve.wait_ge(ex_done, t + 1)
                    link(dve.reduce_sum(sums[:, :], ex[:, :, :], AX_X))
                    link(dve.reciprocal(sums[:, :], sums[:, :]))
                    link(dve.tensor_tensor(probs[:, :, :], ex[:, :, :], sums[:, :].unsqueeze(2).broadcast_to([P, SUB, E]), ALU.mult))
                    dve.memset(carrier[:, :], 0.0)
                    for s in range(SUB):
                        last = dve.max(top[:, s, :], probs[:, s, :])
                    link(last)
                    dve.memset(carrier[:, :], 0.0)
                    for s in range(SUB):
                        dve.max_index(top_i[:, s, :], top[:, s, :], probs[:, s, :])
                    link(dve.tensor_tensor(sums[:, :], top[:, :, 0], top[:, :, 1], ALU.add))
                    dve.tensor_copy(top_f[:, :, :], top_i[:, :, 0:2])
                    link(dve.tensor_scalar_add(sums[:, :], sums[:, :], 1e-6))
                    link(dve.reciprocal(sums[:, :], sums[:, :]))
                    link(dve.tensor_tensor(norm_w[:, :, :], top[:, :, 0:2], sums[:, :].unsqueeze(2).broadcast_to([P, SUB, 2]), ALU.mult))
                    for k in range(2):
                        last = dve.tensor_tensor(pick[:, k, :, :], iota16[:, :].unsqueeze(1).broadcast_to([P, SUB, E]),
                                                 top_f[:, :, k:k + 1].broadcast_to([P, SUB, E]), ALU.is_equal)
                    link(last)
                    for k in range(2):
                        last = dve.tensor_tensor(pick[:, k, :, :], pick[:, k, :, :],
                                                 norm_w[:, :, k:k + 1].broadcast_to([P, SUB, E]), ALU.mult)
                    link(last)
                    assert step[0] == SOFT_STEPS
                    dve.tensor_tensor(comb[:, j, :, :], pick[:, 0, :, :], pick[:, 1, :, :], ALU.add).then_inc(comb_done, 1)

                def weight_up(i, off, u):
                    t = 2 * i + off
                    n, b, e = E * t + u, u % 2, u - 1
                    dve.wait_ge(gateup_done, n + 1)
                    dve.wait_ge(h_done, n - 1 + CREDIT)
                    if u == 0:
                        dve.tensor_copy(weighted[:, b, :], up_ps[:, b, :]).then_inc(weighted_done, 1)
                        return
                    g, r = divmod(e, CB_GROUP)
                    s = GROUPS * off + g
                    if r == 0:
                        dve.wait_ge(cb_in[s % 2], 16 * (GROUPS * i + s // 2 + 1))
                    done = dve.tensor_tensor(weighted[:, b, :], up_ps[:, b, :], cb[:, s % 2, r * TILE:(r + 1) * TILE], ALU.mult)
                    done.then_inc(weighted_done, 1)
                    if r == CB_GROUP - 1:
                        dve.wait_ge(weighted_done, n + 1 + CREDIT)
                        dve.sem_inc(group_used, 1)

                def low_product(t, u):
                    n, b = E * t + u, u % 2
                    dve.wait_ge(h_hi_done, n + 1 + CREDIT)
                    dve.tensor_tensor(h_lo[:, b, :], h[:, b, :], h_hi[:, b, :].bitcast(F32), ALU.subtract).then_inc(h_lo_done, 1)

                def finish(t, j):
                    dve.wait_ge(back_done, t)
                    back = t_ps[:, :, :].rearrange("p a n -> p (a n)").rearrange("p (s d) -> p s d", d=D)
                    for s in range(SUB):
                        last = dve.scalar_tensor_tensor(xn[:, j, s, :], xn[:, j, s, :], comb[:, j, s, E - 1:E],
                                                        back[:, s, :], ALU.mult, ALU.add)
                    last.then_inc(mixed_done, 1)
                    dve.wait_ge(mixed_done, t)
                    for s in range(SUB):
                        row = (t - 1) * SUB + s
                        last = dve.scalar_tensor_tensor(x_sb[:, row, :], xn[:, j, s, :], 0.5, x_sb[:, row, :], ALU.mult, ALU.add)
                    last.then_inc(x_done, 1)

                def tile(i, off, last):
                    t, j = 2 * i + off, off % 2
                    begin = isinstance(i, int) and off == 0
                    for u in range(E):
                        weight_up(i, off, u)
                        if u > 0:
                            low_product(t, u - 1)
                        elif not begin:
                            low_product(t - 1, E - 1)
                        if begin and u + PREPARED < len(pieces):
                            split_weights(u + PREPARED)
                        if u == 2 and not begin:
                            finish(t, 1 - j)
                        if not last:
                            if u == 1:
                                statistics(t + 1)
                            if u == 3:
                                normalise(t + 1, 1 - j)
                            if u == 5:
                                low_parts(t + 1, 1 - j)
                            if u == 9:
                                take_maximum(t + 1)
                            if u == 10:
                                choose(t + 1, 1 - j)

                statistics(0)
                normalise(0, 0)
                split_weights(0)
                low_parts(0, 0)
                split_weights(1)
                take_maximum(0)
                split_weights(2)
                choose(0, 0)
                for n in range(3, PREPARED):
                    split_weights(n)
                steps(dve, tile)
                low_product(NT - 1, E - 1)
                finish(NT, 1)

            @block.tensor
            def _(pe):
                pe.sem_inc(down_done, CREDIT)

                def turn_x(t, j):
                    pe.wait_ge(xn_done, t + 1)
                    pe.wait_ge(x_done, t - 1 + CREDIT)
                    for k in range(KD):
                        for s in range(SUB):
                            last = pe.transpose(t_ps[:, k, s * P:(s + 1) * P], xn[:, j, s, k * P:(k + 1) * P], ident[:, :])
                    last.then_inc(xT_done, 1)

                def route(t, j):
                    pe.wait_ge(x_lo_done, t + 1)
                    pe.wait_ge(w_lo_done, 1)
                    for k in range(KD):
                        last = split3(pe, t_ps[:, 0, :], rw_hi[:, k, :], rw_lo[:, k, :], x_hi[:, j, k, HALO:],
                                      x_lo[:, j, k, HALO:], k == 0, k == KD - 1)
                    last.then_inc(logits_done, 1)

                def turn_logits(t):
                    pe.wait_ge(lgT_done, t + 1)
                    for s in range(SUB):
                        last = pe.transpose(t_ps[:, 1, s * P:(s + 1) * P], lgT[:, s * P:(s + 1) * P], ident[:, :])
                    last.then_inc(lg_done, 1)

                def turn_comb(t, j):
                    pe.wait_ge(comb_done, t + 1)
                    for s in range(SUB):
                        last = pe.transpose(t_ps[0:E, 0, s * P:(s + 1) * P], comb[:, j, s, :], ident[:, :])
                    last.then_inc(combT_ps_done, 1)

                def gateup(t, j, u):
                    n, b = E * t + u, u % 2
                    pe.wait_ge(w_lo_done, u + 3)
                    pe.wait_ge(silu_done, n - 1 + CREDIT)
                    pe.wait_ge(weighted_done, n - 1 + CREDIT)
                    a = wcol(u)
                    if u == 0:
                        if j == 1:
                            pe.wait_ge(halo_done, t + 1)
                        if j == 0:
                            pe.wait_ge(halo_zero, 2)
                        taps = TAPS
                    else:
                        taps = 1
                    for c in range(taps):
                        lead = c if u == 0 else HALO
                        for k in range(KD):
                            w = slice(a + (c * KD + k) * P, a + (c * KD + k + 1) * P)
                            split3(pe, gate_ps[:, b, :], w_hi[:, w], w_lo[:, w], x_hi[:, j, k, lead:lead + TILE],
                                   x_lo[:, j, k, lead:lead + TILE], c == 0 and k == 0, c == taps - 1 and k == KD - 1)
                    a += taps * KD * P
                    for k in range(KD):
                        w = slice(a + k * P, a + (k + 1) * P)
                        last = split3(pe, up_ps[:, b, :], w_hi[:, w], w_lo[:, w], x_hi[:, j, k, HALO:],
                                      x_lo[:, j, k, HALO:], k == 0, k == KD - 1)
                    last.then_inc(gateup_done, 1)

                def down(t, u):
                    n, b = E * t + u, u % 2
                    pe.wait_ge(h_lo_done, n + 1 + CREDIT)
                    if u == 0:
                        pe.wait_ge(oT_done, t + CREDIT)
                    a = wcol(u) + cols(u) - D
                    for k in range(KD):
                        w = slice(a + k * P, a + (k + 1) * P)
                        last = split3(pe, acc_ps[:, k, :], w_hi[:, w], w_lo[:, w], h_hi[:, b, :], h_lo[:, b, :],
                                      u == 0, u == E - 1)
                    last.then_inc(down_done, 1)

                def turn_back(t):
                    pe.wait_ge(oT_done, t + CREDIT)
                    if not isinstance(t, int) or t < NT:
                        pe.wait_ge(combT_done, t + 1)
                    back = t_ps[:, :, :].rearrange("p a n -> p (a n)")
                    for s in range(SUB):
                        for k in range(KD):
                            done = pe.transpose(back[:, s * D + k * P:s * D + (k + 1) * P], oT[:, k, s * P:(s + 1) * P], ident[:, :])
                    done.then_inc(back_done, 1)

                def tile(i, off, last):
                    t, j = 2 * i + off, off % 2
                    begin = isinstance(i, int) and off == 0
                    for u in range(E):
                        if u + 2 < E:
                            gateup(t, j, u + 2)
                        elif not last:
                            gateup(t + 1, 1 - j, u + 2 - E)
                        down(t, u)
                        if u == 0 and not begin:
                            turn_back(t)
                        if not last:
                            if u == 3:
                                turn_x(t + 1, 1 - j)
                            if u == 5:
                                route(t + 1, 1 - j)
                            if u == 7:
                                turn_logits(t + 1)
                            if u == 10:
                                turn_comb(t + 1, 1 - j)

                turn_x(0, 0)
                route(0, 0)
                turn_logits(0)
                turn_comb(0, 0)
                gateup(0, 0, 0)
                gateup(0, 0, 1)
                steps(pe, tile)
                turn_back(NT)

        hand_back(nc, sems)


def hand_back(nc, sems):
    nc.clear_and_free_semaphores(sems)
    nc.all_engine_barrier()


def retention_layer(nc, layer, h_sb, ident, eps, ins, x_dram):
    first, final = layer == 0, layer == NL - 1
    tag = f"l{layer}"
    with ExitStack() as ctx:
        def sb(name, shape, dt=F32):
            return ctx.enter_context(nc.sbuf_tensor(f"{tag}_{name}", shape, dt))

        sems = []

        def sem(name):
            sems.append(nc.alloc_semaphore(f"{tag}_{name}"))
            return sems[-1]

        def halves(name, shape):
            return sb(name + "_hi", shape, F32R), sb(name + "_lo", shape, F32R)

        wp_hi, wp_lo = halves("wp", [P, KD, 4 * D])
        wr_hi, wr_lo = halves("wr", [P, KD, D])
        w1_hi, w1_lo = halves("w1", [P, KD, F])
        w2_hi, w2_lo = halves("w2", [P, KF, D])
        decay = sb("decay", [P, H * P])
        key_decay = sb("key_decay", [P, D])
        query_decay = sb("query_decay", [P, KD, P])
        state_decay = sb("state_decay", [P, KD])
        own_head = sb("own_head", [P, P])
        head_mask = sb("head_mask", [P, HG])
        norm1 = sb("norm1", [P, 2, KD])
        norm2 = sb("norm2", [P, 2, KD])
        proj_b = sb("proj_b", [P, 8])
        ffn1_b = sb("ffn1_b", [P, KF])
        ffn2_b = sb("ffn2_b", [P, KD])
        v_b = sb("v_b", [P, D])
        reto_b = sb("reto_b", [P, D])
        if final:
            normf = sb("normf", [P, 2, D])
            x_old = sb("x_old", [P, SUB, D])
        carrier = sb("carrier", [P, 1])

        xn = sb("xn", [P, SUB, D])
        full = sb("full", [P, KD, TILE])
        a_hi, a_lo = halves("a", [P, KD, TILE])
        b_hi, b_lo = halves("b", [P, KD, TILE])
        q = sb("q", [P, KD, TILE])
        gated = q
        qs = sb("qs", [P, KD, TILE])
        kT = sb("kT", [P, KD, TILE])
        gate = sb("gate", [P, KD, TILE])
        v = sb("v", [P, SUB, D])
        q_wide = sb("q_wide", [P, KD, HG, P])
        v_wide = sb("v_wide", [P, KD, HG * (P + HD)])
        probs = sb("probs", [P, H * P])
        stage = probs[:, :].rearrange("p (b n) -> p b n", b=2)
        ks = sb("ks", [P, D])
        state = sb("state", [P, KD, P])
        fresh = sb("fresh", [P, KD, P])
        g_hi, g_lo = halves("g", [P, KD, TILE])
        act_f = sb("act_f", [P, 2, TILE])
        f_hi, f_lo = halves("f", [P, 2, TILE])
        oT = sb("oT", [P, KD, TILE])

        banks = ctx.enter_context(nc.psum_tensor(f"{tag}_banks", [P, 4, TILE], F32))
        t_ps = ctx.enter_context(nc.psum_tensor(f"{tag}_t_ps", [P, 2, TILE], F32))
        ret_ps = ctx.enter_context(nc.psum_tensor(f"{tag}_ret_ps", [P, TILE], F32))
        m_ps = ctx.enter_context(nc.psum_tensor(f"{tag}_m_ps", [P, TILE], F32))
        token_ps = banks[:, 0:2, :].rearrange("p a n -> p (a n)").rearrange("p (s d) -> p s d", d=D)
        back_ps = t_ps[:, :, :].rearrange("p a n -> p (a n)").rearrange("p (s d) -> p s d", d=D)

        const_in = sem("const_in")
        stage_in = [sem(f"stage_in{i}") for i in range(2)]
        w_hi_done, w_lo_done, wide_zero = sem("w_hi_done"), sem("w_lo_done"), sem("wide_zero")
        xn0_done, xn_done, xn2_done = sem("xn0_done"), sem("xn_done"), sem("xn2_done")
        aT_done, a_full, a_hi_done, a_lo_done = sem("aT_done"), sem("a_full"), sem("a_hi_done"), sem("a_lo_done")
        bT_done, b_full, b_hi_done, b_lo_done = sem("bT_done"), sem("b_full"), sem("b_hi_done"), sem("b_lo_done")
        proj_done, q_done, k_done, gate_done, v_done, qs_done = (
            sem("proj_done"), sem("q_done"), sem("k_done"), sem("gate_done"), sem("v_done"), sem("qs_done"))
        wide_q_done, wide_v_done = sem("wide_q_done"), sem("wide_v_done")
        scores_done, probs_done, kturn_done, ks_done = (
            sem("scores_done"), sem("probs_done"), sem("kturn_done"), sem("ks_done"))
        ret_done, gated_done, st_done, fresh_done, state_done = (
            sem("ret_done"), sem("gated_done"), sem("st_done"), sem("fresh_done"), sem("state_done"))
        g_hi_done, g_lo_done, reto_done, reto_read, reto_added = (
            sem("g_hi_done"), sem("g_lo_done"), sem("reto_done"), sem("reto_read"), sem("reto_added"))
        ffn1_done, act_done, f_hi_done, f_lo_done, ffn2_done = (
            sem("ffn1_done"), sem("act_done"), sem("f_hi_done"), sem("f_lo_done"), sem("ffn2_done"))
        oT_done, back_done, added = sem("oT_done"), sem("back_done"), sem("added")
        x_old_in, final_step, final_done = sem("x_old_in"), sem("final_step"), sem("final_done")
        norms = {}
        for kind in ("0", "1", "2", "f"):
            norms[kind] = (sb(f"stats{kind}", [P, SUB, 6]), sb(f"mv{kind}", [P, SUB, 2]), sb(f"std{kind}", [P, SUB]),
                           sb(f"rstd{kind}", [P, SUB]), sem(f"stats{kind}_done"), sem(f"var{kind}_done"),
                           sem(f"std{kind}_done"), sem(f"rstd{kind}_done"))

        def rows(w, k, n=1):
            return w[k * P:(k + n) * P, :].rearrange("(k p) i -> p k i", p=P)

        proj_w, reto_w, ffn1_w, ffn2_w = (ins[n][layer] for n in ("proj_w", "reto_w", "ffn1_w", "ffn2_w"))
        half = KF // 2
        pieces = [(wp_hi[:, k:k + 1, :], wp_lo[:, k:k + 1, :], rows(proj_w, k)) for k in range(KD)]
        pieces += [(wr_hi[:, :, :], wr_lo[:, :, :], rows(reto_w, 0, KD))]
        pieces += [(w1_hi[:, k:k + 1, :], w1_lo[:, k:k + 1, :], rows(ffn1_w, k)) for k in range(KD)]
        pieces += [(w2_hi[:, k:k + half, :], w2_lo[:, k:k + half, :], rows(ffn2_w, k, half)) for k in (0, half)]
        PROJ_READY, RETO_READY, FFN_READY = KD, KD + 1, len(pieces)

        def staged(n):
            blocks, width = pieces[n][2].shape[1:]
            return stage[:, n % 2, 0:blocks * width].rearrange("p (k i) -> p k i", k=blocks)

        consts = [(decay[:, :], ins["decay"]), (key_decay[:, :], ins["key_decay"]),
                  (query_decay[:, :, :], ins["query_decay"]), (state_decay[:, :], ins["state_decay"]),
                  (own_head[:, :], ins["own_head"]), (head_mask[:, :], ins["head_mask"]),
                  (norm1[:, 0, :], ins["ln1_g"][layer]), (norm1[:, 1, :], ins["ln1_b"][layer]),
                  (norm2[:, 0, :], ins["ln2_g"][layer]), (norm2[:, 1, :], ins["ln2_b"][layer]),
                  (proj_b[:, :], ins["proj_b_cols"][layer]), (ffn1_b[:, :], ins["ffn1_b"][layer]),
                  (ffn2_b[:, :], ins["ffn2_b"][layer]),
                  (v_b[:, :], ins["proj_b"][layer, 2 * D:3 * D].partition_broadcast(P)),
                  (reto_b[:, :], ins["reto_b"][layer].partition_broadcast(P))]
        if final:
            consts += [(normf[:, 0, :], ins["lnf_g"].partition_broadcast(P)),
                       (normf[:, 1, :], ins["lnf_b"].partition_broadcast(P))]
        consts_ready = 16 * len(consts)
        UPDATES = 2 * SUB - 1

        def steps(engine, step):
            step(0, 0, 0, None, True)
            with engine.Fori(0, PAIRS - 1) as i:
                step(2 * i + 1, 1, i, 2 * i, True)
                step(2 * i + 2, 0, i + 1, 2 * i + 1, True)
            step(NT - 1, 1, PAIRS - 1, NT - 2, False)
            step(None, None, None, NT - 1, False)

        with nc.Block() as block:

            @block.sync
            def _(sp):
                for n, (_, _, src) in enumerate(pieces):
                    if n >= 2:
                        sp.wait_ge(w_lo_done, n - 1)
                    sp.dma_start(staged(n), src).then_inc(stage_in[n % 2], 16)
                if final:
                    view = x_dram.rearrange("(t s p) d -> t p s d", s=SUB, p=P)
                    sp.dma_start(x_old[:, :, :], view[0]).then_inc(x_old_in, 16)
                    with sp.Fori(1, NT) as t:
                        sp.wait_ge(final_done, t)
                        sp.dma_start(x_old[:, :, :], view[t]).then_inc(x_old_in, 16)

            @block.scalar
            def _(act):
                for dst, src in consts:
                    act.dma_start(dst, src).then_inc(const_in, 16)

                def root(kind, t):
                    _, mv, std, _, _, var_done, std_done, _ = norms[kind]
                    act.wait_ge(var_done, t + 1)
                    nc.scalar.activation(std[:, :], mv[:, :, 1], ACT.Sqrt, bias=eps[:, :]).then_inc(std_done, 1)

                def high(full_sem, hi, done, t):
                    act.wait_ge(full_sem, t + 1)
                    nc.scalar.activation(hi[:, :, :], full[:, :, :], ACT.Copy).then_inc(done, 1)

                def first_norms(t):
                    if first:
                        root("0", t)
                    root("1", t)

                def project(a):
                    for g in range(KD):
                        act.wait_ge(proj_done, 10 * a + g + 1)
                        nc.scalar.activation(q[:, g, :], banks[:, g, :], ACT.Identity, bias=proj_b[:, g:g + 1]).then_inc(q_done, 1)
                    for g in range(KD):
                        act.wait_ge(proj_done, 10 * a + g + 3)
                        nc.scalar.activation(kT[:, g, :], banks[:, 2 + g, :], ACT.Identity, bias=proj_b[:, 2 + g:3 + g]).then_inc(k_done, 1)
                    for g in range(KD):
                        act.wait_ge(proj_done, 10 * a + g + 5)
                        nc.scalar.activation(gate[:, g, :], banks[:, g, :], ACT.Silu, bias=proj_b[:, 6 + g:7 + g]).then_inc(gate_done, 1)

                def widen_values(a, c):
                    cc = SUB * a + c
                    act.wait_ge(v_done, cc + 1)
                    act.wait_ge(ret_done, 2 * cc + CREDIT)
                    blocks = v_wide[:, :, :].rearrange("p g (h x) -> p g h x", h=HG)
                    for g in range(KD):
                        last = nc.scalar.activation(blocks[:, g, :, 0:HD], v[:, c, g * P:(g + 1) * P].rearrange("p (h x) -> p h x", h=HG), ACT.Copy)
                    last.then_inc(wide_v_done, 1)

                def feed(b, f):
                    n, slot = KF * b + f, f % 2
                    act.wait_ge(ffn1_done, n + 1)
                    act.wait_ge(f_lo_done, n - 1 + CREDIT)
                    nc.scalar.activation(act_f[:, slot, :], banks[:, slot, :], ACT.Gelu, bias=ffn1_b[:, f:f + 1]).then_inc(act_done, 1)
                    act.wait_ge(ffn2_done, n - 1 + CREDIT)
                    nc.scalar.activation(f_hi[:, slot, :], banks[:, slot, :], ACT.Gelu, bias=ffn1_b[:, f:f + 1]).then_inc(f_hi_done, 1)

                def step(a, j, batch, b, more):
                    if a is not None:
                        project(a)
                        widen_values(a, 0)
                        widen_values(a, 1)
                        widen_values(a, 2)
                    if b is not None:
                        high(b_full, b_hi, b_hi_done, b)
                    if a is not None:
                        widen_values(a, 3)
                        if more:
                            first_norms(a + 1)
                        act.wait_ge(gated_done, SUB * (a + 1))
                        nc.scalar.activation(g_hi[:, :, :], gated[:, :, :], ACT.Copy).then_inc(g_hi_done, 1)
                    if b is not None:
                        for f in range(KF):
                            feed(b, f)
                            if f == 5 and more:
                                high(a_full, a_hi, a_hi_done, a + 1)
                        act.wait_ge(ffn2_done, KF * (b + 1) + CREDIT)
                        for k in range(KD):
                            last = nc.scalar.activation(oT[:, k, :], banks[:, 2 + k, :], ACT.Identity, bias=ffn2_b[:, k:k + 1])
                        last.then_inc(oT_done, 1)
                    elif more:
                        high(a_full, a_hi, a_hi_done, a + 1)
                    if a is not None:
                        root("2", a)
                    if b is not None and final:
                        root("f", b)

                act.wait_ge(const_in, consts_ready)
                act.wait_ge(wide_zero, 1)
                first_norms(0)
                high(a_full, a_hi, a_hi_done, 0)
                steps(act, step)

            @block.gpsimd
            def _(pool):
                pool.memset(v_wide[:, :, :], 0.0).then_inc(wide_zero, 1)

                def widen_queries(a, c):
                    cc = SUB * a + c
                    for g in range(KD):
                        if g == 0:
                            pool.wait_ge(q_done, KD * (a + 1))
                        pool.wait_ge(scores_done, 2 * cc - 1 + g + CREDIT)
                        pool.tensor_tensor(q_wide[:, g, :, :],
                                           q[:, g, c * P:(c + 1) * P].unsqueeze(1).broadcast_to([P, HG, P]),
                                           head_mask[:, :].unsqueeze(2).broadcast_to([P, HG, P]), ALU.mult).then_inc(wide_q_done, 1)

                def low(hi_sem, source, hi, lo, done, t):
                    pool.wait_ge(hi_sem, t + 1)
                    pool.tensor_tensor(lo[:, :, :], source[:, :, :], hi[:, :, :].bitcast(F32), ALU.subtract).then_inc(done, 1)

                def step(a, j, batch, b, more):
                    if a is not None:
                        for c in range(SUB):
                            widen_queries(a, c)
                    if b is not None:
                        low(b_hi_done, full, b_hi, b_lo, b_lo_done, b)
                    if a is not None:
                        low(g_hi_done, gated, g_hi, g_lo, g_lo_done, a)
                        if more:
                            low(a_hi_done, full, a_hi, a_lo, a_lo_done, a + 1)

                for n, (hi, lo, _) in enumerate(pieces):
                    pool.wait_ge(w_hi_done, n + 1)
                    pool.tensor_tensor(lo, staged(n), hi.bitcast(F32), ALU.subtract).then_inc(w_lo_done, 1)
                    if n == KD - 1:
                        low(a_hi_done, full, a_hi, a_lo, a_lo_done, 0)
                pool.wait_ge(const_in, consts_ready)
                pool.wait_ge(wide_zero, 1)
                steps(pool, step)

            @block.vector
            def _(dve):
                dve.sem_inc(f_lo_done, CREDIT)
                dve.sem_inc(added, CREDIT)

                def tile_of(t, s=None):
                    if s is None:
                        return h_sb[:, bass.ds(t * SUB, SUB), :]
                    return h_sb[:, t * SUB + s, :]

                def normalise(kind, t, dst):
                    stats, mv, std, rstd, stats_done, var_done, std_done, rstd_done = norms[kind]
                    dve.memset(carrier[:, :], 0.0)
                    for s in range(SUB):
                        last = dve.bn_stats(stats[:, s, :], tile_of(t, s))
                    last.then_inc(stats_done, 1)
                    dve.wait_ge(stats_done, t + 1)
                    dve.memset(carrier[:, :], 0.0)
                    for s in range(SUB):
                        last = dve.bn_aggr(mv[:, s, :], stats[:, s, :])
                    last.then_inc(var_done, 1)
                    dve.wait_ge(std_done, t + 1)
                    dve.reciprocal(rstd[:, :], std[:, :]).then_inc(rstd_done, 1)
                    dve.wait_ge(rstd_done, t + 1)
                    for s in range(SUB):
                        last = dve.tensor_scalar(dst(s), tile_of(t, s), mv[:, s, 0:1], rstd[:, s:s + 1],
                                                 ALU.subtract, ALU.mult)
                    return last

                def first_norms(t):
                    if first:
                        normalise("0", t, lambda s: tile_of(t, s)).then_inc(xn0_done, 1)
                        dve.wait_ge(xn0_done, t + 1)
                    normalise("1", t, lambda s: xn[:, s, :]).then_inc(xn_done, 1)

                def scale(turned, norm, done, t):
                    dve.wait_ge(turned, t + 1)
                    for k in range(KD):
                        last = dve.tensor_scalar(full[:, k, :], t_ps[:, k, :], norm[:, 0, k:k + 1], norm[:, 1, k:k + 1],
                                                 ALU.mult, ALU.add)
                    last.then_inc(done, 1)

                def project(a):
                    dve.wait_ge(q_done, KD * (a + 1))
                    for g in range(KD):
                        last = dve.tensor_tensor(qs[:, g, :].rearrange("p (c n) -> p c n", n=P),
                                                 q[:, g, :].rearrange("p (c n) -> p c n", n=P),
                                                 query_decay[:, g:g + 1, :].broadcast_to([P, SUB, P]), ALU.mult)
                    last.then_inc(qs_done, 1)
                    for s in range(SUB):
                        dve.wait_ge(proj_done, 10 * a + 7 + s)
                        dve.tensor_tensor(v[:, s, :], banks[:, 2 + s % 2, 0:D], v_b[:, :], ALU.add).then_inc(v_done, 1)

                def decayed(a, c, j):
                    cc, w = SUB * a + c, 4 * P
                    dve.wait_ge(scores_done, 2 * cc + j // 2 + 1 + CREDIT)
                    dve.wait_ge(ret_done, 2 * cc - 1 + j // 2 + CREDIT)
                    dve.tensor_tensor(probs[:, j * w:(j + 1) * w], banks[:, j, :], decay[:, j * w:(j + 1) * w],
                                      ALU.mult).then_inc(probs_done, 1)

                def decay_keys(a, c, n):
                    dve.wait_ge(kturn_done, n + 1)
                    dve.tensor_tensor(ks[:, :], m_ps[:, 0:D], key_decay[:, :], ALU.mult).then_inc(ks_done, 1)

                def gate_result(a, c):
                    cc = SUB * a + c
                    dve.wait_ge(ret_done, 2 * (cc + 1) + CREDIT)
                    part = slice(c * P, (c + 1) * P)
                    dve.tensor_tensor(gated[:, :, part], ret_ps[:, 0:KD * P].rearrange("p (g n) -> p g n", g=KD),
                                      gate[:, :, part], ALU.mult).then_inc(gated_done, 1)

                def update_state(batch, k):
                    dve.wait_ge(st_done, UPDATES * batch + k + 1)
                    part = m_ps[:, D:2 * D].rearrange("p (g n) -> p g n", g=KD)
                    mask = own_head[:, :].unsqueeze(1).broadcast_to([P, KD, P])
                    if k == 0:
                        dve.tensor_tensor(state[:, :, :], part, mask, ALU.mult).then_inc(state_done, 1)
                        return
                    dve.tensor_tensor(fresh[:, :, :], part, mask, ALU.mult).then_inc(fresh_done, 1)
                    dve.wait_ge(fresh_done, (UPDATES - 1) * batch + k)
                    for g in range(KD):
                        last = dve.scalar_tensor_tensor(state[:, g, :], state[:, g, :], state_decay[:, g:g + 1],
                                                        fresh[:, g, :], ALU.mult, ALU.add)
                    last.then_inc(state_done, 1)

                def feed(b, f):
                    dve.wait_ge(f_hi_done, KF * b + f + 1)
                    dve.tensor_tensor(f_lo[:, f % 2, :], act_f[:, f % 2, :], f_hi[:, f % 2, :].bitcast(F32),
                                      ALU.subtract).then_inc(f_lo_done, 1)

                def add_retention(a):
                    dve.wait_ge(reto_done, a + 1)
                    dve.tensor_tensor(tile_of(a), tile_of(a), token_ps, ALU.add).then_inc(reto_read, 1)
                    dve.wait_ge(reto_read, a + 1)
                    dve.tensor_tensor(tile_of(a), tile_of(a), reto_b[:, :].unsqueeze(1).broadcast_to([P, SUB, D]),
                                      ALU.add).then_inc(reto_added, 1)
                    dve.wait_ge(reto_added, a + 1)
                    normalise("2", a, lambda s: xn[:, s, :]).then_inc(xn2_done, 1)

                def add_feed(b):
                    dve.wait_ge(back_done, b + 1)
                    dve.tensor_tensor(tile_of(b), tile_of(b), back_ps, ALU.add).then_inc(added, 1)
                    if not final:
                        return
                    dve.wait_ge(added, b + 1 + CREDIT)
                    normalise("f", b, lambda s: tile_of(b, s)).then_inc(final_step, 1)
                    for r, op in ((0, ALU.mult), (1, ALU.add)):
                        dve.wait_ge(final_step, 3 * b + r + 1)
                        dve.tensor_tensor(tile_of(b), tile_of(b), normf[:, r:r + 1, :].broadcast_to([P, SUB, D]),
                                          op).then_inc(final_step, 1)
                    dve.wait_ge(final_step, 3 * b + 3)
                    dve.wait_ge(x_old_in, 16 * (b + 1))
                    dve.tensor_tensor(tile_of(b), tile_of(b), x_old[:, :, :], ALU.add).then_inc(final_done, 1)

                def step(a, j, batch, b, more):
                    if a is not None:
                        project(a)
                        if isinstance(a, int) and a == 0:
                            dve.wait_ge(w_lo_done, FFN_READY)
                        for bank in range(4):
                            decayed(a, 0, bank)
                        for c in range(SUB):
                            k = SUB * j + c
                            if k < UPDATES:
                                decay_keys(a, c, UPDATES * batch + k)
                            if c == 2 and b is not None:
                                scale(bT_done, norm2, b_full, b)
                            if c + 1 < SUB:
                                decayed(a, c + 1, 0)
                                decayed(a, c + 1, 1)
                            gate_result(a, c)
                            if c + 1 < SUB:
                                decayed(a, c + 1, 2)
                                decayed(a, c + 1, 3)
                            if k < UPDATES:
                                update_state(batch, k)
                            if c == 2 and more:
                                first_norms(a + 1)
                    elif b is not None:
                        scale(bT_done, norm2, b_full, b)
                    if b is not None:
                        for f in range(KF):
                            feed(b, f)
                            if f == 5 and more:
                                scale(aT_done, norm1, a_full, a + 1)
                    elif more:
                        scale(aT_done, norm1, a_full, a + 1)
                    if a is not None:
                        add_retention(a)
                    if b is not None:
                        add_feed(b)

                dve.wait_ge(const_in, consts_ready)
                first_norms(0)
                scale(aT_done, norm1, a_full, 0)
                for n, (hi, _, _) in enumerate(pieces):
                    dve.wait_ge(stage_in[n % 2], 16 * (n // 2 + 1))
                    dve.tensor_copy(hi, staged(n)).then_inc(w_hi_done, 1)
                steps(dve, step)

            @block.tensor
            def _(pe):
                pe.sem_inc(scores_done, CREDIT)
                pe.sem_inc(ret_done, CREDIT)
                pe.sem_inc(ffn2_done, CREDIT)

                def turn(ready, done, t):
                    pe.wait_ge(ready, t + 1)
                    for k in range(KD):
                        for s in range(SUB):
                            last = pe.transpose(t_ps[:, k, s * P:(s + 1) * P], xn[:, s, k * P:(k + 1) * P], ident[:, :])
                    last.then_inc(done, 1)

                def project(a):
                    pe.wait_ge(a_lo_done, a + 1)
                    pe.wait_ge(w_lo_done, PROJ_READY)
                    if not isinstance(a, int) or a > 0:
                        pe.wait_ge(reto_read, a)
                    for n, m in enumerate((0, 1, 2, 3, 6, 7)):
                        if n >= 4:
                            pe.wait_ge(q_done, KD * a + n - 3)
                        for k in range(KD):
                            w = slice(m * P, (m + 1) * P)
                            last = split3(pe, banks[:, n % 4, :], wp_hi[:, k, w], wp_lo[:, k, w], a_hi[:, k, :],
                                          a_lo[:, k, :], k == 0, k == KD - 1)
                        last.then_inc(proj_done, 1)
                    for s in range(SUB):
                        if s < 2:
                            pe.wait_ge(k_done, KD * a + s + 1)
                        else:
                            pe.wait_ge(v_done, SUB * a + s - 1)
                        for k in range(KD):
                            t, w = slice(s * P, (s + 1) * P), slice(2 * D, 3 * D)
                            last = split3(pe, banks[:, 2 + s % 2, 0:D], a_hi[:, k, t], a_lo[:, k, t], wp_hi[:, k, w],
                                          wp_lo[:, k, w], k == 0, k == KD - 1)
                        last.then_inc(proj_done, 1)

                def scores(a, c):
                    cc = SUB * a + c
                    for bank in range(4):
                        g = bank // 2
                        if bank % 2 == 0:
                            pe.wait_ge(wide_q_done, 2 * cc + g + 1)
                        if c == 0 and bank == 0:
                            pe.wait_ge(k_done, KD * (a + 1))
                        if c > 0:
                            pe.wait_ge(probs_done, 4 * (cc - 1) + bank + 1)
                        elif bank < 2:
                            pe.wait_ge(gate_done, KD * a + bank + 1)
                        else:
                            pe.wait_ge(v_done, SUB * a + bank + 1)
                        wide = q_wide[:, g, 4 * (bank % 2):4 * (bank % 2) + 4, :].rearrange("p h n -> p (h n)")
                        last = pe.matmul(banks[:, bank, :], kT[:, g, c * P:(c + 1) * P], wide, start=True, stop=True)
                        if bank % 2 == 1:
                            last.then_inc(scores_done, 1)

                def turn_keys(c, n):
                    if not isinstance(n, int) or n > 0:
                        pe.wait_ge(state_done, n)
                    for g in range(KD):
                        last = pe.transpose(m_ps[:, g * P:(g + 1) * P], kT[:, g, c * P:(c + 1) * P], ident[:, :])
                    last.then_inc(kturn_done, 1)

                def retain(a, c, k, n):
                    cc = SUB * a + c
                    if not isinstance(a, int) or cc > 0:
                        pe.wait_ge(gated_done, cc)
                    pe.wait_ge(wide_v_done, cc + 1)
                    if k > 0:
                        pe.wait_ge(qs_done, a + 1)
                        pe.wait_ge(state_done, n)
                    for g in range(KD):
                        out = ret_ps[:, g * P:(g + 1) * P]
                        if k > 0:
                            pe.matmul(out, state[:, g, :], qs[:, g, c * P:(c + 1) * P], start=True, stop=False)
                        for hh in range(HG):
                            if hh % 4 == 0:
                                pe.wait_ge(probs_done, 4 * cc + 2 * g + hh // 4 + 1)
                            head = g * HG + hh
                            last = pe.matmul(out, v_wide[:, g, hh * P:(hh + 1) * P], probs[:, head * P:(head + 1) * P],
                                             start=(k == 0 and hh == 0), stop=(hh == HG - 1))
                        last.then_inc(ret_done, 1)

                def outer(c, n):
                    pe.wait_ge(ks_done, n + 1)
                    for g in range(KD):
                        w = slice(g * P, (g + 1) * P)
                        last = pe.matmul(m_ps[:, D + g * P:D + (g + 1) * P], ks[:, w], v[:, c, w], start=True, stop=True)
                    last.then_inc(st_done, 1)

                def feed_in(b, f):
                    if f >= 2:
                        pe.wait_ge(f_hi_done, KF * b + f - 1)
                    for k in range(KD):
                        w = slice(f * P, (f + 1) * P)
                        last = split3(pe, banks[:, f % 2, :], w1_hi[:, k, w], w1_lo[:, k, w], b_hi[:, k, :], b_lo[:, k, :],
                                      k == 0, k == KD - 1)
                    last.then_inc(ffn1_done, 1)

                def feed_out(b, f):
                    pe.wait_ge(f_lo_done, KF * b + f + 1 + CREDIT)
                    for k in range(KD):
                        w = slice(k * P, (k + 1) * P)
                        last = split3(pe, banks[:, 2 + k, :], w2_hi[:, f, w], w2_lo[:, f, w], f_hi[:, f % 2, :],
                                      f_lo[:, f % 2, :], f == 0, f == KF - 1)
                    last.then_inc(ffn2_done, 1)

                def project_out(a):
                    pe.wait_ge(g_lo_done, a + 1)
                    pe.wait_ge(w_lo_done, RETO_READY)
                    for s in range(SUB):
                        t = slice(s * P, (s + 1) * P)
                        for k in range(KD):
                            last = split3(pe, token_ps[:, s, :], g_hi[:, k, t], g_lo[:, k, t], wr_hi[:, k, :],
                                          wr_lo[:, k, :], k == 0, k == KD - 1)
                    last.then_inc(reto_done, 1)

                def turn_back(a, b, more):
                    pe.wait_ge(oT_done, b + 1)
                    if more:
                        pe.wait_ge(a_lo_done, a + 2)
                    for s in range(SUB):
                        for k in range(KD):
                            last = pe.transpose(back_ps[:, s, k * P:(k + 1) * P], oT[:, k, s * P:(s + 1) * P], ident[:, :])
                    last.then_inc(back_done, 1)

                def turn_b(b):
                    pe.wait_ge(added, b + CREDIT)
                    turn(xn2_done, bT_done, b)

                def step(a, j, batch, b, more):
                    if a is not None:
                        project(a)
                        scores(a, 0)
                        for c in range(SUB):
                            k = SUB * j + c
                            n = UPDATES * batch + k
                            if c + 1 < SUB:
                                scores(a, c + 1)
                            if k < UPDATES:
                                turn_keys(c, n)
                            retain(a, c, k, n)
                            if k < UPDATES:
                                outer(c, n)
                            if c == 1 and b is not None:
                                turn_b(b)
                        pe.wait_ge(probs_done, 4 * SUB * (a + 1))
                    else:
                        turn_b(b)
                    if b is not None:
                        pe.wait_ge(b_lo_done, b + 1)
                        pe.wait_ge(w_lo_done, FFN_READY)
                        feed_in(b, 0)
                        feed_in(b, 1)
                        for f in range(KF):
                            feed_out(b, f)
                            if f + 2 < KF:
                                feed_in(b, f + 2)
                            if f == 4 and more:
                                turn(xn_done, aT_done, a + 1)
                    elif more:
                        turn(xn_done, aT_done, a + 1)
                    if a is not None:
                        project_out(a)
                    if b is not None:
                        turn_back(a, b, more)

                turn(xn_done, aT_done, 0)
                steps(pe, step)

        hand_back(nc, sems)


def macaron(nc, ins, out):
    with ExitStack() as ctx:
        x_sb = ctx.enter_context(nc.sbuf_tensor("x_sb", [P, TOK // P, D], F32))
        ident = ctx.enter_context(nc.sbuf_tensor("ident", [P, P], F32))
        iota16 = ctx.enter_context(nc.sbuf_tensor("iota16", [P, E], F32))
        eps = ctx.enter_context(nc.sbuf_tensor("eps", [P, 1], F32))
        const_in = ctx.enter_context(nc.semaphore("const_in"))
        eps_set = ctx.enter_context(nc.semaphore("eps_set"))
        x_dram = nc.dram_tensor("x_dram", (TOK, D), F32).ap()
        comb_dram = nc.dram_tensor("comb_dram", (2, E, TILE), F32).ap()

        with nc.Block() as block:
            @block.sync
            def _(sp):
                sp.dma_start(ident[:, :], ins["ident"]).then_inc(const_in, 16)
                sp.dma_start(iota16[:, :], ins["iota16"]).then_inc(const_in, 16)
                sp.wait_ge(const_in, 32)
                sp.wait_ge(eps_set, 1)

            @block.vector
            def _(dve):
                dve.memset(eps[:, :], EPS).then_inc(eps_set, 1)

        def ffn(tag, x_in, x_out):
            moe(nc, tag, x_sb, ident, iota16, eps, x_in, x_out, ins["router_w"], ins["router_b"], ins["gate_w"],
                ins["up_w"], ins["down_w"], ins["conv_w"], ins["shared_up"], ins["shared_down"], comb_dram)

        ffn("a", ins["x"], x_dram)
        for layer in range(NL):
            retention_layer(nc, layer, x_sb, ident, eps, ins, x_dram)
        ffn("b", None, out)


def kernel(**inputs):
    import concourse.bacc as bacc
    from concourse.bass_utils import run_bass_kernel_spmd

    a = {k: np.ascontiguousarray(v) for k, v in inputs.items()}
    arrays = {
        "x": a["L0_attn_x"].reshape(TOK, D),
        "router_w": a["L0_ffn_router_w"],
        "router_b": a["L0_ffn_router_bias"].reshape(E, 1),
        "gate_w": a["L0_ffn_expert_gate_w"],
        "up_w": a["L0_ffn_expert_up_w"],
        "down_w": a["L0_ffn_expert_down_w"],
        "conv_w": np.ascontiguousarray(a["L0_ffn_conv_w"].transpose(2, 1, 0)).reshape(TAPS * D, P),
        "shared_up": a["L0_ffn_shared_up_w"],
        "shared_down": a["L0_ffn_shared_down_w"],
    }
    for name in ("proj_w", "proj_b", "reto_w", "reto_b", "ffn1_w", "ffn2_w", "lnf_g", "lnf_b"):
        arrays[name] = a[f"L0_attn_{name}"]

    def by_partition(name):
        return np.ascontiguousarray(a[f"L0_attn_{name}"].reshape(NL, -1, P).transpose(0, 2, 1))

    for name in ("ln1_g", "ln1_b", "ln2_g", "ln2_b", "ffn1_b", "ffn2_b"):
        arrays[name] = by_partition(name)
    arrays["proj_b_cols"] = by_partition("proj_b")
    arrays.update(shape_constants())
    nc = bacc.Bacc("TRN2", target_bir_lowering=False, num_devices=1)
    ins = {k: nc.dram_tensor(f"in_{k}", v.shape, F32, kind="ExternalInput").ap() for k, v in arrays.items()}
    out = nc.dram_tensor("out_x", (TOK, D), F32, kind="ExternalOutput").ap()
    macaron(nc, ins, out)
    result = run_bass_kernel_spmd(nc, [{f"in_{k}": v for k, v in arrays.items()}], core_ids=[0])
    return result.results[0]["out_x"].reshape(B, S, D)


def shape_constants():
    gamma = 1.0 - 2.0 ** (-5.0 - np.arange(H, dtype=np.float64))
    n = np.arange(P)
    ahead = n[None, :] - n[:, None]
    decay = np.where(ahead[:, None, :] >= 0, gamma[None, :, None] ** np.maximum(ahead, 0)[:, None, :], 0.0)
    head = (np.arange(D) // HD).reshape(KD, P).T
    own = n // HD
    f32 = np.float32
    return {
        "decay": decay.reshape(P, H * P).astype(f32),
        "key_decay": (gamma[np.arange(D) // HD][None, :] ** (P - n)[:, None]).astype(f32),
        "query_decay": (gamma[head][:, :, None] ** n[None, None, :]).astype(f32),
        "state_decay": (gamma[head] ** P).astype(f32),
        "own_head": (own[:, None] == own[None, :]).astype(f32),
        "head_mask": (own[:, None] == np.arange(HG)[None, :]).astype(f32),
        "ident": np.eye(P, dtype=np.float32),
        "iota16": np.tile(np.arange(E, dtype=np.float32), (P, 1)),
    }
```

```python
from contextlib import ExitStack

import numpy as np

import concourse.bass as bass
from concourse import mybir

F32 = mybir.dt.float32
F32R = mybir.dt.float32r
U32 = mybir.dt.uint32
ALU = mybir.AluOpType
ACT = mybir.ActivationFunctionType
AX_X = mybir.AxisListType.X

P = 128
B, S, D = 4, 1024, 256
TOK = B * S
TILE = 512
SUB = TILE // P
NT = TOK // TILE
PAIRS = NT // 2
KD = D // P
E = 16
NE = E - 1
TAPS = 3
HALO = TAPS - 1
SHARED_COLS = (TAPS * KD + KD) * P + D
EXPERT_COLS = 2 * KD * P + D
CB_GROUP = 3
GROUPS = NE // CB_GROUP
EPS = 1e-5
CREDIT = 2
PREPARED = 4

NL = 2
H = 16
HD = D // H
F = 4 * D
KF = F // P
HG = P // HD


def split3(tensor, out, w_hi, w_lo, x_hi, x_lo, start, stop):
    tensor.matmul(out, w_hi, x_hi, start=start, stop=False)
    tensor.matmul(out, w_hi, x_lo, start=False, stop=False)
    return tensor.matmul(out, w_lo, x_hi, start=False, stop=stop)



def ahead_buffers(nc, ctx):
    shapes = (("stats", [P, SUB, 6]), ("mv", [P, SUB, 2]), ("std", [P, SUB]), ("rstd", [P, SUB]), ("carrier", [P, 1]))
    return [ctx.enter_context(nc.sbuf_tensor(f"ahead_{name}", shape, F32)) for name, shape in shapes]


def ahead_signals(sem):
    return [sem(f"ahead_{name}_done") for name in ("stats", "var", "std", "rstd")]


def measure_ahead(dve, ahead, signals, x_sb, n):
    (stats, mv, _, _, carrier), (stats_done, var_done, _, _) = ahead, signals
    dve.memset(carrier[:, :], 0.0)
    for s in range(SUB):
        last = dve.bn_stats(stats[:, s, :], x_sb[:, s, :])
    last.then_inc(stats_done, 1)
    dve.wait_ge(stats_done, n + 1)
    dve.memset(carrier[:, :], 0.0)
    for s in range(SUB):
        last = dve.bn_aggr(mv[:, s, :], stats[:, s, :])
    last.then_inc(var_done, 1)


def root_ahead(nc, act, ahead, signals, eps, n):
    (_, mv, std, _, _), (_, var_done, std_done, _) = ahead, signals
    act.wait_ge(var_done, n + 1)
    nc.scalar.activation(std[:, :], mv[:, :, 1], ACT.Sqrt, bias=eps[:, :]).then_inc(std_done, 1)


def invert_ahead(dve, ahead, signals, n):
    (_, _, std, rstd, _), (_, _, std_done, rstd_done) = ahead, signals
    dve.wait_ge(std_done, n + 1)
    dve.reciprocal(rstd[:, :], std[:, :]).then_inc(rstd_done, 1)


def apply_ahead(dve, ahead, x_sb, dst):
    _, mv, _, rstd, _ = ahead
    for s in range(SUB):
        last = dve.tensor_scalar(dst(s), x_sb[:, s, :], mv[:, s, 0:1], rstd[:, s:s + 1], ALU.subtract, ALU.mult)
    return last


def moe(nc, tag, x_sb, ident, iota16, eps, x_in, out, router_w, router_b, gate_w, up_w, down_w, conv_w,
        shared_up, shared_down, comb_dram, ahead):
    with ExitStack() as ctx:
        def sb(name, shape, dt=F32):
            return ctx.enter_context(nc.sbuf_tensor(f"{tag}_{name}", shape, dt))

        sems = []

        def sem(name):
            sems.append(nc.alloc_semaphore(f"{tag}_{name}"))
            return sems[-1]

        w_hi = sb("w_hi", [P, SHARED_COLS + NE * EXPERT_COLS], F32R)
        w_lo = sb("w_lo", [P, SHARED_COLS + NE * EXPERT_COLS], F32R)
        stage = sb("stage", [P, 2, EXPERT_COLS])
        rw_f = sb("rw_f", [P, KD, P])
        rw_hi = sb("rw_hi", [P, KD, P], F32R)
        rw_lo = sb("rw_lo", [P, KD, P], F32R)
        rb = sb("rb", [P, 1])
        xn = sb("xn", [P, 2, SUB, D])
        x_hi = sb("x_hi", [P, 2, KD, HALO + TILE], F32R)
        x_lo = sb("x_lo", [P, 2, KD, HALO + TILE], F32R)
        silu_g = sb("silu_g", [P, 2, TILE])
        weighted = sb("weighted", [P, 2, TILE])
        h = sb("h", [P, 2, TILE])
        h_hi = sb("h_hi", [P, 2, TILE], F32R)
        h_lo = sb("h_lo", [P, 2, TILE], F32R)
        cb = sb("cb", [P, 2, CB_GROUP * TILE])
        oT = sb("oT", [P, KD, TILE])
        stats = sb("stats", [P, SUB, 6])
        mv = sb("mv", [P, SUB, 2])
        std = sb("std", [P, SUB])
        rstd = sb("rstd", [P, SUB])
        lgT = sb("lgT", [P, TILE])
        carrier = sb("carrier", [P, 1])
        warm_out = sb("warm_out", [P, 1])
        lmax = sb("lmax", [P, SUB])
        shifted = sb("shifted", [P, SUB, E])
        ex = sb("ex", [P, SUB, E])
        probs = sb("probs", [P, SUB, E])
        top = sb("top", [P, SUB, 8])
        top_i = sb("top_i", [P, SUB, 8], U32)
        top_f = sb("top_f", [P, SUB, 2])
        sums = sb("sums", [P, SUB])
        norm_w = sb("norm_w", [P, SUB, 2])
        pick = sb("pick", [P, 2, SUB, E])
        comb = sb("comb", [P, 2, SUB, E])
        combT = lgT

        gate_ps = ctx.enter_context(nc.psum_tensor(f"{tag}_gate_ps", [P, 2, TILE], F32))
        up_ps = ctx.enter_context(nc.psum_tensor(f"{tag}_up_ps", [P, 2, TILE], F32))
        acc_ps = ctx.enter_context(nc.psum_tensor(f"{tag}_acc_ps", [P, KD, TILE], F32))
        t_ps = ctx.enter_context(nc.psum_tensor(f"{tag}_t_ps", [P, 2, TILE], F32))

        x0_in, x1_in, x_rest_in, group_used = sem("x0_in"), sem("x1_in"), sem("x_rest_in"), sem("group_used")
        stage_in = [sem(f"stage_in{i}") for i in range(2)]
        rw_in, rw_zero, rw_hi_done = sem("rw_in"), sem("rw_zero"), sem("rw_hi_done")
        w_hi_done, w_lo_done = sem("w_hi_done"), sem("w_lo_done")
        halo_zero = sem("halo_zero")
        stats_done, var_done, std_done, rstd_done = (
            sem("stats_done"), sem("var_done"), sem("std_done"), sem("rstd_done"))
        xn_done, xT_done, x_hi_done, x_lo_done, halo_done = (
            sem("xn_done"), sem("xT_done"), sem("x_hi_done"), sem("x_lo_done"), sem("halo_done"))
        logits_done, lgT_done, lg_done = sem("logits_done"), sem("lgT_done"), sem("lg_done")
        lmax_done, shifted_done, ex_done = sem("lmax_done"), sem("shifted_done"), sem("ex_done")
        soft_step = sem("soft_step")
        comb_done, combT_ps_done, combT_done = sem("comb_done"), sem("combT_ps_done"), sem("combT_done")
        comb_stored = sem("comb_stored")
        cb_in = [sem(f"cb_in{i}") for i in range(2)]
        gateup_done, silu_done, weighted_done, h_done, h_hi_done, h_lo_done, down_done = (
            sem("gateup_done"), sem("silu_done"), sem("weighted_done"), sem("h_done"),
            sem("h_hi_done"), sem("h_lo_done"), sem("down_done"))
        oT_done, back_done, mixed_done, x_done = (
            sem("oT_done"), sem("back_done"), sem("mixed_done"), sem("x_done"))
        stored = sem("stored")
        begins, ends = x_in is not None, out is None or x_in is None
        signals = ahead_signals(sem)
        ahead_applied = sem("ahead_applied")

        def wcol(u):
            return 0 if u == 0 else SHARED_COLS + (u - 1) * EXPERT_COLS

        def cols(u):
            return SHARED_COLS if u == 0 else EXPERT_COLS

        taps, pair = TAPS * KD * P, KD * P
        pieces = [(0, [(0, taps, conv_w)]), (taps, [(0, pair, shared_up), (pair, D, shared_down)])]
        pieces += [(wcol(e + 1), [(0, pair, gate_w[e]), (pair, pair, up_w[e]), (2 * pair, D, down_w[e])])
                   for e in range(NE)]

        def piece_cols(n):
            return sum(width for _, width, _ in pieces[n][1])

        def stage_count(n):
            return 16 * sum(len(pieces[m][1]) for m in range(n % 2, n + 1, 2))

        def tile_view(dram, t):
            return dram.rearrange("(t s p) d -> t p s d", s=SUB, p=P)[t]

        def steps(engine, tile):
            tile(0, 0, False)
            with engine.Fori(0, PAIRS - 1) as i:
                tile(i, 1, False)
                tile(i, 2, False)
            tile(0, NT - 1, True)

        with nc.Block() as block:

            @block.sync
            def _(sp):
                if x_in is not None:
                    sp.dma_start(x_sb[:, 0:SUB, :], tile_view(x_in, 0)).then_inc(x0_in, 16)
                sp.wait_ge(rw_zero, 2)
                sp.dma_start(rw_f[:, :, 0:E], router_w.rearrange("(k p) e -> p k e", p=P)).then_inc(rw_in, 16)
                sp.dma_start(rb[0:E, :], router_b).then_inc(rw_in, 16)

                def load_pieces(first, end):
                    for n in range(first, end):
                        if n >= 2:
                            sp.wait_ge(w_lo_done, n)
                        for at, width, src in pieces[n][1]:
                            dst = stage[:, n % 2, at:at + width]
                            if width > D or src.shape[0] > P:
                                dst = dst.rearrange("p (k i) -> p k i", i=P)
                                src = src.rearrange("(k p) i -> p k i", p=P)
                            sp.dma_start(dst, src).then_inc(stage_in[n % 2], 16)

                def store_comb(i, off):
                    t = 2 * i + off
                    sp.wait_ge(combT_done, t + 1)
                    sp.dma_start(comb_dram[off % 2], combT[0:E, :]).then_inc(comb_stored, 16)

                def load_cb(i, off, g):
                    s = GROUPS * off + g
                    if g == 0:
                        sp.wait_ge(comb_stored, 16 * (2 * i + off + 1))
                    else:
                        sp.wait_ge(group_used, 2 * GROUPS * i + s - 1 + CREDIT)
                    src = comb_dram[off % 2][g * CB_GROUP:(g + 1) * CB_GROUP, :].rearrange("e n -> (e n)")
                    sp.dma_start(cb[:, s % 2, :], src.partition_broadcast(P)).then_inc(cb_in[s % 2], 16)

                def tile(i, off, last):
                    t = 2 * i + off
                    begin = isinstance(i, int) and off == 0
                    for g, upto in ((2, 10), (3, 13), (4, 16)):
                        if begin:
                            load_pieces(upto - (4 if g == 2 else 3), upto)
                        load_cb(i, off, g)
                    if begin:
                        load_pieces(16, len(pieces))
                    if out is not None and not begin:
                        sp.wait_ge(x_done, t + CREDIT)
                        sp.dma_start(tile_view(out, t - 1), x_sb[:, bass.ds((t - 1) * SUB, SUB), :]).then_inc(stored, 16)
                    if not last:
                        store_comb(i, off + 1)
                        for g in range(2):
                            load_cb(i, off + 1, g)

                load_pieces(0, 6)
                store_comb(0, 0)
                for g in range(2):
                    load_cb(0, 0, g)
                steps(sp, tile)
                if out is not None:
                    sp.wait_ge(x_done, NT + CREDIT)
                    sp.dma_start(tile_view(out, NT - 1), x_sb[:, (NT - 1) * SUB:, :]).then_inc(stored, 16)
                    sp.wait_ge(stored, 16 * NT)

            @block.scalar
            def _(act):
                def load_x(t, done):
                    act.dma_start(x_sb[:, t * SUB:(t + 1) * SUB, :], tile_view(x_in, t)).then_inc(done, 16)

                if x_in is not None:
                    load_x(1, x1_in)
                act.sem_inc(h_hi_done, CREDIT)
                act.sem_inc(oT_done, CREDIT)
                act.sem_inc(silu_done, CREDIT)
                if not begins:
                    act.sem_inc(std_done, 1)

                def warm(func):
                    nc.scalar.activation(warm_out[:, :], eps[:, :], func)

                def root(t):
                    act.wait_ge(var_done, t + 1)
                    nc.scalar.activation(std[:, :], mv[:, :, 1], ACT.Sqrt, bias=eps[:, :]).then_inc(std_done, 1)
                    warm(ACT.Silu)

                def evacuate_xT(t, j):
                    act.wait_ge(xT_done, t + 1)
                    nc.scalar.activation(x_hi[:, j, :, HALO:], t_ps[:, :, :], ACT.Copy).then_inc(x_hi_done, 1)

                def evacuate_logits(t):
                    act.wait_ge(logits_done, t + 1)
                    nc.scalar.activation(lgT[:, :], t_ps[:, 0, :], ACT.Identity, bias=rb[:, :]).then_inc(lgT_done, 1)

                def exponent(t):
                    act.wait_ge(shifted_done, t + 1)
                    nc.scalar.activation(ex[:, :, :], shifted[:, :, :], ACT.Exp).then_inc(ex_done, 1)
                    warm(ACT.Silu)

                def evacuate_comb(t):
                    act.wait_ge(combT_ps_done, t + 1)
                    if not isinstance(t, int) or t > 0:
                        act.wait_ge(comb_stored, 16 * t)
                        act.wait_ge(group_used, GROUPS * t - 1 + CREDIT)
                    nc.scalar.activation(combT[0:E, :], t_ps[0:E, 0, :], ACT.Copy).then_inc(combT_done, 1)

                def unit(t, u):
                    n, b = E * t + u, u % 2
                    act.wait_ge(gateup_done, n + 1)
                    act.wait_ge(h_done, n - 1 + CREDIT)
                    nc.scalar.activation(silu_g[:, b, :], gate_ps[:, b, :], ACT.Silu).then_inc(silu_done, 1)
                    act.wait_ge(h_done, n + 1 + CREDIT)
                    act.wait_ge(down_done, n - 1 + CREDIT)
                    nc.scalar.activation(h_hi[:, b, :], h[:, b, :], ACT.Copy).then_inc(h_hi_done, 1)

                def copy_sum(t):
                    act.wait_ge(down_done, E * t + CREDIT)
                    nc.scalar.activation(oT[:, :, :], acc_ps[:, :, :], ACT.Copy).then_inc(oT_done, 1)

                def tile(i, off, last):
                    t, j = 2 * i + off, off % 2
                    begin = isinstance(i, int) and off == 0
                    for u in range(E):
                        unit(t, u)
                        if u == 0 and not begin:
                            copy_sum(t)
                        if begin and u == 4 and x_in is not None:
                            for later in range(2, NT):
                                load_x(later, x_rest_in)
                        if not last:
                            if u == 2:
                                root(t + 1)
                            if u == 5:
                                evacuate_xT(t + 1, 1 - j)
                            if u == 7:
                                evacuate_logits(t + 1)
                            if u == 9:
                                exponent(t + 1)
                            if u == 13:
                                evacuate_comb(t + 1)
                        elif not ends and u in (2, 6):
                            root_ahead(nc, act, ahead, signals, eps, u // 4)
                            warm(ACT.Silu)

                if begins:
                    root(0)
                else:
                    warm(ACT.Silu)
                evacuate_xT(0, 0)
                evacuate_logits(0)
                exponent(0)
                evacuate_comb(0)
                steps(act, tile)
                copy_sum(NT)

            @block.gpsimd
            def _(pool):
                pool.memset(rw_f[:, :, :], 0.0).then_inc(rw_zero, 1)
                pool.memset(rb[:, :], 0.0).then_inc(rw_zero, 1)
                pool.memset(x_hi[:, 0, :, 0:HALO].bitcast(F32), 0.0).then_inc(halo_zero, 1)
                pool.memset(x_lo[:, 0, :, 0:HALO].bitcast(F32), 0.0).then_inc(halo_zero, 1)
                pool.sem_inc(h_done, CREDIT)
                pool.wait_ge(rw_hi_done, 1)
                pool.tensor_tensor(rw_lo[:, :, :], rw_f[:, :, :], rw_hi[:, :, :].bitcast(F32), ALU.subtract).then_inc(w_lo_done, 1)

                def low_weights(n):
                    a, width = pieces[n][0], piece_cols(n)
                    pool.wait_ge(w_hi_done, n + 1)
                    pool.tensor_tensor(w_lo[:, a:a + width], stage[:, n % 2, 0:width],
                                       w_hi[:, a:a + width].bitcast(F32), ALU.subtract).then_inc(w_lo_done, 1)

                def unit(t, u):
                    n, b = E * t + u, u % 2
                    pool.wait_ge(silu_done, n + 1 + CREDIT)
                    pool.wait_ge(weighted_done, n + 1 + CREDIT)
                    pool.wait_ge(h_lo_done, n - 1 + CREDIT)
                    pool.tensor_tensor(h[:, b, :], silu_g[:, b, :], weighted[:, b, :], ALU.mult).then_inc(h_done, 1)

                def tile(i, off, last):
                    for u in range(E):
                        unit(2 * i + off, u)
                        if isinstance(i, int) and off == 0 and u + PREPARED < len(pieces):
                            low_weights(u + PREPARED)

                for n in range(PREPARED):
                    low_weights(n)
                steps(pool, tile)

            @block.vector
            def _(dve):
                dve.sem_inc(weighted_done, CREDIT)
                dve.sem_inc(h_lo_done, CREDIT)
                dve.sem_inc(group_used, CREDIT)
                dve.sem_inc(x_done, CREDIT)
                def split_weights(n):
                    a, width = pieces[n][0], piece_cols(n)
                    dve.wait_ge(stage_in[n % 2], stage_count(n))
                    dve.tensor_copy(w_hi[:, a:a + width], stage[:, n % 2, 0:width]).then_inc(w_hi_done, 1)

                def statistics(t):
                    if x_in is not None:
                        if not isinstance(t, int) or t > 1:
                            dve.wait_ge(x_rest_in, 16 * (NT - 2))
                        else:
                            dve.wait_ge((x0_in, x1_in)[t], 16)
                    for s in range(SUB):
                        last = dve.bn_stats(stats[:, s, :], x_sb[:, t * SUB + s, :])
                    last.then_inc(stats_done, 1)
                    dve.wait_ge(stats_done, t + 1)
                    dve.memset(carrier[:, :], 0.0)
                    for s in range(SUB):
                        last = dve.bn_aggr(mv[:, s, :], stats[:, s, :])
                    last.then_inc(var_done, 1)

                def normalise(t, j):
                    dve.wait_ge(std_done, t + 1)
                    dve.reciprocal(rstd[:, :], std[:, :]).then_inc(rstd_done, 1)
                    dve.wait_ge(rstd_done, t + 1)
                    for s in range(SUB):
                        last = dve.tensor_scalar(xn[:, j, s, :], x_sb[:, t * SUB + s, :], mv[:, s, 0:1],
                                                 rstd[:, s:s + 1], ALU.subtract, ALU.mult)
                    last.then_inc(xn_done, 1)

                def low_parts(t, j):
                    if j == 1:
                        dve.wait_ge(x_lo_done, t)
                        dve.tensor_copy(x_lo[:, 1, :, 0:HALO], x_lo[:, 0, :, TILE:]).then_inc(halo_done, 1)
                        dve.tensor_copy(x_hi[:, 1, :, 0:HALO], x_hi[:, 0, :, TILE:]).then_inc(halo_done, 1)
                    dve.wait_ge(x_hi_done, t + 1)
                    dve.tensor_tensor(x_lo[:, j, :, HALO:], t_ps[:, :, :], x_hi[:, j, :, HALO:].bitcast(F32),
                                      ALU.subtract).then_inc(x_lo_done, 1)

                def take_maximum(t):
                    dve.wait_ge(lg_done, t + 1)
                    lg = t_ps[:, 1, :].rearrange("p (s e) -> p s e", e=P)[:, :, 0:E]
                    dve.reduce_max(lmax[:, :], lg, AX_X).then_inc(lmax_done, 1)
                    dve.wait_ge(lmax_done, t + 1)
                    dve.tensor_tensor(shifted[:, :, :], lg, lmax[:, :].unsqueeze(2).broadcast_to([P, SUB, E]),
                                      ALU.subtract).then_inc(shifted_done, 1)

                SOFT_STEPS = 10

                def choose(t, j):
                    step = [0]

                    def link(ins):
                        step[0] += 1
                        ins.then_inc(soft_step, 1)
                        dve.wait_ge(soft_step, t * SOFT_STEPS + step[0])

                    dve.wait_ge(ex_done, t + 1)
                    link(dve.reduce_sum(sums[:, :], ex[:, :, :], AX_X))
                    link(dve.reciprocal(sums[:, :], sums[:, :]))
                    link(dve.tensor_tensor(probs[:, :, :], ex[:, :, :], sums[:, :].unsqueeze(2).broadcast_to([P, SUB, E]), ALU.mult))
                    dve.memset(carrier[:, :], 0.0)
                    for s in range(SUB):
                        last = dve.max(top[:, s, :], probs[:, s, :])
                    link(last)
                    dve.memset(carrier[:, :], 0.0)
                    for s in range(SUB):
                        dve.max_index(top_i[:, s, :], top[:, s, :], probs[:, s, :])
                    link(dve.tensor_tensor(sums[:, :], top[:, :, 0], top[:, :, 1], ALU.add))
                    dve.tensor_copy(top_f[:, :, :], top_i[:, :, 0:2])
                    link(dve.tensor_scalar_add(sums[:, :], sums[:, :], 1e-6))
                    link(dve.reciprocal(sums[:, :], sums[:, :]))
                    link(dve.tensor_tensor(norm_w[:, :, :], top[:, :, 0:2], sums[:, :].unsqueeze(2).broadcast_to([P, SUB, 2]), ALU.mult))
                    for k in range(2):
                        last = dve.tensor_tensor(pick[:, k, :, :], iota16[:, :].unsqueeze(1).broadcast_to([P, SUB, E]),
                                                 top_f[:, :, k:k + 1].broadcast_to([P, SUB, E]), ALU.is_equal)
                    link(last)
                    for k in range(2):
                        last = dve.tensor_tensor(pick[:, k, :, :], pick[:, k, :, :],
                                                 norm_w[:, :, k:k + 1].broadcast_to([P, SUB, E]), ALU.mult)
                    link(last)
                    assert step[0] == SOFT_STEPS
                    dve.tensor_tensor(comb[:, j, :, :], pick[:, 0, :, :], pick[:, 1, :, :], ALU.add).then_inc(comb_done, 1)

                def weight_up(i, off, u):
                    t = 2 * i + off
                    n, b, e = E * t + u, u % 2, u - 1
                    dve.wait_ge(gateup_done, n + 1)
                    dve.wait_ge(h_done, n - 1 + CREDIT)
                    if u == 0:
                        dve.tensor_copy(weighted[:, b, :], up_ps[:, b, :]).then_inc(weighted_done, 1)
                        return
                    g, r = divmod(e, CB_GROUP)
                    s = GROUPS * off + g
                    if r == 0:
                        dve.wait_ge(cb_in[s % 2], 16 * (GROUPS * i + s // 2 + 1))
                    done = dve.tensor_tensor(weighted[:, b, :], up_ps[:, b, :], cb[:, s % 2, r * TILE:(r + 1) * TILE], ALU.mult)
                    done.then_inc(weighted_done, 1)
                    if r == CB_GROUP - 1:
                        dve.wait_ge(weighted_done, n + 1 + CREDIT)
                        dve.sem_inc(group_used, 1)

                def low_product(t, u):
                    n, b = E * t + u, u % 2
                    dve.wait_ge(h_hi_done, n + 1 + CREDIT)
                    dve.tensor_tensor(h_lo[:, b, :], h[:, b, :], h_hi[:, b, :].bitcast(F32), ALU.subtract).then_inc(h_lo_done, 1)

                def finish(t, j):
                    dve.wait_ge(back_done, t)
                    back = t_ps[:, :, :].rearrange("p a n -> p (a n)").rearrange("p (s d) -> p s d", d=D)
                    for s in range(SUB):
                        last = dve.scalar_tensor_tensor(xn[:, j, s, :], xn[:, j, s, :], comb[:, j, s, E - 1:E],
                                                        back[:, s, :], ALU.mult, ALU.add)
                    last.then_inc(mixed_done, 1)
                    dve.wait_ge(mixed_done, t)
                    for s in range(SUB):
                        row = (t - 1) * SUB + s
                        last = dve.scalar_tensor_tensor(x_sb[:, row, :], xn[:, j, s, :], 0.5, x_sb[:, row, :], ALU.mult, ALU.add)
                    last.then_inc(x_done, 1)

                def tile(i, off, last):
                    t, j = 2 * i + off, off % 2
                    begin = isinstance(i, int) and off == 0
                    for u in range(E):
                        weight_up(i, off, u)
                        if u > 0:
                            low_product(t, u - 1)
                        elif not begin:
                            low_product(t - 1, E - 1)
                        if begin and u + PREPARED < len(pieces):
                            split_weights(u + PREPARED)
                        if u == 2 and not begin:
                            finish(t, 1 - j)
                        if not last:
                            if u == 1:
                                statistics(t + 1)
                            if u == 3:
                                normalise(t + 1, 1 - j)
                            if u == 5:
                                low_parts(t + 1, 1 - j)
                            if u == 9:
                                take_maximum(t + 1)
                            if u == 10:
                                choose(t + 1, 1 - j)
                        elif not ends:
                            if u == 1:
                                measure_ahead(dve, ahead, signals, x_sb, 0)
                            if u == 4:
                                invert_ahead(dve, ahead, signals, 0)
                                dve.wait_ge(signals[3], 1)
                                dve.wait_ge(stored, 16)
                                dve.memset(carrier[:, :], 0.0)
                                apply_ahead(dve, ahead, x_sb, lambda s: x_sb[:, s, :]).then_inc(ahead_applied, 1)
                            if u == 5:
                                dve.wait_ge(ahead_applied, 1)
                                measure_ahead(dve, ahead, signals, x_sb, 1)
                            if u == 8:
                                invert_ahead(dve, ahead, signals, 1)

                if begins:
                    statistics(0)
                    normalise(0, 0)
                else:
                    for done in (stats_done, var_done, rstd_done):
                        dve.sem_inc(done, 1)
                    apply_ahead(dve, ahead, x_sb, lambda s: xn[:, 0, s, :]).then_inc(xn_done, 1)
                dve.wait_ge(rw_in, 32)
                dve.tensor_copy(rw_hi[:, :, :], rw_f[:, :, :]).then_inc(rw_hi_done, 1)
                split_weights(0)
                low_parts(0, 0)
                split_weights(1)
                take_maximum(0)
                split_weights(2)
                choose(0, 0)
                for n in range(3, PREPARED):
                    split_weights(n)
                steps(dve, tile)
                low_product(NT - 1, E - 1)
                finish(NT, 1)

            @block.tensor
            def _(pe):
                pe.sem_inc(down_done, CREDIT)

                def turn_x(t, j):
                    pe.wait_ge(xn_done, t + 1)
                    pe.wait_ge(x_done, t - 1 + CREDIT)
                    for k in range(KD):
                        for s in range(SUB):
                            last = pe.transpose(t_ps[:, k, s * P:(s + 1) * P], xn[:, j, s, k * P:(k + 1) * P], ident[:, :])
                    last.then_inc(xT_done, 1)

                def route(t, j):
                    pe.wait_ge(x_lo_done, t + 1)
                    pe.wait_ge(w_lo_done, 1)
                    for k in range(KD):
                        last = split3(pe, t_ps[:, 0, :], rw_hi[:, k, :], rw_lo[:, k, :], x_hi[:, j, k, HALO:],
                                      x_lo[:, j, k, HALO:], k == 0, k == KD - 1)
                    last.then_inc(logits_done, 1)

                def turn_logits(t):
                    pe.wait_ge(lgT_done, t + 1)
                    for s in range(SUB):
                        last = pe.transpose(t_ps[:, 1, s * P:(s + 1) * P], lgT[:, s * P:(s + 1) * P], ident[:, :])
                    last.then_inc(lg_done, 1)

                def turn_comb(t, j):
                    pe.wait_ge(comb_done, t + 1)
                    for s in range(SUB):
                        last = pe.transpose(t_ps[0:E, 0, s * P:(s + 1) * P], comb[:, j, s, :], ident[:, :])
                    last.then_inc(combT_ps_done, 1)

                def gateup(t, j, u):
                    n, b = E * t + u, u % 2
                    pe.wait_ge(w_lo_done, u + 3)
                    pe.wait_ge(silu_done, n - 1 + CREDIT)
                    pe.wait_ge(weighted_done, n - 1 + CREDIT)
                    a = wcol(u)
                    if u == 0:
                        if j == 1:
                            pe.wait_ge(halo_done, t + 1)
                        if j == 0:
                            pe.wait_ge(halo_zero, 2)
                        taps = TAPS
                    else:
                        taps = 1
                    for c in range(taps):
                        lead = c if u == 0 else HALO
                        for k in range(KD):
                            w = slice(a + (c * KD + k) * P, a + (c * KD + k + 1) * P)
                            split3(pe, gate_ps[:, b, :], w_hi[:, w], w_lo[:, w], x_hi[:, j, k, lead:lead + TILE],
                                   x_lo[:, j, k, lead:lead + TILE], c == 0 and k == 0, c == taps - 1 and k == KD - 1)
                    a += taps * KD * P
                    for k in range(KD):
                        w = slice(a + k * P, a + (k + 1) * P)
                        last = split3(pe, up_ps[:, b, :], w_hi[:, w], w_lo[:, w], x_hi[:, j, k, HALO:],
                                      x_lo[:, j, k, HALO:], k == 0, k == KD - 1)
                    last.then_inc(gateup_done, 1)

                def down(t, u):
                    n, b = E * t + u, u % 2
                    pe.wait_ge(h_lo_done, n + 1 + CREDIT)
                    if u == 0:
                        pe.wait_ge(oT_done, t + CREDIT)
                    a = wcol(u) + cols(u) - D
                    for k in range(KD):
                        w = slice(a + k * P, a + (k + 1) * P)
                        last = split3(pe, acc_ps[:, k, :], w_hi[:, w], w_lo[:, w], h_hi[:, b, :], h_lo[:, b, :],
                                      u == 0, u == E - 1)
                    last.then_inc(down_done, 1)

                def turn_back(t):
                    pe.wait_ge(oT_done, t + CREDIT)
                    if not isinstance(t, int) or t < NT:
                        pe.wait_ge(combT_done, t + 1)
                    back = t_ps[:, :, :].rearrange("p a n -> p (a n)")
                    for s in range(SUB):
                        for k in range(KD):
                            done = pe.transpose(back[:, s * D + k * P:s * D + (k + 1) * P], oT[:, k, s * P:(s + 1) * P], ident[:, :])
                    done.then_inc(back_done, 1)

                def tile(i, off, last):
                    t, j = 2 * i + off, off % 2
                    begin = isinstance(i, int) and off == 0
                    for u in range(E):
                        if u + 2 < E:
                            gateup(t, j, u + 2)
                        elif not last:
                            gateup(t + 1, 1 - j, u + 2 - E)
                        down(t, u)
                        if u == 0 and not begin:
                            turn_back(t)
                        if not last:
                            if u == 3:
                                turn_x(t + 1, 1 - j)
                            if u == 5:
                                route(t + 1, 1 - j)
                            if u == 7:
                                turn_logits(t + 1)
                            if u == 10:
                                turn_comb(t + 1, 1 - j)

                turn_x(0, 0)
                route(0, 0)
                turn_logits(0)
                gateup(0, 0, 0)
                turn_comb(0, 0)
                gateup(0, 0, 1)
                steps(pe, tile)
                turn_back(NT)

        hand_back(nc, sems)


def hand_back(nc, sems):
    nc.clear_and_free_semaphores(sems)
    nc.all_engine_barrier()


def retention_layer(nc, layer, h_sb, ident, eps, ins, x_dram, ahead):
    first, final = layer == 0, layer == NL - 1
    tag = f"l{layer}"
    with ExitStack() as ctx:
        def sb(name, shape, dt=F32):
            return ctx.enter_context(nc.sbuf_tensor(f"{tag}_{name}", shape, dt))

        sems = []

        def sem(name):
            sems.append(nc.alloc_semaphore(f"{tag}_{name}"))
            return sems[-1]

        def halves(name, shape):
            return sb(name + "_hi", shape, F32R), sb(name + "_lo", shape, F32R)

        wp_hi, wp_lo = halves("wp", [P, KD, 4 * D])
        wr_hi, wr_lo = halves("wr", [P, KD, D])
        w1_hi, w1_lo = halves("w1", [P, KD, F])
        w2_hi, w2_lo = halves("w2", [P, KF, D])
        past = sb("past", [P, P])
        query_decay = sb("query_decay", [P, KD, P])
        key_decay = sb("key_decay", [P, KD, P])
        state_decay = sb("state_decay", [P, KD])
        own_head = sb("own_head", [P, KD, P])
        head_mask = sb("head_mask", [P, HG])
        norm1 = sb("norm1", [P, 2, KD])
        norm2 = sb("norm2", [P, 2, KD])
        proj_b = sb("proj_b", [P, 8])
        ffn1_b = sb("ffn1_b", [P, KF])
        ffn2_b = sb("ffn2_b", [P, KD])
        v_b = sb("v_b", [P, D])
        reto_b = sb("reto_b", [P, D])
        if final:
            normf = sb("normf", [P, 2, D])
            x_old = sb("x_old", [P, SUB, D])
            pool_carrier = sb("pool_carrier", [P, 4])
        carrier = sb("carrier", [P, 1])

        warm_out = sb("warm_out", [P, 1])

        xn = sb("xn", [P, SUB, D])
        full = sb("full", [P, KD, TILE])
        a_hi, a_lo = halves("a", [P, KD, TILE])
        b_hi, b_lo = halves("b", [P, KD, TILE])
        q = sb("q", [P, KD, TILE])
        gated = q
        kT = sb("kT", [P, KD, TILE])
        gate = sb("gate", [P, KD, TILE])
        v = sb("v", [P, SUB, D])
        q_wide = sb("q_wide", [P, 2, KD, HG, P])
        v_wide = sb("v_wide", [P, KD, HG * (P + HD)])
        probs = sb("probs", [P, H * P])
        stage = sb("stage", [P, 2, KD * TILE])
        ks = sb("ks", [P, D])
        state = sb("state", [P, 2, KD, P])
        fresh = sb("fresh", [P, KD, P])
        g_hi, g_lo = halves("g", [P, KD, TILE])
        act_f = sb("act_f", [P, 2, TILE])
        f_hi, f_lo = halves("f", [P, 2, TILE])
        oT = sb("oT", [P, KD, TILE])

        banks = ctx.enter_context(nc.psum_tensor(f"{tag}_banks", [P, 4, TILE], F32))
        t_ps = ctx.enter_context(nc.psum_tensor(f"{tag}_t_ps", [P, 2, TILE], F32))
        rm_ps = ctx.enter_context(nc.psum_tensor(f"{tag}_rm_ps", [P, 2, TILE], F32))
        ret_ps, m_ps = rm_ps[:, 0, :], rm_ps[:, 1, :]
        token_ps = rm_ps[:, :, :].rearrange("p a n -> p (a n)").rearrange("p (s d) -> p s d", d=D)
        back_ps = t_ps[:, :, :].rearrange("p a n -> p (a n)").rearrange("p (s d) -> p s d", d=D)

        norm_in, const_in = sem("norm_in"), sem("const_in")
        stage_in = [sem(f"stage_in{i}") for i in range(2)]
        w_hi_done, w_lo_done, wide_zero = sem("w_hi_done"), sem("w_lo_done"), sem("wide_zero")
        xn0_done, xn_done, xn2_done = sem("xn0_done"), sem("xn_done"), sem("xn2_done")
        aT_done, a_full, a_hi_done, a_lo_done = sem("aT_done"), sem("a_full"), sem("a_hi_done"), sem("a_lo_done")
        bT_done, b_full, b_hi_done, b_lo_done = sem("bT_done"), sem("b_full"), sem("b_hi_done"), sem("b_lo_done")
        proj_done, q_done, k_done, gate_done, v_done = (
            sem("proj_done"), sem("q_done"), sem("k_done"), sem("gate_done"), sem("v_done"))
        wide_q_done, wide_v_done = sem("wide_q_done"), sem("wide_v_done")
        scores_done, probs_done, kturn_done, ks_done = (
            sem("scores_done"), sem("probs_done"), sem("kturn_done"), sem("ks_done"))
        ret_done, gated_done, st_done, fresh_done, state_done = (
            sem("ret_done"), sem("gated_done"), sem("st_done"), sem("fresh_done"), sem("state_done"))
        g_hi_done, g_lo_done, reto_done, reto_read, reto_added = (
            sem("g_hi_done"), sem("g_lo_done"), sem("reto_done"), sem("reto_read"), sem("reto_added"))
        ffn1_done, act_done, f_hi_done, f_lo_done, ffn2_done = (
            sem("ffn1_done"), sem("act_done"), sem("f_hi_done"), sem("f_lo_done"), sem("ffn2_done"))
        oT_done, back_done, added = sem("oT_done"), sem("back_done"), sem("added")
        x_old_in, xf_done, scaled, shifted, final_done = (
            sem("x_old_in"), sem("xf_done"), sem("scaled"), sem("shifted"), sem("final_done"))
        signals = ahead_signals(sem)
        norms = {}
        for kind in ("0", "1", "2", "f"):
            norms[kind] = (sb(f"stats{kind}", [P, SUB, 6]), sb(f"mv{kind}", [P, SUB, 2]), sb(f"std{kind}", [P, SUB]),
                           sb(f"rstd{kind}", [P, SUB]), sem(f"stats{kind}_done"), sem(f"var{kind}_done"),
                           sem(f"std{kind}_done"), sem(f"rstd{kind}_done"))

        def rows(w, k, n=1):
            return w[k * P:(k + n) * P, :].rearrange("(k p) i -> p k i", p=P)

        proj_w, reto_w, ffn1_w, ffn2_w = (ins[n][layer] for n in ("proj_w", "reto_w", "ffn1_w", "ffn2_w"))
        half = KF // 2
        pieces = [(wp_hi[:, k:k + 1, :], wp_lo[:, k:k + 1, :], rows(proj_w, k)) for k in range(KD)]
        pieces += [(wr_hi[:, :, :], wr_lo[:, :, :], rows(reto_w, 0, KD))]
        pieces += [(w1_hi[:, k:k + 1, :], w1_lo[:, k:k + 1, :], rows(ffn1_w, k)) for k in range(KD)]
        pieces += [(w2_hi[:, k:k + half, :], w2_lo[:, k:k + half, :], rows(ffn2_w, k, half)) for k in (0, half)]
        RETO_READY, FFN_READY = KD + 1, len(pieces)

        def staged(n):
            blocks, width = pieces[n][2].shape[1:]
            return stage[:, n % 2, 0:blocks * width].rearrange("p (k i) -> p k i", k=blocks)

        consts = [(norm1[:, 0, :], ins["ln1_g"][layer]), (norm1[:, 1, :], ins["ln1_b"][layer]),
                  (proj_b[:, :], ins["proj_b_cols"][layer]), (query_decay[:, :, :], ins["query_decay"]),
                  (key_decay[:, :, :], ins["key_decay"]), (head_mask[:, :], ins["head_mask"]),
                  (v_b[:, :], ins["proj_b"][layer, 2 * D:3 * D].partition_broadcast(P)),
                  (past[:, :], ins["past"]), (state_decay[:, :], ins["state_decay"]),
                  (own_head[:, :, :], ins["own_head"]),
                  (norm2[:, 0, :], ins["ln2_g"][layer]), (norm2[:, 1, :], ins["ln2_b"][layer]),
                  (ffn1_b[:, :], ins["ffn1_b"][layer]), (ffn2_b[:, :], ins["ffn2_b"][layer]),
                  (reto_b[:, :], ins["reto_b"][layer].partition_broadcast(P))]
        if final:
            consts += [(normf[:, 0, :], ins["lnf_g"].partition_broadcast(P)),
                       (normf[:, 1, :], ins["lnf_b"].partition_broadcast(P))]
        consts_ready = 16 * (len(consts) - 2)
        NORM1_CONSTS = 16 * 2
        SCORES_CREDIT = 2 * KD
        UPDATES = 2 * SUB - 1

        def steps(engine, step):
            step(0, 0, 0, None, True)
            if final:
                step(1, 1, 0, 0, True)
                with engine.Fori(1, PAIRS - 1) as i:
                    step(2 * i, 0, i, 2 * i - 1, True)
                    step(2 * i + 1, 1, i, 2 * i, True)
                step(NT - 2, 0, PAIRS - 1, NT - 3, True)
            else:
                with engine.Fori(0, PAIRS - 1) as i:
                    step(2 * i + 1, 1, i, 2 * i, True)
                    step(2 * i + 2, 0, i + 1, 2 * i + 1, True)
            step(NT - 1, 1, PAIRS - 1, NT - 2, False)
            step(None, None, None, NT - 1, False)

        def finishes(b):
            return final and b is not None and not (isinstance(b, int) and b == 0)

        def turns_last(a, more):
            return a is not None and not more

        with nc.Block() as block:

            @block.sync
            def _(sp):
                for dst, const in consts[:2]:
                    sp.dma_start(dst, const).then_inc(norm_in, 16)
                for n, (_, _, src) in enumerate(pieces):
                    if n == 2:
                        for dst, const in consts[2:]:
                            sp.dma_start(dst, const).then_inc(const_in, 16)
                    if n >= 2:
                        sp.wait_ge(w_lo_done, n - 1)
                    sp.dma_start(staged(n), src).then_inc(stage_in[n % 2], 16)
                if final:
                    view = x_dram.rearrange("(t s p) d -> t p s d", s=SUB, p=P)
                    sp.dma_start(x_old[:, :, :], view[0]).then_inc(x_old_in, 16)
                    with sp.Fori(1, NT) as t:
                        sp.wait_ge(final_done, t)
                        sp.dma_start(x_old[:, :, :], view[t]).then_inc(x_old_in, 16)

            @block.scalar
            def _(act):
                def warm(func):
                    nc.scalar.activation(warm_out[:, :], eps[:, :], func)

                def split_piece(n):
                    act.wait_ge(stage_in[n % 2], 16 * (n // 2 + 1))
                    nc.scalar.activation(pieces[n][0], staged(n), ACT.Copy).then_inc(w_hi_done, 1)

                def root(kind, t):
                    _, mv, std, _, _, var_done, std_done, _ = norms[kind]
                    act.wait_ge(var_done, t + 1)
                    nc.scalar.activation(std[:, :], mv[:, :, 1], ACT.Sqrt, bias=eps[:, :]).then_inc(std_done, 1)

                def high(full_sem, hi, done, t):
                    act.wait_ge(full_sem, t + 1)
                    nc.scalar.activation(hi[:, :, :], full[:, :, :], ACT.Copy).then_inc(done, 1)

                def project(a):
                    for g in range(KD):
                        act.wait_ge(proj_done, 10 * a + g + 5)
                        nc.scalar.activation(gate[:, g, :], banks[:, g, :], ACT.Silu, bias=proj_b[:, 6 + g:7 + g]).then_inc(gate_done, 1)

                def widen_values(a, c):
                    cc = SUB * a + c
                    act.wait_ge(v_done, cc + 1)
                    act.wait_ge(ret_done, 2 * cc + CREDIT)
                    blocks = v_wide[:, :, :].rearrange("p g (h x) -> p g h x", h=HG)
                    for g in range(KD):
                        last = nc.scalar.activation(blocks[:, g, :, 0:HD], v[:, c, g * P:(g + 1) * P].rearrange("p (h x) -> p h x", h=HG), ACT.Copy)
                    last.then_inc(wide_v_done, 1)

                def feed(b, f):
                    n, slot = KF * b + f, f % 2
                    act.wait_ge(ffn1_done, n + 1)
                    act.wait_ge(f_lo_done, n - 1 + CREDIT)
                    nc.scalar.activation(act_f[:, slot, :], banks[:, slot, :], ACT.Gelu, bias=ffn1_b[:, f:f + 1]).then_inc(act_done, 1)
                    act.wait_ge(ffn2_done, n - 1 + CREDIT)
                    nc.scalar.activation(f_hi[:, slot, :], banks[:, slot, :], ACT.Gelu, bias=ffn1_b[:, f:f + 1]).then_inc(f_hi_done, 1)

                def step(a, j, batch, b, more):
                    begin = isinstance(a, int) and a == 0
                    if a is not None:
                        widen_values(a, 0)
                        if begin:
                            split_piece(3)
                        widen_values(a, 1)
                        if begin:
                            split_piece(4)
                        if more and first:
                            root("0", a + 1)
                        widen_values(a, 2)
                        if begin:
                            split_piece(5)
                    if a is not None and b is not None:
                        high(b_full, b_hi, b_hi_done, b)
                    if a is not None:
                        widen_values(a, 3)
                        if more:
                            root("1", a + 1)
                        if begin:
                            split_piece(6)
                    if b is not None:
                        warm(ACT.Gelu)
                    if a is not None:
                        act.wait_ge(gated_done, SUB * (a + 1))
                        nc.scalar.activation(g_hi[:, :, :], gated[:, :, :], ACT.Copy).then_inc(g_hi_done, 1)
                    if b is not None:
                        for f in range(KF):
                            feed(b, f)
                            if f == 3 and more:
                                high(a_full, a_hi, a_hi_done, a + 1)
                            if f == 2 and a is None:
                                root_ahead(nc, act, ahead, signals, eps, 0)
                                warm(ACT.Gelu)
                            if f == 4 and turns_last(a, more):
                                root("2", a)
                                warm(ACT.Gelu)
                        if turns_last(a, more):
                            high(b_full, b_hi, b_hi_done, a)
                        act.wait_ge(ffn2_done, KF * (b + 1) + CREDIT)
                        for k in range(KD):
                            last = nc.scalar.activation(oT[:, k, :], banks[:, 2 + k, :], ACT.Identity, bias=ffn2_b[:, k:k + 1])
                        last.then_inc(oT_done, 1)
                    elif more:
                        high(a_full, a_hi, a_hi_done, a + 1)
                    if a is not None and more:
                        root("2", a)
                        project(a + 1)
                    if b is not None and final:
                        root("f", b)

                for kind in ("0", "1") if first else ("1",):
                    act.sem_inc(norms[kind][6], 1)
                split_piece(0)
                high(a_full, a_hi, a_hi_done, 0)
                split_piece(1)
                act.wait_ge(const_in, consts_ready)
                split_piece(2)
                project(0)
                act.wait_ge(wide_zero, 1)
                steps(act, step)

            @block.gpsimd
            def _(pool):
                pool.memset(v_wide[:, :, :], 0.0).then_inc(wide_zero, 1)

                def split_piece(n):
                    pool.wait_ge(w_hi_done, n + 1)
                    pool.tensor_tensor(pieces[n][1], staged(n), pieces[n][0].bitcast(F32), ALU.subtract).then_inc(w_lo_done, 1)

                def widen_queries(a, c):
                    cc = SUB * a + c
                    for g in range(KD):
                        if c == 0:
                            pool.wait_ge(q_done, KD * a + g + 1)
                        pool.wait_ge(scores_done, 2 * cc - 3 + g + SCORES_CREDIT)
                        pool.tensor_tensor(q_wide[:, c % 2, g, :, :],
                                           q[:, g, c * P:(c + 1) * P].unsqueeze(1).broadcast_to([P, HG, P]),
                                           head_mask[:, :].unsqueeze(2).broadcast_to([P, HG, P]), ALU.mult).then_inc(wide_q_done, 1)

                def low(hi_sem, source, hi, lo, done, t):
                    pool.wait_ge(hi_sem, t + 1)
                    pool.tensor_tensor(lo[:, :, :], source[:, :, :], hi[:, :, :].bitcast(F32), ALU.subtract).then_inc(done, 1)

                def carry(k):
                    pool.tensor_tensor(pool_carrier[:, k:k + 1], norm1[:, 0, 0:1], norm1[:, 1, 0:1], ALU.mult)

                def finish(b):
                    tile = h_sb[:, bass.ds(b * SUB, SUB), :]
                    pool.wait_ge(xf_done, b + 1)
                    carry(0)
                    pool.tensor_tensor(tile, tile, normf[:, 0:1, :].broadcast_to([P, SUB, D]), ALU.mult).then_inc(scaled, 1)
                    pool.wait_ge(scaled, b + 1)
                    carry(1)
                    pool.tensor_tensor(tile, tile, normf[:, 1:2, :].broadcast_to([P, SUB, D]), ALU.add).then_inc(shifted, 1)
                    pool.wait_ge(shifted, b + 1)
                    carry(2)
                    pool.wait_ge(x_old_in, 16 * (b + 1))
                    carry(3)
                    pool.tensor_tensor(tile, tile, x_old[:, :, :], ALU.add).then_inc(final_done, 1)

                def step(a, j, batch, b, more):
                    begin = isinstance(a, int) and a == 0
                    if a is not None:
                        for c in range(2, SUB):
                            widen_queries(a, c)
                            if begin:
                                split_piece(1 + c)
                        if begin:
                            split_piece(1 + SUB)
                            split_piece(2 + SUB)
                    if b is not None:
                        low(b_hi_done, full, b_hi, b_lo, b_lo_done, b)
                    if a is not None:
                        low(g_hi_done, gated, g_hi, g_lo, g_lo_done, a)
                        if more:
                            low(a_hi_done, full, a_hi, a_lo, a_lo_done, a + 1)
                    if finishes(b):
                        finish(b - 1)
                    if more:
                        widen_queries(a + 1, 0)
                        widen_queries(a + 1, 1)

                split_piece(0)
                split_piece(1)
                split_piece(2)
                pool.wait_ge(const_in, consts_ready)
                pool.wait_ge(norm_in, NORM1_CONSTS)
                widen_queries(0, 0)
                widen_queries(0, 1)
                steps(pool, step)

            @block.vector
            def _(dve):
                dve.sem_inc(f_lo_done, CREDIT)
                dve.sem_inc(added, CREDIT)

                def tile_of(t, s=None):
                    if s is None:
                        return h_sb[:, bass.ds(t * SUB, SUB), :]
                    return h_sb[:, t * SUB + s, :]

                def measure(kind, t):
                    stats, mv, _, _, stats_done, var_done, _, _ = norms[kind]
                    dve.memset(carrier[:, :], 0.0)
                    for s in range(SUB):
                        last = dve.bn_stats(stats[:, s, :], tile_of(t, s))
                    last.then_inc(stats_done, 1)
                    dve.wait_ge(stats_done, t + 1)
                    dve.memset(carrier[:, :], 0.0)
                    for s in range(SUB):
                        last = dve.bn_aggr(mv[:, s, :], stats[:, s, :])
                    last.then_inc(var_done, 1)

                def normalise(kind, t, dst):
                    _, mv, std, rstd, _, _, std_done, rstd_done = norms[kind]
                    dve.wait_ge(std_done, t + 1)
                    dve.reciprocal(rstd[:, :], std[:, :]).then_inc(rstd_done, 1)
                    dve.wait_ge(rstd_done, t + 1)
                    for s in range(SUB):
                        last = dve.tensor_scalar(dst(s), tile_of(t, s), mv[:, s, 0:1], rstd[:, s:s + 1],
                                                 ALU.subtract, ALU.mult)
                    return last

                def first_norm(phase, t):
                    if phase == 0 and first:
                        measure("0", t)
                    if phase == 1 and first:
                        normalise("0", t, lambda s: tile_of(t, s)).then_inc(xn0_done, 1)
                    if phase == 2:
                        if first:
                            dve.wait_ge(xn0_done, t + 1)
                        measure("1", t)
                    if phase == 3:
                        normalise("1", t, lambda s: xn[:, s, :]).then_inc(xn_done, 1)

                def scale(turned, norm, done, t):
                    dve.wait_ge(turned, t + 1)
                    for k in range(KD):
                        last = dve.tensor_scalar(full[:, k, :], t_ps[:, k, :], norm[:, 0, k:k + 1], norm[:, 1, k:k + 1],
                                                 ALU.mult, ALU.add)
                    last.then_inc(done, 1)

                def keys_queries(a):
                    for i, (dst, table, done) in enumerate(((q, query_decay, q_done), (kT, key_decay, k_done))):
                        for g in range(KD):
                            m = KD * i + g
                            dve.wait_ge(proj_done, 10 * a + m + 1)
                            dve.scalar_tensor_tensor(dst[:, g, :].rearrange("p (c n) -> p c n", n=P),
                                                     banks[:, m, :].rearrange("p (c n) -> p c n", n=P), proj_b[:, m:m + 1],
                                                     table[:, g:g + 1, :].broadcast_to([P, SUB, P]), ALU.add,
                                                     ALU.mult).then_inc(done, 1)

                def values(a):
                    for s in range(SUB):
                        dve.wait_ge(proj_done, 10 * a + 7 + s)
                        dve.tensor_tensor(v[:, s, :], banks[:, 2 + s % 2, 0:D], v_b[:, :], ALU.add).then_inc(v_done, 1)

                def masked(a, c, j):
                    cc, w = SUB * a + c, 4 * P
                    dve.wait_ge(scores_done, 2 * cc + j // 2 + 1 + SCORES_CREDIT)
                    dve.wait_ge(ret_done, 2 * cc - 1 + j // 2 + CREDIT)
                    dve.tensor_tensor(probs[:, j * w:(j + 1) * w].rearrange("p (h n) -> p h n", n=P),
                                      banks[:, j, :].rearrange("p (h n) -> p h n", n=P),
                                      past[:, :].unsqueeze(1).broadcast_to([P, 4, P]), ALU.mult).then_inc(probs_done, 1)

                def copy_keys(n):
                    dve.wait_ge(kturn_done, n + 1)
                    dve.tensor_copy(ks[:, :], m_ps[:, 0:D]).then_inc(ks_done, 1)

                def gate_result(a, c):
                    cc = SUB * a + c
                    dve.wait_ge(ret_done, 2 * (cc + 1) + CREDIT)
                    part = slice(c * P, (c + 1) * P)
                    dve.tensor_tensor(gated[:, :, part], ret_ps[:, 0:KD * P].rearrange("p (g n) -> p g n", g=KD),
                                      gate[:, :, part], ALU.mult).then_inc(gated_done, 1)

                def update_state(batch, k):
                    dve.wait_ge(st_done, UPDATES * batch + k + 1)
                    part = m_ps[:, D:2 * D].rearrange("p (g n) -> p g n", g=KD)
                    if k == 0:
                        dve.tensor_tensor(state[:, 0, :, :], part, own_head[:, :, :], ALU.mult).then_inc(state_done, 1)
                        return
                    dve.tensor_tensor(fresh[:, :, :], part, own_head[:, :, :], ALU.mult).then_inc(fresh_done, 1)
                    dve.wait_ge(fresh_done, (UPDATES - 1) * batch + k)
                    for g in range(KD):
                        last = dve.scalar_tensor_tensor(state[:, k % 2, g, :], state[:, (k - 1) % 2, g, :], state_decay[:, g:g + 1],
                                                        fresh[:, g, :], ALU.mult, ALU.add)
                    last.then_inc(state_done, 1)

                def feed(b, f):
                    dve.wait_ge(f_hi_done, KF * b + f + 1)
                    dve.tensor_tensor(f_lo[:, f % 2, :], act_f[:, f % 2, :], f_hi[:, f % 2, :].bitcast(F32),
                                      ALU.subtract).then_inc(f_lo_done, 1)

                def add_retention(a):
                    dve.wait_ge(reto_done, a + 1)
                    dve.tensor_tensor(tile_of(a), tile_of(a), token_ps, ALU.add).then_inc(reto_read, 1)

                def add_bias(a):
                    dve.wait_ge(reto_read, a + 1)
                    dve.tensor_tensor(tile_of(a), tile_of(a), reto_b[:, :].unsqueeze(1).broadcast_to([P, SUB, D]),
                                      ALU.add).then_inc(reto_added, 1)

                def measure_retained(a):
                    dve.wait_ge(reto_added, a + 1)
                    measure("2", a)

                def add_feed(b):
                    dve.wait_ge(back_done, b + 1)
                    dve.tensor_tensor(tile_of(b), tile_of(b), back_ps, ALU.add).then_inc(added, 1)
                    if final:
                        dve.wait_ge(added, b + 1 + CREDIT)
                        measure("f", b)

                def step(a, j, batch, b, more):
                    if a is not None:
                        for c in range(SUB):
                            k = SUB * j + c
                            if k < UPDATES:
                                copy_keys(UPDATES * batch + k)
                            if c == 2 and b is not None:
                                scale(bT_done, norm2, b_full, b)
                            if k < UPDATES and c + 1 < SUB:
                                update_state(batch, k)
                            if c + 1 < SUB:
                                masked(a, c + 1, 0)
                                masked(a, c + 1, 1)
                            gate_result(a, c)
                            if k < UPDATES and c + 1 == SUB:
                                update_state(batch, k)
                            if c + 1 < SUB:
                                masked(a, c + 1, 2)
                                masked(a, c + 1, 3)
                            if more:
                                first_norm(c, a + 1)
                    if b is not None:
                        for f in range(KF):
                            feed(b, f)
                            if a is None and f == 1:
                                if final:
                                    dve.wait_ge(final_done, 1)
                                measure_ahead(dve, ahead, signals, h_sb, 0)
                            if a is None and f == 4:
                                invert_ahead(dve, ahead, signals, 0)
                            if turns_last(a, more):
                                if f == 5:
                                    normalise("2", a, lambda s: xn[:, s, :]).then_inc(xn2_done, 1)
                                if f == 6:
                                    scale(bT_done, norm2, b_full, a)
                            if f == 1 and more:
                                scale(aT_done, norm1, a_full, a + 1)
                            if f == 5 and finishes(b):
                                normalise("f", b - 1, lambda s: tile_of(b - 1, s)).then_inc(xf_done, 1)
                            if a is not None:
                                if f == 2:
                                    add_retention(a)
                                if f == 3:
                                    add_bias(a)
                                if f == 4:
                                    measure_retained(a)
                    else:
                        scale(aT_done, norm1, a_full, a + 1)
                        add_retention(a)
                        add_bias(a)
                        measure_retained(a)
                    if more:
                        keys_queries(a + 1)
                    if b is not None:
                        add_feed(b)
                    if more:
                        values(a + 1)
                        for bank in range(4):
                            masked(a + 1, 0, bank)
                        normalise("2", a, lambda s: xn[:, s, :]).then_inc(xn2_done, 1)

                for kind in ("0", "1") if first else ("1",):
                    for i in (4, 5, 7):
                        dve.sem_inc(norms[kind][i], 1)
                if first:
                    dve.sem_inc(xn0_done, 1)
                apply_ahead(dve, ahead, h_sb, lambda s: xn[:, s, :]).then_inc(xn_done, 1)
                dve.wait_ge(norm_in, NORM1_CONSTS)
                scale(aT_done, norm1, a_full, 0)
                dve.wait_ge(a_hi_done, 1)
                dve.tensor_tensor(a_lo[:, :, :], full[:, :, :], a_hi[:, :, :].bitcast(F32), ALU.subtract).then_inc(a_lo_done, 1)
                dve.wait_ge(const_in, consts_ready)
                keys_queries(0)
                values(0)
                for bank in range(4):
                    masked(0, 0, bank)
                steps(dve, step)
                if final:
                    normalise("f", NT - 1, lambda s: tile_of(NT - 1, s)).then_inc(xf_done, 1)
                    for r, op in ((0, ALU.mult), (1, ALU.add)):
                        dve.wait_ge(xf_done, NT + r)
                        dve.tensor_tensor(tile_of(NT - 1), tile_of(NT - 1),
                                          normf[:, r:r + 1, :].broadcast_to([P, SUB, D]), op).then_inc(xf_done, 1)
                    dve.wait_ge(xf_done, NT + 2)
                    dve.wait_ge(x_old_in, 16 * NT)
                    dve.tensor_tensor(tile_of(NT - 1), tile_of(NT - 1), x_old[:, :, :], ALU.add).then_inc(added, 1)

            @block.tensor
            def _(pe):
                pe.sem_inc(scores_done, SCORES_CREDIT)
                pe.sem_inc(ret_done, CREDIT)
                pe.sem_inc(ffn2_done, CREDIT)

                def turn(ready, done, t):
                    pe.wait_ge(ready, t + 1)
                    for k in range(KD):
                        for s in range(SUB):
                            last = pe.transpose(t_ps[:, k, s * P:(s + 1) * P], xn[:, s, k * P:(k + 1) * P], ident[:, :])
                    last.then_inc(done, 1)

                def project_block(a, bank, m):
                    for k in range(KD):
                        if isinstance(a, int) and a == 0:
                            pe.wait_ge(w_lo_done, k + 1)
                        w = slice(m * P, (m + 1) * P)
                        last = split3(pe, banks[:, bank, :], wp_hi[:, k, w], wp_lo[:, k, w], a_hi[:, k, :],
                                      a_lo[:, k, :], k == 0, k == KD - 1)
                    last.then_inc(proj_done, 1)

                def project_first(a):
                    pe.wait_ge(a_lo_done, a + 1)
                    project_block(a, 0, 0)

                def project(a, b):
                    for m in range(1, 4):
                        if m == 2 and b is not None:
                            pe.wait_ge(oT_done, b + 1)
                        project_block(a, m, m)
                    if b is not None:
                        turn_back(b)
                    for g in range(KD):
                        pe.wait_ge(q_done, KD * a + g + 1)
                        project_block(a, g, 6 + g)
                    for s in range(SUB):
                        if s < 2:
                            pe.wait_ge(k_done, KD * a + s + 1)
                        else:
                            pe.wait_ge(v_done, SUB * a + s - 1)
                        for k in range(KD):
                            t, w = slice(s * P, (s + 1) * P), slice(2 * D, 3 * D)
                            last = split3(pe, banks[:, 2 + s % 2, 0:D], a_hi[:, k, t], a_lo[:, k, t], wp_hi[:, k, w],
                                          wp_lo[:, k, w], k == 0, k == KD - 1)
                        last.then_inc(proj_done, 1)

                def scores(a, c):
                    cc = SUB * a + c
                    for bank in range(4):
                        g = bank // 2
                        if bank % 2 == 0:
                            pe.wait_ge(wide_q_done, 2 * cc + g + 1)
                        if c > 0:
                            pe.wait_ge(probs_done, 4 * (cc - 1) + bank + 1)
                        elif bank < 2:
                            pe.wait_ge(gate_done, KD * a + bank + 1)
                        else:
                            pe.wait_ge(v_done, SUB * a + bank + 1)
                        wide = q_wide[:, c % 2, g, 4 * (bank % 2):4 * (bank % 2) + 4, :].rearrange("p h n -> p (h n)")
                        last = pe.matmul(banks[:, bank, :], kT[:, g, c * P:(c + 1) * P], wide, start=True, stop=True)
                        if bank % 2 == 1:
                            last.then_inc(scores_done, 1)

                def turn_keys(a, c, n):
                    if not isinstance(a, int) or a > 0:
                        if c == 0:
                            pe.wait_ge(reto_read, a)
                    if not isinstance(n, int) or n > 0:
                        pe.wait_ge(state_done, n)
                    for g in range(KD):
                        last = pe.transpose(m_ps[:, g * P:(g + 1) * P], kT[:, g, c * P:(c + 1) * P], ident[:, :])
                    last.then_inc(kturn_done, 1)

                def retain(a, c, k, n):
                    cc = SUB * a + c
                    if not isinstance(a, int) or cc > 0:
                        pe.wait_ge(gated_done, cc)
                    pe.wait_ge(wide_v_done, cc + 1)
                    if k > 0:
                        pe.wait_ge(state_done, n)
                    for g in range(KD):
                        out = ret_ps[:, g * P:(g + 1) * P]
                        if k > 0:
                            pe.matmul(out, state[:, (k - 1) % 2, g, :], q[:, g, c * P:(c + 1) * P], start=True, stop=False)
                        for hh in range(HG):
                            if hh % 4 == 0:
                                pe.wait_ge(probs_done, 4 * cc + 2 * g + hh // 4 + 1)
                            head = g * HG + hh
                            last = pe.matmul(out, v_wide[:, g, hh * P:(hh + 1) * P], probs[:, head * P:(head + 1) * P],
                                             start=(k == 0 and hh == 0), stop=(hh == HG - 1))
                        last.then_inc(ret_done, 1)

                def outer(c, n):
                    pe.wait_ge(ks_done, n + 1)
                    for g in range(KD):
                        w = slice(g * P, (g + 1) * P)
                        last = pe.matmul(m_ps[:, D + g * P:D + (g + 1) * P], ks[:, w], v[:, c, w], start=True, stop=True)
                    last.then_inc(st_done, 1)

                def feed_in(b, f):
                    if f >= 2:
                        pe.wait_ge(f_hi_done, KF * b + f - 1)
                    for k in range(KD):
                        w = slice(f * P, (f + 1) * P)
                        last = split3(pe, banks[:, f % 2, :], w1_hi[:, k, w], w1_lo[:, k, w], b_hi[:, k, :], b_lo[:, k, :],
                                      k == 0, k == KD - 1)
                    last.then_inc(ffn1_done, 1)

                def feed_out(b, f):
                    pe.wait_ge(f_lo_done, KF * b + f + 1 + CREDIT)
                    for k in range(KD):
                        w = slice(k * P, (k + 1) * P)
                        last = split3(pe, banks[:, 2 + k, :], w2_hi[:, f, w], w2_lo[:, f, w], f_hi[:, f % 2, :],
                                      f_lo[:, f % 2, :], f == 0, f == KF - 1)
                    last.then_inc(ffn2_done, 1)

                def project_out(a, n):
                    pe.wait_ge(gated_done, SUB * (a + 1))
                    if n is not None:
                        pe.wait_ge(state_done, n)
                    pe.wait_ge(g_lo_done, a + 1)
                    pe.wait_ge(w_lo_done, RETO_READY)
                    for s in range(SUB):
                        t = slice(s * P, (s + 1) * P)
                        for k in range(KD):
                            last = split3(pe, token_ps[:, s, :], g_hi[:, k, t], g_lo[:, k, t], wr_hi[:, k, :],
                                          wr_lo[:, k, :], k == 0, k == KD - 1)
                    last.then_inc(reto_done, 1)

                def turn_back(b):
                    for s in range(SUB):
                        for k in range(KD):
                            last = pe.transpose(back_ps[:, s, k * P:(k + 1) * P], oT[:, k, s * P:(s + 1) * P], ident[:, :])
                    last.then_inc(back_done, 1)

                def turn_b(b):
                    pe.wait_ge(added, b + CREDIT)
                    turn(xn2_done, bT_done, b)

                def step(a, j, batch, b, more):
                    if a is not None:
                        for c in range(SUB):
                            k = SUB * j + c
                            n = UPDATES * batch + k
                            if k < UPDATES:
                                turn_keys(a, c, n)
                            if c + 1 < SUB:
                                scores(a, c + 1)
                            if k < UPDATES and c + 1 < SUB:
                                outer(c, n)
                            retain(a, c, k, n)
                            if k < UPDATES and c + 1 == SUB:
                                outer(c, n)
                            if c == 1 and b is not None:
                                turn_b(b)
                        pe.wait_ge(probs_done, 4 * SUB * (a + 1))
                    if b is not None:
                        pe.wait_ge(b_lo_done, b + 1)
                        pe.wait_ge(w_lo_done, FFN_READY)
                        feed_in(b, 0)
                        feed_in(b, 1)
                    if more:
                        turn(xn_done, aT_done, a + 1)
                    if b is not None:
                        for f in range(KF):
                            if f == KF - 1 and more:
                                project_first(a + 1)
                            feed_out(b, f)
                            if f + 2 < KF:
                                feed_in(b, f + 2)
                            if f == 0 and a is not None:
                                project_out(a, UPDATES * batch + min(UPDATES, SUB * (j + 1)))
                            if f == KF - 3 and turns_last(a, more):
                                turn(xn2_done, bT_done, a)
                    else:
                        project_out(a, UPDATES * batch + SUB * (j + 1))
                        project_first(a + 1)
                    if more:
                        project(a + 1, b)
                        scores(a + 1, 0)
                    elif b is not None:
                        pe.wait_ge(oT_done, b + 1)
                        pe.wait_ge(b_full, NT)
                        turn_back(b)

                turn(xn_done, aT_done, 0)
                project_first(0)
                project(0, None)
                scores(0, 0)
                steps(pe, step)

        hand_back(nc, sems)


def macaron(nc, ins, out):
    with ExitStack() as ctx:
        x_sb = ctx.enter_context(nc.sbuf_tensor("x_sb", [P, TOK // P, D], F32))
        ident = ctx.enter_context(nc.sbuf_tensor("ident", [P, P], F32))
        iota16 = ctx.enter_context(nc.sbuf_tensor("iota16", [P, E], F32))
        eps = ctx.enter_context(nc.sbuf_tensor("eps", [P, 1], F32))
        ahead = ahead_buffers(nc, ctx)
        const_in = ctx.enter_context(nc.semaphore("const_in"))
        eps_set = ctx.enter_context(nc.semaphore("eps_set"))
        x_dram = nc.dram_tensor("x_dram", (TOK, D), F32).ap()
        comb_dram = nc.dram_tensor("comb_dram", (2, E, TILE), F32).ap()

        with nc.Block() as block:
            @block.sync
            def _(sp):
                sp.dma_start(ident[:, :], ins["ident"]).then_inc(const_in, 16)
                sp.dma_start(iota16[:, :], ins["iota16"]).then_inc(const_in, 16)
                sp.wait_ge(const_in, 32)
                sp.wait_ge(eps_set, 1)

            @block.vector
            def _(dve):
                dve.memset(eps[:, :], EPS).then_inc(eps_set, 1)

        def ffn(tag, x_in, x_out):
            moe(nc, tag, x_sb, ident, iota16, eps, x_in, x_out, ins["router_w"], ins["router_b"], ins["gate_w"],
                ins["up_w"], ins["down_w"], ins["conv_w"], ins["shared_up"], ins["shared_down"], comb_dram, ahead)

        ffn("a", ins["x"], x_dram)
        for layer in range(NL):
            retention_layer(nc, layer, x_sb, ident, eps, ins, x_dram, ahead)
        ffn("b", None, out)


def kernel(**inputs):
    import concourse.bacc as bacc
    from concourse.bass_utils import run_bass_kernel_spmd

    a = {k: np.ascontiguousarray(v) for k, v in inputs.items()}
    arrays = {
        "x": a["L0_attn_x"].reshape(TOK, D),
        "router_w": a["L0_ffn_router_w"],
        "router_b": a["L0_ffn_router_bias"].reshape(E, 1),
        "gate_w": a["L0_ffn_expert_gate_w"],
        "up_w": a["L0_ffn_expert_up_w"],
        "down_w": a["L0_ffn_expert_down_w"],
        "conv_w": np.ascontiguousarray(a["L0_ffn_conv_w"].transpose(2, 1, 0)).reshape(TAPS * D, P),
        "shared_up": a["L0_ffn_shared_up_w"],
        "shared_down": a["L0_ffn_shared_down_w"],
    }
    for name in ("proj_w", "proj_b", "reto_w", "reto_b", "ffn1_w", "ffn2_w", "lnf_g", "lnf_b"):
        arrays[name] = a[f"L0_attn_{name}"]

    def by_partition(name):
        return np.ascontiguousarray(a[f"L0_attn_{name}"].reshape(NL, -1, P).transpose(0, 2, 1))

    for name in ("ln1_g", "ln1_b", "ln2_g", "ln2_b", "ffn1_b", "ffn2_b"):
        arrays[name] = by_partition(name)
    arrays["proj_b_cols"] = by_partition("proj_b")
    arrays.update(shape_constants())
    nc = bacc.Bacc("TRN2", target_bir_lowering=False, num_devices=1)
    ins = {k: nc.dram_tensor(f"in_{k}", v.shape, F32, kind="ExternalInput").ap() for k, v in arrays.items()}
    out = nc.dram_tensor("out_x", (TOK, D), F32, kind="ExternalOutput").ap()
    macaron(nc, ins, out)
    result = run_bass_kernel_spmd(nc, [{f"in_{k}": v for k, v in arrays.items()}], core_ids=[0])
    return result.results[0]["out_x"].reshape(B, S, D)


def shape_constants():
    gamma = 1.0 - 2.0 ** (-5.0 - np.arange(H, dtype=np.float64))
    n = np.arange(P)
    head = (np.arange(D) // HD).reshape(KD, P).T
    own = n // HD
    f32 = np.float32
    return {
        "past": (n[:, None] <= n[None, :]).astype(f32),
        "query_decay": (gamma[head][:, :, None] ** n[None, None, :]).astype(f32),
        "key_decay": (gamma[head][:, :, None] ** -n[None, None, :]).astype(f32),
        "state_decay": (gamma[head] ** P).astype(f32),
        "own_head": ((own[:, None] == own[None, :])[:, None, :] * (gamma[head] ** P)[:, :, None]).astype(f32),
        "head_mask": (own[:, None] == np.arange(HG)[None, :]).astype(f32),
        "ident": np.eye(P, dtype=np.float32),
        "iota16": np.tile(np.arange(E, dtype=np.float32), (P, 1)),
    }
```
